# Optimizing a Trainium2 kernel written in Bass

```python
import numpy as np
import jax
import jax.numpy as jnp

def _softmax(x, axis=-1):
    return jax.nn.softmax(x, axis=axis)
def _gelu(x):
    return jax.nn.gelu(x, approximate=True)
def _silu(x):
    return jax.nn.silu(x)
def _sigmoid(x):
    return jax.nn.sigmoid(x)
def _layernorm(x, axis=-1, eps=1e-5):
    m = jnp.mean(x, axis=axis, keepdims=True)
    v = jnp.var(x, axis=axis, keepdims=True)
    return (x - m) / jnp.sqrt(v + eps)
def _scatter_add(tgt, idx, src, axis=0):
    return tgt.at[idx].add(src)
def _segment_sum(src, seg, n):
    return jax.ops.segment_sum(src, seg, n)

kernel_name = 'mk_adj_preln_d4_adj_256_01d9a2'

def setup_inputs(seed: int = 0):
    np.random.seed(seed)
    _w = jnp.asarray
    def _rec_inputs():
        import jax
        import jax.numpy as jnp
        _gk = jax.random.key(seed)
        x = -0.0005207 + 1.001 * jax.random.normal(jax.random.fold_in(_gk, 1), (4096, 256), jnp.float32)
        _a = jax.random.bernoulli(jax.random.fold_in(_gk, 2), 0.0078125, (4096, 4096))
        adj = _a.astype(jnp.int32)
        return x, adj
    x, adj = _rec_inputs()
    def _L0_gnn_setup():
        import jax, jax.numpy as jnp
        import numpy as np
        N = 8192
        F_IN = 256
        F_OUT = 256
        S = 128
        D_INNER = 512

        def _ln(x, g, b, eps=1e-05):
            m = x.mean(-1, keepdims=True)
            v = ((x - m) ** 2).mean(-1, keepdims=True)
            return (x - m) / jnp.sqrt(v + eps) * g + b
        key = jax.random.key(seed)
        ks = jax.random.split(key, 20)
        s = 0.05
        d = {}
        d['h'] = jax.random.normal(ks[0], (N, F_IN), dtype=jnp.float32)
        d['adj'] = jax.random.randint(ks[1], (N, N), 0, 2, dtype=jnp.int32)
        d['W'] = jax.random.normal(ks[2], (F_IN, F_OUT), dtype=jnp.float32) * s
        d['a_src'] = jax.random.normal(ks[3], (F_OUT, 1), dtype=jnp.float32) * s
        d['a_dst'] = jax.random.normal(ks[4], (F_OUT, 1), dtype=jnp.float32) * s
        d['W_bcdt'] = jax.random.normal(ks[5], (F_OUT, 3 * S), dtype=jnp.float32) * s
        d['b_bcdt'] = jnp.zeros((3 * S,), jnp.float32)
        d['abp_w'] = jax.random.normal(ks[6], (S, F_OUT), dtype=jnp.float32) * s
        d['abp_b'] = jnp.zeros((F_OUT,), jnp.float32)
        d['cp_w'] = jax.random.normal(ks[7], (S, 1), dtype=jnp.float32) * s
        d['cp_b'] = jnp.zeros((1,), jnp.float32)
        d['W_hz'] = jax.random.normal(ks[8], (F_OUT, 2 * D_INNER), dtype=jnp.float32) * s
        d['b_hz'] = jnp.zeros((2 * D_INNER,), jnp.float32)
        d['out_w'] = jax.random.normal(ks[9], (D_INNER, F_OUT), dtype=jnp.float32) * s
        d['out_b'] = jnp.zeros((F_OUT,), jnp.float32)
        d['fe1_w'] = jax.random.normal(ks[10], (F_OUT, D_INNER), dtype=jnp.float32) * s
        d['fe1_b'] = jnp.zeros((D_INNER,), jnp.float32)
        d['fe_ln_g'] = jnp.ones((D_INNER,), jnp.float32)
        d['fe_ln_b'] = jnp.zeros((D_INNER,), jnp.float32)
        d['fe2_w'] = jax.random.normal(ks[11], (D_INNER, F_OUT), dtype=jnp.float32) * s
        d['fe2_b'] = jnp.zeros((F_OUT,), jnp.float32)
        d['A'] = jax.random.uniform(ks[12], (S,), minval=1.0, maxval=64.0, dtype=jnp.float32)
        d['D'] = jnp.ones((1,), jnp.float32)
        d['g1_w'] = jax.random.normal(ks[13], (2 * F_OUT, 2 * F_OUT), dtype=jnp.float32) * s
        d['g1_b'] = jnp.zeros((2 * F_OUT,), jnp.float32)
        d['g_ln_g'] = jnp.ones((2 * F_OUT,), jnp.float32)
        d['g_ln_b'] = jnp.zeros((2 * F_OUT,), jnp.float32)
        d['g2_w'] = jax.random.normal(ks[14], (2 * F_OUT, F_OUT), dtype=jnp.float32) * s
        d['g2_b'] = jnp.zeros((F_OUT,), jnp.float32)
        d['ln_g'] = jnp.ones((F_OUT,), jnp.float32)
        d['ln_b'] = jnp.zeros((F_OUT,), jnp.float32)
        return d
    _L0_gnn_all = _L0_gnn_setup()
    _L0_gnn_in = {k: v for k, v in _L0_gnn_all.items() if k in ('W', 'a_src', 'a_dst', 'W_bcdt', 'b_bcdt', 'abp_w', 'abp_b', 'cp_w', 'cp_b', 'W_hz', 'b_hz', 'out_w', 'out_b', 'fe1_w', 'fe1_b', 'fe_ln_g', 'fe_ln_b', 'fe2_w', 'fe2_b', 'A', 'D', 'g1_w', 'g1_b', 'g_ln_g', 'g_ln_b', 'g2_w', 'g2_b', 'ln_g', 'ln_b', )}
    del _L0_gnn_all

    def _L1_gnn_setup():
        import jax, jax.numpy as jnp
        import numpy as np
        N = 16384
        D = 256
        key = jax.random.key(seed)
        k1, k2, k3, k4 = jax.random.split(key, 4)
        x = jax.random.normal(k1, (N, D), dtype=jnp.float32)
        adj = jax.random.randint(k2, (N, N), 0, 2, dtype=jnp.int32)
        W = jax.random.normal(k3, (D, D), dtype=jnp.float32) * 0.05
        b = jax.random.normal(k4, (D,), dtype=jnp.float32) * 0.05
        return {'x': x, 'adj': adj, 'W': W, 'b': b}
    _L1_gnn_all = _L1_gnn_setup()
    _L1_gnn_in = {k: v for k, v in _L1_gnn_all.items() if k in ('W', 'b', )}
    del _L1_gnn_all

    def _L2_gnn_setup():
        import jax, jax.numpy as jnp
        import numpy as np
        N = 8192
        D = 256
        NEG_SLOPE = 0.01
        MASK_VAL = -1000000000000.0
        key = jax.random.key(seed)
        k1, k2, k3, k4 = jax.random.split(key, 4)
        x = jax.random.normal(k1, (N, D), dtype=jnp.float32)
        adj = jax.random.randint(k2, (N, N), 0, 2, dtype=jnp.int32)
        W = jax.random.normal(k3, (D, D), dtype=jnp.float32) * (1.0 / np.sqrt(D))
        a = jax.random.normal(k4, (2 * D, 1), dtype=jnp.float32) * (1.0 / np.sqrt(2 * D))
        return {'x': x, 'adj': adj, 'W': W, 'a': a}
    _L2_gnn_all = _L2_gnn_setup()
    _L2_gnn_in = {k: v for k, v in _L2_gnn_all.items() if k in ('W', 'a', )}
    del _L2_gnn_all

    def _L3_gnn_setup():
        import jax, jax.numpy as jnp
        import numpy as np
        N = 8192
        D_IN = 256
        D_HID = 256
        D_OUT = 256
        key = jax.random.key(seed)
        k_x, k_a, k_q, k_k, k_v = jax.random.split(key, 5)
        X = jax.random.normal(k_x, (N, D_IN), dtype=jnp.float32)
        A = jax.random.randint(k_a, (N, N), 0, 2, dtype=jnp.int32)
        A = A * (1 - jnp.eye(N, dtype=jnp.int32))
        Wq = jax.random.normal(k_q, (D_IN, D_HID), dtype=jnp.float32) / 10.0
        Wk = jax.random.normal(k_k, (D_IN, D_HID), dtype=jnp.float32) / 10.0
        Wv = jax.random.normal(k_v, (D_IN, D_OUT), dtype=jnp.float32) / 10.0
        return {'X': X, 'A': A, 'Wq': Wq, 'Wk': Wk, 'Wv': Wv}
    _L3_gnn_all = _L3_gnn_setup()
    _L3_gnn_in = {k: v for k, v in _L3_gnn_all.items() if k in ('Wq', 'Wk', 'Wv', )}
    del _L3_gnn_all

    return {
        "x": x,
        "adj": adj,
        "L0_gnn_W": _L0_gnn_in["W"],
        "L0_gnn_a_src": _L0_gnn_in["a_src"],
        "L0_gnn_a_dst": _L0_gnn_in["a_dst"],
        "L0_gnn_W_bcdt": _L0_gnn_in["W_bcdt"],
        "L0_gnn_b_bcdt": _L0_gnn_in["b_bcdt"],
        "L0_gnn_abp_w": _L0_gnn_in["abp_w"],
        "L0_gnn_abp_b": _L0_gnn_in["abp_b"],
        "L0_gnn_cp_w": _L0_gnn_in["cp_w"],
        "L0_gnn_cp_b": _L0_gnn_in["cp_b"],
        "L0_gnn_W_hz": _L0_gnn_in["W_hz"],
        "L0_gnn_b_hz": _L0_gnn_in["b_hz"],
        "L0_gnn_out_w": _L0_gnn_in["out_w"],
        "L0_gnn_out_b": _L0_gnn_in["out_b"],
        "L0_gnn_fe1_w": _L0_gnn_in["fe1_w"],
        "L0_gnn_fe1_b": _L0_gnn_in["fe1_b"],
        "L0_gnn_fe_ln_g": _L0_gnn_in["fe_ln_g"],
        "L0_gnn_fe_ln_b": _L0_gnn_in["fe_ln_b"],
        "L0_gnn_fe2_w": _L0_gnn_in["fe2_w"],
        "L0_gnn_fe2_b": _L0_gnn_in["fe2_b"],
        "L0_gnn_A": _L0_gnn_in["A"],
        "L0_gnn_D": _L0_gnn_in["D"],
        "L0_gnn_g1_w": _L0_gnn_in["g1_w"],
        "L0_gnn_g1_b": _L0_gnn_in["g1_b"],
        "L0_gnn_g_ln_g": _L0_gnn_in["g_ln_g"],
        "L0_gnn_g_ln_b": _L0_gnn_in["g_ln_b"],
        "L0_gnn_g2_w": _L0_gnn_in["g2_w"],
        "L0_gnn_g2_b": _L0_gnn_in["g2_b"],
        "L0_gnn_ln_g": _L0_gnn_in["ln_g"],
        "L0_gnn_ln_b": _L0_gnn_in["ln_b"],
        "L1_gnn_W": _L1_gnn_in["W"],
        "L1_gnn_b": _L1_gnn_in["b"],
        "L2_gnn_W": _L2_gnn_in["W"],
        "L2_gnn_a": _L2_gnn_in["a"],
        "L3_gnn_Wq": _L3_gnn_in["Wq"],
        "L3_gnn_Wk": _L3_gnn_in["Wk"],
        "L3_gnn_Wv": _L3_gnn_in["Wv"],
    }

def reference(x, adj, L0_gnn_W, L0_gnn_a_src, L0_gnn_a_dst, L0_gnn_W_bcdt, L0_gnn_b_bcdt, L0_gnn_abp_w, L0_gnn_abp_b, L0_gnn_cp_w, L0_gnn_cp_b, L0_gnn_W_hz, L0_gnn_b_hz, L0_gnn_out_w, L0_gnn_out_b, L0_gnn_fe1_w, L0_gnn_fe1_b, L0_gnn_fe_ln_g, L0_gnn_fe_ln_b, L0_gnn_fe2_w, L0_gnn_fe2_b, L0_gnn_A, L0_gnn_D, L0_gnn_g1_w, L0_gnn_g1_b, L0_gnn_g_ln_g, L0_gnn_g_ln_b, L0_gnn_g2_w, L0_gnn_g2_b, L0_gnn_ln_g, L0_gnn_ln_b, L1_gnn_W, L1_gnn_b, L2_gnn_W, L2_gnn_a, L3_gnn_Wq, L3_gnn_Wk, L3_gnn_Wv):
    import jax
    import jax.numpy as jnp
    def _L0_gnn_ref(h, adj, W, a_src, a_dst, W_bcdt, b_bcdt, abp_w, abp_b, cp_w, cp_b, W_hz, b_hz, out_w, out_b, fe1_w, fe1_b, fe_ln_g, fe_ln_b, fe2_w, fe2_b, A, D, g1_w, g1_b, g_ln_g, g_ln_b, g2_w, g2_b, ln_g, ln_b):
        import jax, jax.numpy as jnp
        import numpy as np
        N = 8192
        F_IN = 256
        F_OUT = 256
        S = 128
        D_INNER = 512

        def _ln(x, g, b, eps=1e-05):
            m = x.mean(-1, keepdims=True)
            v = ((x - m) ** 2).mean(-1, keepdims=True)
            return (x - m) / jnp.sqrt(v + eps) * g + b
        Wh = h @ W
        e = Wh @ a_src + (Wh @ a_dst).T
        e = jnp.where(e > 0, e, 0.2 * e)
        e = jnp.where(adj > 0, e, jnp.float32(-9000000000000000.0))
        attn = jax.nn.softmax(e, axis=1)
        h_attn = attn @ Wh
        h_enh = jax.nn.silu(_ln(Wh @ fe1_w + fe1_b, fe_ln_g, fe_ln_b)) @ fe2_w + fe2_b
        BCdt = Wh @ W_bcdt + b_bcdt
        B, C, dt = jnp.split(BCdt, 3, axis=1)
        Asm = jax.nn.softmax(dt + A[None, :], axis=1)
        ab = Asm * B @ abp_w + abp_b
        hs = Wh * ab
        hz = hs @ W_hz + b_hz
        h_part, z = jnp.split(hz, 2, axis=1)
        hs = (h_part * jax.nn.silu(z) + h_part * D) @ out_w + out_b
        c_proj = C @ cp_w + cp_b
        hs = hs * (1.0 + c_proj)
        comb = jnp.concatenate([h_attn, hs], axis=1)
        g = jax.nn.sigmoid(jax.nn.silu(_ln(comb @ g1_w + g1_b, g_ln_g, g_ln_b)) @ g2_w + g2_b)
        fused = g * h_attn + (1.0 - g) * hs + h_enh
        return _ln(fused, ln_g, ln_b)

    def _L1_gnn_ref(x, adj, W, b):
        import jax, jax.numpy as jnp
        import numpy as np
        N = 16384
        D = 256
        a = (adj == 1).astype(x.dtype)
        deg = jnp.sum(a, axis=1, keepdims=True)
        agg = jnp.einsum('ij,jf->if', a, x) / deg
        return agg @ W.T + b

    def _L2_gnn_ref(x, adj, W, a):
        import jax, jax.numpy as jnp
        import numpy as np
        N = 8192
        D = 256
        NEG_SLOPE = 0.01
        MASK_VAL = -1000000000000.0
        h = x @ W
        e_src = h @ a[:D, 0]
        e_dst = h @ a[D:, 0]
        e = e_src[:, None] + e_dst[None, :]
        e = jnp.where(e > 0, e, NEG_SLOPE * e)
        att_logits = jnp.where(adj > 0, e, MASK_VAL)
        attention = jax.nn.softmax(att_logits, axis=1)
        h_prime = attention @ h
        return jax.nn.elu(h_prime)

    def _L3_gnn_ref(X, A, Wq, Wk, Wv):
        import jax, jax.numpy as jnp
        import numpy as np
        N = 8192
        D_IN = 256
        D_HID = 256
        D_OUT = 256
        n = A.shape[0]
        Af = A.astype(X.dtype) + jnp.eye(n, dtype=X.dtype)
        Q = X @ Wq
        K = X @ Wk
        V = X @ Wv
        S = Q @ K.T
        mask = jnp.nan_to_num(-jnp.inf * (1.0 - Af), nan=0.0)
        P = jax.nn.softmax(S + mask, axis=1)
        return P @ V

    h = jnp.maximum(_layernorm(x, axis=-1), 0.0)
    x = x + _L0_gnn_ref(h, adj, L0_gnn_W, L0_gnn_a_src, L0_gnn_a_dst, L0_gnn_W_bcdt, L0_gnn_b_bcdt, L0_gnn_abp_w, L0_gnn_abp_b, L0_gnn_cp_w, L0_gnn_cp_b, L0_gnn_W_hz, L0_gnn_b_hz, L0_gnn_out_w, L0_gnn_out_b, L0_gnn_fe1_w, L0_gnn_fe1_b, L0_gnn_fe_ln_g, L0_gnn_fe_ln_b, L0_gnn_fe2_w, L0_gnn_fe2_b, L0_gnn_A, L0_gnn_D, L0_gnn_g1_w, L0_gnn_g1_b, L0_gnn_g_ln_g, L0_gnn_g_ln_b, L0_gnn_g2_w, L0_gnn_g2_b, L0_gnn_ln_g, L0_gnn_ln_b)
    h = jnp.maximum(_layernorm(x, axis=-1), 0.0)
    x = x + _L1_gnn_ref(h, adj, L1_gnn_W, L1_gnn_b)
    h = jnp.maximum(_layernorm(x, axis=-1), 0.0)
    x = x + _L2_gnn_ref(h, adj, L2_gnn_W, L2_gnn_a)
    h = jnp.maximum(_layernorm(x, axis=-1), 0.0)
    x = x + _L3_gnn_ref(h, adj, L3_gnn_Wq, L3_gnn_Wk, L3_gnn_Wv)
    return x


_drawn_inputs = setup_inputs


def setup_inputs(seed=0):
    import zlib

    import numpy as np

    out = dict(_drawn_inputs(seed))
    spreads = {'L0_gnn_b_bcdt': (0.0, 0.38),
     'L0_gnn_abp_b': (0.0, 0.278),
     'L0_gnn_b_hz': (0.0, 0.1),
     'L0_gnn_out_b': (0.0, 0.1),
     'L0_gnn_fe1_b': (0.0, 0.1),
     'L0_gnn_fe_ln_g': (1.0, 0.2),
     'L0_gnn_fe_ln_b': (0.0, 0.1),
     'L0_gnn_fe2_b': (0.0, 0.1),
     'L0_gnn_g1_b': (0.0, 0.287),
     'L0_gnn_g_ln_g': (1.0, 0.6),
     'L0_gnn_g_ln_b': (0.0, 0.8),
     'L0_gnn_g2_b': (0.0, 0.616),
     'L0_gnn_ln_g': (1.0, 0.2),
     'L0_gnn_ln_b': (0.0, 0.1)}
    factors = {'L0_gnn_a_src': 33.172, 'L0_gnn_abp_w': 8.0, 'L0_gnn_A': 8.0}
    for name, (base, spread) in spreads.items():
        noise = np.random.default_rng([zlib.crc32(name.encode()), seed]).standard_normal(out[name].shape)
        drawn = base * np.exp(spread * noise) if base else spread * noise
        out[name] = jnp.asarray(drawn.astype(out[name].dtype))
    for name, factor in factors.items():
        out[name] = (out[name] * factor).astype(out[name].dtype)
    return out
```

```python
from contextlib import ExitStack

import concourse.bass as bass
from concourse import mybir

F32 = mybir.dt.float32
F16 = mybir.dt.float16
U8 = mybir.dt.uint8
I32 = mybir.dt.int32
ALU = mybir.AluOpType
ACT = mybir.ActivationFunctionType
AX_X = mybir.AxisListType.X
RMAX = bass.bass_isa.ReduceOp.max
ds = bass.ds

P = 128
N = 4096
D = 256
T = N // P
R = 4
G = T // R
GW = R * P
K = D // P
S = 128
H = 512
HK = H // P
VW = D + 2
EPS = 1e-5
BIG = 32768.0
PSCALE = 16384.0
TOP = 60000.0


class Steps:

    def __init__(self, sem):
        self.sem, self.base = sem, 0

    def plan(self, *stages):
        self.first, self.per, self.made = {}, 0, 0
        for name, n in stages:
            self.first[name] = self.per
            self.per += n

    def at(self, rnd, stage, i=0):
        return self.base + rnd * self.per + (self.first[stage] + i + 1)

    def before(self, rnd, stage, i=0, back=1):
        assert self.base >= back * self.per
        return self.at(rnd - back, stage, i)

    def one(self, stage, i=0):
        assert self.first[stage] + i == self.made % self.per, (stage, i, self.made % self.per)
        self.made += 1
        return 1

    def close(self, rounds):
        assert self.made % self.per == 0 and self.made
        self.base += rounds * self.per


def layout():
    dense = [("W0", K, D + 2), ("fe1", K, H), ("bcdt", K, 2 * S + 1), ("abp", 1, D), ("hz", K, 2 * H),
             ("out", HK, D), ("fe2", HK, D)]
    gate = [("g1", 2 * K, H), ("g2", HK, D)]
    later = [("W1", K, D), ("W2", K, D + 2), ("Wq", K, D), ("Wk", K, D), ("Wv", K, D)]
    where = {}
    sizes = []
    for pack, group in enumerate((dense, gate, later)):
        at = 0
        for name, k, n in group:
            where[name] = (pack, at, k, n)
            at += k * n
        sizes.append(at)
    bias, at = {}, 0
    for name, n in [("bcdt", 2 * S + 1), ("fe1", H), ("fe2", D), ("out", D), ("g1", H), ("g2", D), ("W1", D)]:
        bias[name] = (at, n)
        at += n
    return where, sizes, bias, at


def build(nc, a, out):
    where, sizes, bias_at, bias_n = layout()
    top = ExitStack()

    mask_d = nc.dram_tensor("mask_d", [G * P, T * GW], U8, kind="Internal").ap()
    hs_d = nc.dram_tensor("hs_d", [G * P, R * D], F32, kind="Internal").ap()
    w_d = nc.dram_tensor("w_d", [G * P, R * D], F32, kind="Internal").ap()
    qT_d = nc.dram_tensor("qT_d", [G * P, 2 * K * GW], F16, kind="Internal").ap()

    named = set()

    def sb(stack, name, shape, dt):
        n = sum(x.split(".")[0] == name for x in named)
        named.add(f"{name}.{n}")
        return stack.enter_context(nc.sbuf_tensor(f"{name}_{n}" if n else name, shape, dt))

    def sem(name):
        return top.enter_context(nc.semaphore(name))

    with top:
        bank = [top.enter_context(nc.psum_tensor(f"bank{i}", [P, 512], F32)) for i in range(8)]
        pe_s, act_s, dve_s, pool_s = (Steps(sem(n)) for n in ("pe_done", "act_done", "dve_done", "pool_done"))
        pe_q, act_q, dve_q = (Steps(sem(n)) for n in ("pe_quad_done", "act_quad_done", "dve_quad_done"))
        pe_l = Steps(sem("pe_logits_done"))
        s_in = sem("inputs_loaded")
        s_adj = [sem("adj_loaded_0"), sem("adj_loaded_1")]
        s_mst = [sem("mask_stored_0"), sem("mask_stored_1")]
        s_xin = sem("x_loaded")
        s_mask = [sem("mask_loaded_0"), sem("mask_loaded_1")]
        s_qin = [sem("q_loaded_0"), sem("q_loaded_1")]
        s_store = sem("rows_stored")
        s_out = sem("out_stored")
        s_pass = [sem("dve_passed"), sem("pool_passed"), sem("pe_passed")]

        ident = sb(top, "ident", [P, P], F32)
        ident8 = sb(top, "ident8", [P, P], U8)
        ones = sb(top, "ones", [P, P], F32)
        ones16 = sb(top, "ones16", [P, P], F16)
        big16 = sb(top, "big16", [P, P], F16)
        bias3 = sb(top, "bias3", [P, bias_n], F16)
        col_b = sb(top, "col_b", [P, 30], F32)
        lng = sb(top, "lng", [P, D], F32)
        lnb = sb(top, "lnb", [P, D], F32)
        nhalf = sb(top, "nhalf", [P, 8], F32)
        Dcol = sb(top, "Dcol", [P, 1], F32)
        s_col = sb(top, "s_col", [P, T], F32)
        d_col = sb(top, "d_col", [P, T], F32)
        omega = sb(top, "omega", [P, T], F32)
        vprime = sb(top, "vprime", [P, T], F32)
        m_col = sb(top, "m_col", [P, T], F32)
        loop_col = sb(top, "loop_col", [P, T], F32)
        dmax = sb(top, "dmax", [P, 2], F32)
        w_later = [sb(top, f"w_later_{p}", [P, sizes[2]], F16) for p in ("hi", "lo")]

        w_gate = [sb(top, f"w_gate_{p}", [P, sizes[1]], F16) for p in ("hi", "lo")]
        rows = sb(top, "rows", [P, T * D], F32)
        dense_mem = ExitStack()
        w_dense = [sb(dense_mem, f"w_dense_{p}", [P, sizes[0]], F16) for p in ("hi", "lo")]
        packs = (w_dense, w_gate, w_later)
        BZ, BH, BABP, FEG, FEB, GG, GB = 0, 4, 8, 10, 14, 18, 22

        def w(name, k, c0=0, c1=None):
            pack, at, _, n = where[name]
            at += k * n
            c1 = n if c1 is None else c1
            return packs[pack][0][:, at + c0:at + c1], packs[pack][1][:, at + c0:at + c1]

        def products(pe, out_ap, pairs, bias=None):
            todo = []
            for (sh, sl), (mh, ml) in pairs:
                todo += [(sh, mh), (sh, ml), (sl, mh)]
            if bias is not None:
                at, n = bias_at[bias]
                todo.append((ones16[:, :], bias3[:, at:at + n]))
            for i, (st, mv) in enumerate(todo):
                last = nc.tensor.matmul(out_ap, st, mv, start=(i == 0), stop=(i == len(todo) - 1))
            return last

        with ExitStack() as mem, nc.Block() as block:
            stage = [sb(mem, f"stage{i}", [P, sizes[i]], F32) for i in range(3)]
            wc = sb(mem, "wc", [P, K, S], F32)
            junk = sb(mem, "junk", [P, 11, D], F32)
            vecs = sb(mem, "vecs", [P, 4 * D], F32)
            cpw = sb(mem, "cpw", [P, S], F32)
            bc = sb(mem, "bc", [P, S], F32)
            arow = sb(mem, "arow", [P, S], F32)
            cpb = sb(mem, "cpb", [P, 2], F32)
            brow = sb(mem, "brow", [P, bias_n], F32)
            part = sb(mem, "part", [P, bias_n], F16)
            acc3 = sb(mem, "acc3", [P, bias_n], F32)
            loads = []

            def stage_w(name, src, c0=0, n=None):
                pack, at, k, width = where[name]
                view = stage[pack][:, at:at + k * width].rearrange("p (k n) -> p k n", k=k)
                n = src.shape[1] if n is None else n
                loads.append((view[:, :, c0:c0 + n], src.rearrange("(k p) n -> p k n", p=P)))

            stage_w("W0", a["L0_gnn_W"])
            stage_w("fe1", a["L0_gnn_fe1_w"])
            stage_w("bcdt", a["L0_gnn_W_bcdt"][:, 0:S], 0)
            stage_w("bcdt", a["L0_gnn_W_bcdt"][:, 2 * S:3 * S], S)
            stage_w("abp", a["L0_gnn_abp_w"])
            stage_w("hz", a["L0_gnn_W_hz"])
            stage_w("out", a["L0_gnn_out_w"])
            stage_w("fe2", a["L0_gnn_fe2_w"])
            stage_w("g1", a["L0_gnn_g1_w"])
            stage_w("g2", a["L0_gnn_g2_w"])
            stage_w("W1", a["L1_gnn_WT"])
            stage_w("W2", a["L2_gnn_W"])
            stage_w("Wq", a["L3_gnn_Wq"])
            stage_w("Wk", a["L3_gnn_Wk"])
            stage_w("Wv", a["L3_gnn_Wv"])
            loads.append((wc[:, :, :], a["L0_gnn_W_bcdt"][:, S:2 * S].rearrange("(k p) n -> p k n", p=P)))

            def spread(dst, vec):
                loads.append((dst, vec.partition_broadcast(P)))

            spread(vecs[:, 0:D], a["L0_gnn_a_src"])
            spread(vecs[:, D:2 * D], a["L0_gnn_a_dst"])
            spread(vecs[:, 2 * D:4 * D], a["L2_gnn_a"])
            spread(cpw[:, :], a["L0_gnn_cp_w"])
            spread(bc[:, :], a["L0_gnn_b_bcdt"][S:2 * S])
            spread(arow[:, :], a["L0_gnn_A"])
            spread(cpb[:, 0:1], a["L0_gnn_cp_b"])
            spread(Dcol[:, :], a["L0_gnn_D"])
            spread(lng[:, :], a["L0_gnn_ln_g"])
            spread(lnb[:, :], a["L0_gnn_ln_b"])
            spread(brow[:, 0:S], a["L0_gnn_b_bcdt"][0:S])
            spread(brow[:, S:2 * S], a["L0_gnn_b_bcdt"][2 * S:3 * S])
            for name, vec in (("fe1", "L0_gnn_fe1_b"), ("fe2", "L0_gnn_fe2_b"), ("out", "L0_gnn_out_b"),
                              ("g1", "L0_gnn_g1_b"), ("g2", "L0_gnn_g2_b"), ("W1", "L1_gnn_b")):
                at, n = bias_at[name]
                spread(brow[:, at:at + n], a[vec])
            for at, vec in ((BH, a["L0_gnn_b_hz"][0:H]), (BZ, a["L0_gnn_b_hz"][H:2 * H]), (BABP, a["L0_gnn_abp_b"]),
                            (FEG, a["L0_gnn_fe_ln_g"]), (FEB, a["L0_gnn_fe_ln_b"]),
                            (GG, a["L0_gnn_g_ln_g"]), (GB, a["L0_gnn_g_ln_b"])):
                n = vec.shape[0] // P
                loads.append((col_b[:, at:at + n], vec.rearrange("(k p) -> p k", p=P)))

            dve_s.plan(("fold", 9), ("ones", 1), ("split", 3), ("big", 1), ("parts", 8))
            pool_s.plan(("zero", 3), ("ident", 2), ("one", 1))
            act_s.plan(("hi", 3))

            @block.sync
            def _(sp):
                for dst, src in loads:
                    with nc.allow_non_contiguous_dma(reason="small vectors"):
                        sp.dma_start(dst, src).then_inc(s_in, 16)

            @block.gpsimd
            def _(pool):
                nc.gpsimd.memset(ident[:, :], 0.0).then_inc(pool_s.sem, pool_s.one("zero", 0))
                nc.gpsimd.memset(ones[:, :], 1.0).then_inc(pool_s.sem, pool_s.one("zero", 1))
                nc.gpsimd.memset(nhalf[:, :], -0.5).then_inc(pool_s.sem, pool_s.one("zero", 2))
                pool.wait_ge(pool_s.sem, pool_s.at(0, "zero", 0))
                nc.gpsimd.affine_select(out=ident[:, :], in_=ident[:, :], compare_op=ALU.not_equal, fill=1.0,
                                        base=0, pattern=[[-1, P]], channel_multiplier=1
                                        ).then_inc(pool_s.sem, pool_s.one("ident", 0))
                pool.wait_ge(pool_s.sem, pool_s.at(0, "ident", 0))
                nc.gpsimd.tensor_copy(ident8[:, :], ident[:, :]).then_inc(pool_s.sem, pool_s.one("ident", 1))
                nc.gpsimd.tensor_copy(ones16[:, :], ones[:, :]).then_inc(pool_s.sem, pool_s.one("one", 0))

            @block.scalar
            def _(act):
                for i in range(3):
                    act.wait_ge(s_in, 16 * len(loads))
                    act.wait_ge(dve_s.sem, dve_s.at(0, "fold", 8))
                    nc.scalar.copy(packs[i][0][:, :], stage[i][:, :]).then_inc(act_s.sem, act_s.one("hi", i))

            @block.vector
            def _(dve):
                dve.wait_ge(s_in, 16 * len(loads))
                n = 0
                for name, off in (("W0", 0), ("W2", 2 * D)):
                    pack, at, k_, width = where[name]
                    for k in range(K):
                        for j in range(2):
                            base = at + k * width
                            ins = nc.vector.tensor_tensor_reduce(
                                out=junk[:, n, :], in0=stage[pack][:, base:base + D],
                                in1=vecs[:, off + j * D:off + (j + 1) * D], scale=1.0, scalar=0.0,
                                op0=ALU.mult, op1=ALU.add, accum_out=stage[pack][:, base + D + j:base + D + j + 1])
                            ins.then_inc(dve_s.sem, dve_s.one("fold", n))
                            n += 1
                pack, at, k_, width = where["bcdt"]
                for k in range(K):
                    last = nc.vector.tensor_tensor_reduce(
                        out=junk[:, 8 + k, 0:S], in0=wc[:, k, :], in1=cpw[:, :], scale=1.0, scalar=0.0, op0=ALU.mult,
                        op1=ALU.add, accum_out=stage[pack][:, at + k * width + 2 * S:at + k * width + 2 * S + 1])
                last.then_inc(dve_s.sem, dve_s.one("fold", 8))
                nc.vector.tensor_tensor_reduce(
                    out=junk[:, 10, 0:S], in0=bc[:, :], in1=cpw[:, :], scale=1.0, scalar=1.0, op0=ALU.mult,
                    op1=ALU.add, accum_out=cpb[:, 1:2]).then_inc(dve_s.sem, dve_s.one("ones"))
                for i in range(3):
                    dve.wait_ge(act_s.sem, act_s.at(0, "hi", i))
                    nc.vector.tensor_tensor(packs[i][1][:, :], stage[i][:, :], packs[i][0][:, :], ALU.subtract
                                            ).then_inc(dve_s.sem, dve_s.one("split", i))
                dve.wait_ge(pool_s.sem, pool_s.at(0, "one"))
                nc.vector.tensor_scalar(big16[:, :], ident[:, :], BIG, None, ALU.mult
                                        ).then_inc(dve_s.sem, dve_s.one("big"))
                dve.wait_ge(dve_s.sem, dve_s.at(0, "ones"))
                nc.vector.tensor_tensor(brow[:, 2 * S:2 * S + 1], cpb[:, 0:1], cpb[:, 1:2], ALU.add
                                        ).then_inc(dve_s.sem, dve_s.one("parts", 0))
                nc.vector.tensor_tensor(brow[:, S:2 * S], brow[:, S:2 * S], arow[:, :], ALU.add
                                        ).then_inc(dve_s.sem, dve_s.one("parts", 1))
                for q in range(3):
                    dve.wait_ge(dve_s.sem, dve_s.at(0, "parts", 2 * q + 1))
                    nc.vector.tensor_copy(part[:, :], brow[:, :]).then_inc(dve_s.sem, dve_s.one("parts", 2 * q + 2))
                    dve.wait_ge(dve_s.sem, dve_s.at(0, "parts", 2 * q + 2))
                    if q == 0:
                        nc.vector.tensor_scalar(acc3[:, :], part[:, :], ident[:, 0:1], None, ALU.mult)
                    if q == 1:
                        nc.vector.scalar_tensor_tensor(out=acc3[:, :], in0=part[:, :], scalar=ident[:, 1:2],
                                                       in1=acc3[:, :], op0=ALU.mult, op1=ALU.add)
                    if q == 2:
                        nc.vector.scalar_tensor_tensor(out=bias3[:, :], in0=part[:, :], scalar=ident[:, 2:3],
                                                       in1=acc3[:, :], op0=ALU.mult, op1=ALU.add
                                                       ).then_inc(dve_s.sem, dve_s.one("parts", 7))
                    else:
                        nc.vector.tensor_tensor(brow[:, :], brow[:, :], part[:, :], ALU.subtract
                                                ).then_inc(dve_s.sem, dve_s.one("parts", 2 * q + 3))

        for x_ in (dve_s, pool_s, act_s):
            x_.close(1)

        with ExitStack() as mem, nc.Block() as block:
            CH = 4 * GW
            NCH = T * GW // CH
            adj32 = sb(mem, "adj32", [P, 2, CH], I32)
            adj8 = sb(mem, "adj8", [P, 2, CH], U8)
            xg = sb(mem, "xg", [P, R * D], F32)
            h = sb(mem, "h", [P, R * D], F32)
            hT = [sb(mem, f"hT_{p}", [P, K, GW], F16) for p in ("hi", "lo")]
            whT = [sb(mem, f"whT_{p}", [P, K, GW], F16) for p in ("hi", "lo")]
            whT32 = sb(mem, "whT32", [P, K, GW], F32)
            ex = sb(mem, "ex", [P, R, S], F32)
            asmbT = [sb(mem, f"asmbT_{p}", [P, GW], F16) for p in ("hi", "lo")]
            hsT32 = sb(mem, "hsT32", [P, K, GW], F32)
            hsT = [sb(mem, f"hsT_{p}", [P, K, GW], F16) for p in ("hi", "lo")]
            fey = sb(mem, "fey", [P, HK, GW], F32)
            feT32 = sb(mem, "feT32", [P, HK, GW], F32)
            feT = [sb(mem, f"feT_{p}", [P, HK, GW], F16) for p in ("hi", "lo")]
            mT = [sb(mem, f"mT_{p}", [P, HK, GW], F16) for p in ("hi", "lo")]
            hsr = sb(mem, "hsr", [P, R * D], F32)
            wr = sb(mem, "wr", [P, R * D], F32)
            st = sb(mem, "st", [P, R, 6], F32)
            mv = sb(mem, "mv", [P, R, 2], F32)
            ve = sb(mem, "ve", [P, R], F32)
            rstd = sb(mem, "rstd", [P, R], F32)
            nb = sb(mem, "nb", [P, R], F32)
            st2 = sb(mem, "st2", [P, R, 6], F32)
            mv2 = sb(mem, "mv2", [P, R, 2], F32)
            ve2 = sb(mem, "ve2", [P, R], F32)
            rstd2 = sb(mem, "rstd2", [P, R], F32)
            nmax = sb(mem, "nmax", [P, R], F32)
            esum = sb(mem, "esum", [P, R], F32)
            rsum = sb(mem, "rsum", [P, R], F32)
            c1 = sb(mem, "c1", [P, R], F32)

            pe_s.plan(("hT", K), ("whT", K), ("wh", R), ("bcdt", R), ("fe1", R), ("asmbT", 1), ("feT", HK),
                      ("abT", K), ("fe2", R), ("hz", 2 * HK), ("out", R))
            act_s.plan(("h", R), ("hT", K), ("whT32", K), ("whT", K), ("wh", R), ("ex", R), ("asmbT", 1),
                       ("silu", HK), ("feT", HK), ("hsT", K), ("hz", 2 * HK), ("mT", HK))
            dve_s.plan(("stats", R), ("mean", R), ("var", 1), ("nb", 1), ("hT", K), ("whT", K), ("sd", R),
                       ("softmax", 2 * R), ("rsum", R), ("asmb", R), ("stats2", R), ("mean2", R),
                       ("var2", 1), ("fey", R), ("asmbT", 1), ("hsT32", K), ("feT", HK), ("hsT", K),
                       ("mT32", HK), ("mT", HK), ("hs", R), ("w", R))
            pool_s.plan(("rstd", 1), ("adjA", 3), ("rstd2", 1), ("adjB", NCH - 3))

            def chunk_done(g, c):
                return pool_s.at(g, "adjA", c) if c < 3 else pool_s.at(g, "adjB", c - 3)

            @block.sync
            def _(sp):
                sp.dma_start(xg[:, :], a["x"][0:P, :]).then_inc(s_xin, 16)
                with sp.Fori(0, G) as g:
                    for c in range(NCH + 1):
                        if c < NCH:
                            if c >= 2:
                                sp.wait_ge(pool_s.sem, chunk_done(g, c - 2))
                            sp.dma_start(adj32[:, c % 2, :], a["adj"][ds(g * P, P), c * CH:(c + 1) * CH]
                                         ).then_inc(s_adj[c % 2], 16)
                        if c >= 1:
                            sp.wait_ge(pool_s.sem, chunk_done(g, c - 1))
                            sp.dma_start(mask_d[ds(g * P, P), (c - 1) * CH:c * CH], adj8[:, (c - 1) % 2, :]
                                         ).then_inc(s_mst[(c - 1) % 2], 16)
                    sp.wait_ge(act_s.sem, act_s.at(g, "h", R - 1))
                    sp.dma_start(xg[:, :], a["x"][ds(((g + 1) % G) * P, P), :]).then_inc(s_xin, 16)
                    sp.wait_ge(dve_s.sem, dve_s.at(g, "w", R - 1))
                    sp.dma_start(hs_d[ds(g * P, P), :], hsr[:, :]).then_inc(s_store, 16)
                    sp.dma_start(w_d[ds(g * P, P), :], wr[:, :]).then_inc(s_store, 16)
                for q in range(2):
                    sp.wait_ge(s_mst[q], 16 * G * NCH // 2)
                sp.wait_ge(s_store, 32 * G)
                sp.wait_ge(s_xin, 16 * (G + 1))

            @block.gpsimd
            def _(pool):
                def narrow(g, c, stage, i):
                    pool.wait_ge(s_adj[c % 2], g * (16 * NCH // 2) + 16 * (c // 2 + 1))
                    pool.wait_ge(s_mst[c % 2], g * (16 * NCH // 2) + 16 * (c // 2))
                    pool.sem_inc(s_pass[1], 1)
                    nc.gpsimd.tensor_copy(adj8[:, c % 2, :], adj32[:, c % 2, :]
                                          ).then_inc(pool_s.sem, pool_s.one(stage, i))

                with pool.Fori(0, G) as g:
                    pool.wait_ge(dve_s.sem, dve_s.at(g, "var"))
                    nc.gpsimd.tensor_tensor(rstd[:, :], ve[:, :], nhalf[:, 0:R], ALU.pow
                                            ).then_inc(pool_s.sem, pool_s.one("rstd"))
                    for c in range(3):
                        narrow(g, c, "adjA", c)
                    pool.wait_ge(dve_s.sem, dve_s.at(g, "var2"))
                    nc.gpsimd.tensor_tensor(rstd2[:, :], ve2[:, :], nhalf[:, 0:R], ALU.pow
                                            ).then_inc(pool_s.sem, pool_s.one("rstd2"))
                    for c in range(3, NCH):
                        narrow(g, c, "adjB", c - 3)

            @block.scalar
            def _(act):
                def hi(dst, src, stage, i):
                    nc.scalar.copy(dst, src).then_inc(act_s.sem, act_s.one(stage, i))

                with act.Fori(0, G) as g:
                    act.wait_ge(dve_s.sem, dve_s.at(g, "nb"))
                    for r in range(R):
                        nc.scalar.activation(h[:, r * D:(r + 1) * D], xg[:, r * D:(r + 1) * D], ACT.Relu,
                                             bias=nb[:, r:r + 1], scale=rstd[:, r:r + 1]
                                             ).then_inc(act_s.sem, act_s.one("h", r))
                    for k in range(K):
                        act.wait_ge(pe_s.sem, pe_s.at(g, "hT", k))
                        hi(hT[0][:, k, :], bank[k][:, :], "hT", k)
                    for k in range(K):
                        act.wait_ge(pe_s.sem, pe_s.at(g, "whT", k))
                        nc.scalar.copy(whT32[:, k, :], bank[2 + k][:, :]).then_inc(act_s.sem, act_s.one("whT32", k))
                    for k in range(K):
                        act.wait_ge(act_s.sem, act_s.at(g, "whT32", k))
                        hi(whT[0][:, k, :], whT32[:, k, :], "whT", k)
                    for r in range(R):
                        act.wait_ge(pe_s.sem, pe_s.at(g, "wh", r))
                        nc.scalar.copy(rows[:, ds(g * (R * D) + r * D, D)], bank[4 + r][:, 0:D]
                                       ).then_inc(act_s.sem, act_s.one("wh", r))
                    for r in range(R):
                        act.wait_ge(dve_s.sem, dve_s.at(g, "softmax", 2 * r + 1))
                        nc.scalar.activation(ex[:, r, :], bank[r][:, S:2 * S], ACT.Exp, bias=nmax[:, r:r + 1],
                                             scale=1.0, accum_out=esum[:, r:r + 1]
                                             ).then_inc(act_s.sem, act_s.one("ex", r))
                    act.wait_ge(pe_s.sem, pe_s.at(g, "asmbT"))
                    hi(asmbT[0][:, :], bank[0][:, :], "asmbT", 0)
                    for k in range(HK):
                        act.wait_ge(pe_s.sem, pe_s.at(g, "feT", k))
                        nc.scalar.activation(feT32[:, k, :], bank[4 + k][:, :], ACT.Silu,
                                             bias=col_b[:, FEB + k:FEB + k + 1], scale=col_b[:, FEG + k:FEG + k + 1]
                                             ).then_inc(act_s.sem, act_s.one("silu", k))
                    for k in range(HK):
                        act.wait_ge(act_s.sem, act_s.at(g, "silu", k))
                        hi(feT[0][:, k, :], feT32[:, k, :], "feT", k)
                    for k in range(K):
                        act.wait_ge(dve_s.sem, dve_s.at(g, "hsT32", k))
                        hi(hsT[0][:, k, :], hsT32[:, k, :], "hsT", k)
                    act.wait_ge(dve_s.sem, dve_s.at(g, "feT", HK - 1))
                    for m in range(HK):
                        act.wait_ge(pe_s.sem, pe_s.at(g, "hz", 2 * m))
                        nc.scalar.activation(fey[:, m, :], bank[(0, 1)[m % 2]][:, :], ACT.Identity,
                                             bias=col_b[:, BH + m:BH + m + 1], scale=1.0
                                             ).then_inc(act_s.sem, act_s.one("hz", 2 * m))
                        act.wait_ge(pe_s.sem, pe_s.at(g, "hz", 2 * m + 1))
                        nc.scalar.activation(feT32[:, m, :], bank[(3, 2)[m % 2]][:, :], ACT.Silu,
                                             bias=col_b[:, BZ + m:BZ + m + 1], scale=1.0
                                             ).then_inc(act_s.sem, act_s.one("hz", 2 * m + 1))
                    for m in range(HK):
                        act.wait_ge(dve_s.sem, dve_s.at(g, "mT32", m))
                        hi(mT[0][:, m, :], fey[:, m, :], "mT", m)

            @block.vector
            def _(dve):
                def lo(dst, src, hi_part, stage, i):
                    nc.vector.tensor_tensor(dst, src, hi_part, ALU.subtract).then_inc(dve_s.sem, dve_s.one(stage, i))

                with dve.Fori(0, G) as g:
                    dve.wait_ge(s_xin, g * 16 + 16)
                    for r in range(R):
                        nc.vector.bn_stats(st[:, r, :], xg[:, r * D:(r + 1) * D]
                                           ).then_inc(dve_s.sem, dve_s.one("stats", r))
                    dve.wait_ge(dve_s.sem, dve_s.at(g, "stats", R - 1))
                    dve.sem_inc(s_pass[0], 1)
                    for r in range(R):
                        nc.vector.bn_aggr(mv[:, r, :], st[:, r, :]).then_inc(dve_s.sem, dve_s.one("mean", r))
                    dve.wait_ge(dve_s.sem, dve_s.at(g, "mean", R - 1))
                    nc.vector.tensor_scalar(ve[:, :], mv[:, :, 1], EPS, None, ALU.add
                                            ).then_inc(dve_s.sem, dve_s.one("var"))
                    dve.wait_ge(pool_s.sem, pool_s.at(g, "rstd"))
                    nc.vector.scalar_tensor_tensor(out=nb[:, :], in0=mv[:, :, 0], scalar=-1.0, in1=rstd[:, :],
                                                   op0=ALU.mult, op1=ALU.mult
                                                   ).then_inc(dve_s.sem, dve_s.one("nb"))
                    for k in range(K):
                        dve.wait_ge(act_s.sem, act_s.at(g, "hT", k))
                        lo(hT[1][:, k, :], bank[k][:, :], hT[0][:, k, :], "hT", k)
                    for k in range(K):
                        dve.wait_ge(act_s.sem, act_s.at(g, "whT", k))
                        lo(whT[1][:, k, :], whT32[:, k, :], whT[0][:, k, :], "whT", k)
                    for r in range(R):
                        dve.wait_ge(act_s.sem, act_s.at(g, "wh", r))
                        nc.vector.tensor_copy(s_col[:, ds(g * R + r, 1)], bank[4 + r][:, D:D + 1])
                        nc.vector.tensor_copy(d_col[:, ds(g * R + r, 1)], bank[4 + r][:, D + 1:D + 2]
                                              ).then_inc(dve_s.sem, dve_s.one("sd", r))
                    for r in range(R):
                        dve.wait_ge(pe_s.sem, pe_s.at(g, "bcdt", r))
                        nc.vector.tensor_copy(c1[:, r:r + 1], bank[r][:, 2 * S:2 * S + 1]
                                              ).then_inc(dve_s.sem, dve_s.one("softmax", 2 * r))
                        nc.vector.tensor_reduce(nmax[:, r:r + 1], bank[r][:, S:2 * S], AX_X, ALU.max, negate=True
                                                ).then_inc(dve_s.sem, dve_s.one("softmax", 2 * r + 1))
                    for r in range(R):
                        dve.wait_ge(act_s.sem, act_s.at(g, "ex", r))
                        nc.vector.reciprocal(rsum[:, r:r + 1], esum[:, r:r + 1]
                                             ).then_inc(dve_s.sem, dve_s.one("rsum", r))
                    for r in range(R):
                        dve.wait_ge(dve_s.sem, dve_s.at(g, "rsum", r))
                        nc.vector.scalar_tensor_tensor(out=ex[:, r, :], in0=ex[:, r, :], scalar=rsum[:, r:r + 1],
                                                       in1=bank[r][:, 0:S], op0=ALU.mult, op1=ALU.mult
                                                       ).then_inc(dve_s.sem, dve_s.one("asmb", r))
                    for r in range(R):
                        dve.wait_ge(pe_s.sem, pe_s.at(g, "fe1", r))
                        nc.vector.bn_stats(st2[:, r, :], bank[4 + r][:, :]
                                           ).then_inc(dve_s.sem, dve_s.one("stats2", r))
                    dve.wait_ge(dve_s.sem, dve_s.at(g, "stats2", R - 1))
                    dve.sem_inc(s_pass[0], 1)
                    for r in range(R):
                        nc.vector.bn_aggr(mv2[:, r, :], st2[:, r, :]).then_inc(dve_s.sem, dve_s.one("mean2", r))
                    dve.wait_ge(dve_s.sem, dve_s.at(g, "mean2", R - 1))
                    nc.vector.tensor_scalar(ve2[:, :], mv2[:, :, 1], EPS, None, ALU.add
                                            ).then_inc(dve_s.sem, dve_s.one("var2"))
                    dve.wait_ge(pool_s.sem, pool_s.at(g, "rstd2"))
                    for r in range(R):
                        nc.vector.tensor_scalar(fey[:, r, :], bank[4 + r][:, :], mv2[:, r, 0:1], rstd2[:, r:r + 1],
                                                ALU.subtract, ALU.mult).then_inc(dve_s.sem, dve_s.one("fey", r))
                    dve.wait_ge(act_s.sem, act_s.at(g, "asmbT"))
                    lo(asmbT[1][:, :], bank[0][:, :], asmbT[0][:, :], "asmbT", 0)
                    for k in range(K):
                        dve.wait_ge(pe_s.sem, pe_s.at(g, "abT", k))
                        nc.vector.scalar_tensor_tensor(out=hsT32[:, k, :], in0=bank[1 + k][:, :],
                                                       scalar=col_b[:, BABP + k:BABP + k + 1], in1=whT32[:, k, :],
                                                       op0=ALU.add, op1=ALU.mult
                                                       ).then_inc(dve_s.sem, dve_s.one("hsT32", k))
                    for k in range(HK):
                        dve.wait_ge(act_s.sem, act_s.at(g, "feT", k))
                        lo(feT[1][:, k, :], feT32[:, k, :], feT[0][:, k, :], "feT", k)
                    for k in range(K):
                        dve.wait_ge(act_s.sem, act_s.at(g, "hsT", k))
                        lo(hsT[1][:, k, :], hsT32[:, k, :], hsT[0][:, k, :], "hsT", k)
                    for m in range(HK):
                        dve.wait_ge(act_s.sem, act_s.at(g, "hz", 2 * m + 1))
                        nc.vector.scalar_tensor_tensor(out=fey[:, m, :], in0=feT32[:, m, :], scalar=Dcol[:, :],
                                                       in1=fey[:, m, :], op0=ALU.add, op1=ALU.mult
                                                       ).then_inc(dve_s.sem, dve_s.one("mT32", m))
                    for m in range(HK):
                        dve.wait_ge(act_s.sem, act_s.at(g, "mT", m))
                        lo(mT[1][:, m, :], fey[:, m, :], mT[0][:, m, :], "mT", m)
                    dve.wait_ge(s_store, g * 32)
                    for r in range(R):
                        dve.wait_ge(pe_s.sem, pe_s.at(g, "out", r))
                        nc.vector.tensor_scalar(hsr[:, r * D:(r + 1) * D], bank[r][:, 0:D], c1[:, r:r + 1], None,
                                                ALU.mult).then_inc(dve_s.sem, dve_s.one("hs", r))
                    for r in range(R):
                        dve.wait_ge(dve_s.sem, dve_s.at(g, "hs", r))
                        nc.vector.tensor_tensor(wr[:, r * D:(r + 1) * D], bank[4 + r][:, 0:D],
                                                hsr[:, r * D:(r + 1) * D], ALU.add
                                                ).then_inc(dve_s.sem, dve_s.one("w", r))

            @block.tensor
            def _(pe):
                def cols(t, k, r):
                    return t[0][:, k, r * P:(r + 1) * P], t[1][:, k, r * P:(r + 1) * P]

                with pe.Fori(0, G) as g:
                    for k in range(K):
                        for r in range(R):
                            if k == 0:
                                pe.wait_ge(act_s.sem, act_s.at(g, "h", r))
                            last = nc.tensor.transpose(bank[k][:, r * P:(r + 1) * P],
                                                       h[:, r * D + k * P:r * D + (k + 1) * P], ident[:, :])
                        last.then_inc(pe_s.sem, pe_s.one("hT", k))
                    pe.wait_ge(dve_s.sem, dve_s.at(g, "hT", K - 1))
                    for m in range(K):
                        products(pe, bank[2 + m][:, :],
                                 [(w("W0", k, m * P, (m + 1) * P), (hT[0][:, k, :], hT[1][:, k, :]))
                                  for k in range(K)]).then_inc(pe_s.sem, pe_s.one("whT", m))
                    for r in range(R):
                        products(pe, bank[4 + r][:, 0:D + 2],
                                 [(cols(hT, k, r), w("W0", k)) for k in range(K)]
                                 ).then_inc(pe_s.sem, pe_s.one("wh", r))
                    pe.wait_ge(dve_s.sem, dve_s.at(g, "whT", K - 1))
                    pe.wait_ge(act_s.sem, act_s.at(g, "whT32", K - 1))
                    for r in range(R):
                        products(pe, bank[r][:, 0:2 * S + 1],
                                 [(cols(whT, k, r), w("bcdt", k)) for k in range(K)], "bcdt"
                                 ).then_inc(pe_s.sem, pe_s.one("bcdt", r))
                    for r in range(R):
                        pe.wait_ge(act_s.sem, act_s.at(g, "wh", r))
                        pe.wait_ge(dve_s.sem, dve_s.at(g, "sd", r))
                        products(pe, bank[4 + r][:, :],
                                 [(cols(whT, k, r), w("fe1", k)) for k in range(K)], "fe1"
                                 ).then_inc(pe_s.sem, pe_s.one("fe1", r))
                    pe.wait_ge(dve_s.sem, dve_s.at(g, "asmb", R - 1))
                    for r in range(R):
                        last = nc.tensor.transpose(bank[0][:, r * P:(r + 1) * P], ex[:, r, :], ident[:, :])
                    last.then_inc(pe_s.sem, pe_s.one("asmbT"))
                    pe.wait_ge(dve_s.sem, dve_s.at(g, "fey", R - 1))
                    for k in range(HK):
                        for r in range(R):
                            last = nc.tensor.transpose(bank[4 + k][:, r * P:(r + 1) * P],
                                                       fey[:, r, k * P:(k + 1) * P], ident[:, :])
                        last.then_inc(pe_s.sem, pe_s.one("feT", k))
                    pe.wait_ge(dve_s.sem, dve_s.at(g, "asmbT"))
                    for m in range(K):
                        products(pe, bank[1 + m][:, :],
                                 [(w("abp", 0, m * P, (m + 1) * P), (asmbT[0][:, :], asmbT[1][:, :]))]
                                 ).then_inc(pe_s.sem, pe_s.one("abT", m))
                    pe.wait_ge(dve_s.sem, dve_s.at(g, "feT", HK - 1))
                    for r in range(R):
                        products(pe, bank[4 + r][:, 0:D],
                                 [(cols(feT, k, r), w("fe2", k)) for k in range(HK)], "fe2"
                                 ).then_inc(pe_s.sem, pe_s.one("fe2", r))
                    pe.wait_ge(dve_s.sem, dve_s.at(g, "hsT", K - 1))
                    for m in range(HK):
                        if m >= 2:
                            pe.wait_ge(act_s.sem, act_s.at(g, "hz", 2 * (m - 2) + 1))
                        for j, b in ((0, (0, 1)[m % 2]), (1, (3, 2)[m % 2])):
                            c0 = j * H + m * P
                            products(pe, bank[b][:, :],
                                     [(w("hz", k, c0, c0 + P), (hsT[0][:, k, :], hsT[1][:, k, :]))
                                      for k in range(K)]).then_inc(pe_s.sem, pe_s.one("hz", 2 * m + j))
                    pe.wait_ge(dve_s.sem, dve_s.at(g, "mT", HK - 1))
                    for r in range(R):
                        products(pe, bank[r][:, 0:D],
                                 [(cols(mT, m, r), w("out", m)) for m in range(HK)], "out"
                                 ).then_inc(pe_s.sem, pe_s.one("out", r))
        for x_ in (pe_s, act_s, dve_s, pool_s):
            x_.close(G)
        stored = 32 * G
        dense_mem.close()

        V = [sb(top, f"V_{p}", [P, T * VW], F16) for p in ("hi", "lo")]

        def v_row(part, t, n=D + 1):
            return V[part][:, ds(t * VW, n)]

        def weights_and_values(slope, wh):
            with ExitStack() as mem, nc.Block() as block:
                diag = sb(mem, "diag", [P, 2, P], F32)
                v32 = sb(mem, "v32", [P, 2, D + 1], F32)
                red = sb(mem, "red", [P, 1], F32)
                dtil = sb(mem, "dtil", [P, T], F32)
                pe_s.plan(("spread", 2))
                act_s.plan(("omega", 1), ("vprime", 1))
                act_q.plan(("exp", 2), ("hi", 2))
                dve_s.plan(("red", 1), ("shift", 2), ("scale", 1))
                dve_q.plan(("diag", 2), ("relu", 2), ("v32", 2), ("gamma", 2), ("lo", 2))
                pe_q.plan(("spread", 2))
                pool_s.plan(("dmax", 1))

                @block.gpsimd
                def _(pool):
                    pool.wait_ge(dve_s.sem, dve_s.at(0, "red"))
                    nc.gpsimd.partition_all_reduce(dmax[:, 0:1], red[:, :], P, RMAX
                                                   ).then_inc(pool_s.sem, pool_s.one("dmax"))

                @block.scalar
                def _(act):
                    act.wait_ge(dve_s.sem, dve_s.at(0, "shift", 0))
                    nc.scalar.activation(omega[:, :], dtil[:, :], ACT.Exp, scale=1.0 - slope
                                         ).then_inc(act_s.sem, act_s.one("omega"))
                    nc.scalar.activation(vprime[:, :], dtil[:, :], ACT.Exp, scale=slope
                                         ).then_inc(act_s.sem, act_s.one("vprime"))
                    with act.Fori(0, T // 2) as i:
                        for q in range(2):
                            act.wait_ge(dve_q.sem, dve_q.at(i, "relu", q))
                            gam = gamma[:, ds(i * (2 * P) + q * P, P)]
                            nc.scalar.activation(gam, gam, ACT.Exp, scale=slope - 1.0
                                                 ).then_inc(act_q.sem, act_q.one("exp", q))
                        for q in range(2):
                            act.wait_ge(dve_q.sem, dve_q.at(i, "v32", q))
                            nc.scalar.copy(v_row(0, i * 2 + q), v32[:, q, :]
                                           ).then_inc(act_q.sem, act_q.one("hi", q))

                @block.vector
                def _(dve):
                    nc.vector.tensor_reduce(red[:, :], d_col[:, :], AX_X, ALU.max
                                            ).then_inc(dve_s.sem, dve_s.one("red"))
                    dve.wait_ge(pool_s.sem, pool_s.at(0, "dmax"))
                    nc.vector.tensor_scalar(dtil[:, :], d_col[:, :], dmax[:, 0:1], None, ALU.subtract
                                            ).then_inc(dve_s.sem, dve_s.one("shift", 0))
                    nc.vector.tensor_scalar(s_col[:, :], s_col[:, :], dmax[:, 0:1], None, ALU.add
                                            ).then_inc(dve_s.sem, dve_s.one("shift", 1))
                    dve.wait_ge(act_s.sem, act_s.at(0, "vprime"))
                    nc.vector.tensor_scalar(omega[:, :], omega[:, :], PSCALE, None, ALU.mult
                                            ).then_inc(dve_s.sem, dve_s.one("scale"))
                    dve.wait_ge(dve_s.sem, dve_s.at(0, "scale"))
                    with dve.Fori(0, T // 2) as i:
                        for q in range(2):
                            nc.vector.tensor_scalar(diag[:, q, :], ident[:, :], s_col[:, ds(i * 2 + q, 1)], None,
                                                    ALU.mult).then_inc(dve_q.sem, dve_q.one("diag", q))
                        for q in range(2):
                            dve.wait_ge(pe_q.sem, pe_q.at(i, "spread", q))
                            nc.vector.tensor_scalar(gamma[:, ds(i * (2 * P) + q * P, P)], bank[q][:, 0:P], 0.0, None,
                                                    ALU.max).then_inc(dve_q.sem, dve_q.one("relu", q))
                        for q in range(2):
                            nc.vector.tensor_scalar(v32[:, q, 0:D], wh[:, ds(i * (2 * D) + q * D, D)],
                                                    vprime[:, ds(i * 2 + q, 1)], None, ALU.mult)
                            nc.vector.tensor_copy(v32[:, q, D:D + 1], vprime[:, ds(i * 2 + q, 1)]
                                                  ).then_inc(dve_q.sem, dve_q.one("v32", q))
                        for q in range(2):
                            dve.wait_ge(act_q.sem, act_q.at(i, "exp", q))
                            gam = gamma[:, ds(i * (2 * P) + q * P, P)]
                            nc.vector.tensor_scalar(gam, gam, PSCALE, None, ALU.mult
                                                    ).then_inc(dve_q.sem, dve_q.one("gamma", q))
                        for q in range(2):
                            dve.wait_ge(act_q.sem, act_q.at(i, "hi", q))
                            nc.vector.tensor_tensor(v_row(1, i * 2 + q), v32[:, q, :], v_row(0, i * 2 + q),
                                                    ALU.subtract).then_inc(dve_q.sem, dve_q.one("lo", q))

                @block.tensor
                def _(pe):
                    with pe.Fori(0, T // 2) as i:
                        for q in range(2):
                            pe.wait_ge(dve_q.sem, dve_q.at(i, "diag", q))
                            nc.tensor.matmul(bank[q][:, 0:P], ones[:, :], diag[:, q, :], start=True, stop=True
                                             ).then_inc(pe_q.sem, pe_q.one("spread", q))
            act_s.close(1)
            dve_s.close(1)
            pool_s.close(1)
            for x_ in (act_q, dve_q, pe_q):
                x_.close(T // 2)

        loaded = [0]

        def aggregate(agg, weighted):
            with ExitStack() as mem, nc.Block() as block:
                mask = sb(mem, "mask", [P, 2, T * GW], U8)
                p32 = sb(mem, "p32", [P, R, GW], F32)
                ph = sb(mem, "ph", [P, R, GW], F16)
                pl = sb(mem, "pl", [P, R, GW], F16)
                rden = sb(mem, "rden", [P, R], F32)
                Q = T // R
                pe_q.plan(("pv", R))
                act_q.plan(("hi", R))
                dve_q.plan(("p32", R), ("lo", R))
                pe_s.plan(("block", 1))
                act_s.plan(("agg", R))
                dve_s.plan(("rden", R))
                masks = 16 * loaded[0]

                @block.sync
                def _(sp):
                    with sp.Fori(0, G // 2) as b:
                        for half in range(2):
                            sp.wait_ge(pe_s.sem, pe_s.before(b * 2 + half, "block", 0, 2))
                            sp.dma_start(mask[:, half, :], mask_d[ds(b * (2 * P) + half * P, P), :]
                                         ).then_inc(s_mask[half], 16)

                @block.scalar
                def _(act):
                    with act.Fori(0, G // 2) as b:
                        for half in range(2):
                            g = b * 2 + half
                            if not weighted:
                                act.wait_ge(s_mask[half], b * 16 + (masks + 16))
                            with act.Fori(0, Q) as q:
                                n = g * Q + q
                                for r in range(R):
                                    if weighted:
                                        act.wait_ge(dve_q.sem, dve_q.at(n, "p32", r))
                                        src = p32[:, r, :]
                                    else:
                                        src = mask[:, half, ds(q * (R * GW) + r * GW, GW)]
                                    act.wait_ge(pe_q.sem, pe_q.before(n, "pv", r))
                                    nc.scalar.copy(ph[:, r, :], src).then_inc(act_q.sem, act_q.one("hi", r))
                            for r in range(R):
                                act.wait_ge(dve_s.sem, dve_s.at(g, "rden", r))
                                nc.scalar.mul(agg[:, ds(g * (R * D) + r * D, D)], bank[half * R + r][:, 0:D],
                                              rden[:, r:r + 1]).then_inc(act_s.sem, act_s.one("agg", r))

                @block.vector
                def _(dve):
                    with dve.Fori(0, G // 2) as b:
                        for half in range(2):
                            g = b * 2 + half
                            if weighted:
                                dve.wait_ge(s_mask[half], b * 16 + (masks + 16))
                                dve.sem_inc(s_pass[0], 1)
                                with dve.Fori(0, Q) as q:
                                    n = g * Q + q
                                    for r in range(R):
                                        dve.wait_ge(dve_q.sem, dve_q.before(n, "lo", r))
                                        nc.vector.scalar_tensor_tensor(
                                            out=p32[:, r, :], in0=gamma[:, ds(g * GW, GW)],
                                            scalar=omega[:, ds(q * R + r, 1)],
                                            in1=mask[:, half, ds(q * (R * GW) + r * GW, GW)], op0=ALU.max,
                                            op1=ALU.mult).then_inc(dve_q.sem, dve_q.one("p32", r))
                                    for r in range(R):
                                        dve.wait_ge(act_q.sem, act_q.at(n, "hi", r))
                                        nc.vector.tensor_tensor(pl[:, r, :], p32[:, r, :], ph[:, r, :], ALU.subtract
                                                                ).then_inc(dve_q.sem, dve_q.one("lo", r))
                            dve.wait_ge(pe_s.sem, pe_s.at(g, "block"))
                            dve.wait_ge(act_s.sem, act_s.before(g, "agg", R - 1))
                            for r in range(R):
                                nc.vector.reciprocal(rden[:, r:r + 1], bank[half * R + r][:, D:D + 1]
                                                     ).then_inc(dve_s.sem, dve_s.one("rden", r))

                @block.tensor
                def _(pe):
                    def quad(g, q, half, edge=0):
                        n = g * Q + q
                        for r in range(R):
                            if weighted:
                                pe.wait_ge(dve_q.sem, dve_q.at(n, "lo", r))
                            else:
                                pe.wait_ge(act_q.sem, act_q.at(n, "hi", r))
                            first, final = edge == -1 and r == 0, edge == 1 and r == R - 1
                            t = q * R + r
                            for i in range(R):
                                acc = bank[half * R + i]
                                c = slice(i * P, (i + 1) * P)
                                nc.tensor.matmul(acc[:, 0:D + 1], ph[:, r, c], v_row(0, t), start=first, stop=False)
                                if weighted:
                                    nc.tensor.matmul(acc[:, 0:D + 1], ph[:, r, c], v_row(1, t),
                                                     start=False, stop=False)
                                    last = nc.tensor.matmul(acc[:, 0:D + 1], pl[:, r, c], v_row(0, t),
                                                            start=False, stop=final)
                                else:
                                    last = nc.tensor.matmul(acc[:, 0:D + 1], ph[:, r, c], v_row(1, t),
                                                            start=False, stop=final)
                            last.then_inc(pe_q.sem, pe_q.one("pv", r))

                    with pe.Fori(0, G // 2) as b:
                        for half in range(2):
                            g = b * 2 + half
                            pe.wait_ge(act_s.sem, act_s.before(g, "agg", R - 1, 2))
                            quad(g, 0, half, -1)
                            with pe.Fori(1, Q - 1) as q:
                                quad(g, q, half)
                            quad(g, Q - 1, half, 1)
                            pe.wait_ge(pe_q.sem, pe_q.at(g * Q + (Q - 1), "pv", R - 1))
                            pe.sem_inc(pe_s.sem, pe_s.one("block"))
            loaded[0] += G // 2
            for x_ in (act_s, dve_s, pe_s):
                x_.close(G)
            for x_ in (pe_q, act_q) + ((dve_q,) if weighted else ()):
                x_.close(G * Q)

        agg = sb(top, "agg", [P, T * D], F32)

        def value_columns(part):
            return V[part][:, :].rearrange("p (t w) -> p t w", w=VW)[:, :, D:D + 1]

        def moments(dve, g, srcs, st, mv, ve, names, ready_all=None):
            if ready_all is not None:
                dve.wait_ge(*ready_all)
                dve.sem_inc(s_pass[0], 1)
            for r, (src, ready) in enumerate(srcs):
                if ready is not None:
                    dve.wait_ge(*ready)
                nc.vector.bn_stats(st[:, r, :], src).then_inc(dve_s.sem, dve_s.one(names[0], r))
            dve.wait_ge(dve_s.sem, dve_s.at(g, names[0], R - 1))
            dve.sem_inc(s_pass[0], 1)
            for r in range(R):
                nc.vector.bn_aggr(mv[:, r, :], st[:, r, :]).then_inc(dve_s.sem, dve_s.one(names[1], r))
            dve.wait_ge(dve_s.sem, dve_s.at(g, names[1], R - 1))
            nc.vector.tensor_scalar(ve[:, :], mv[:, :, 1], EPS, None, ALU.add
                                    ).then_inc(dve_s.sem, dve_s.one(names[2]))

        def inverse_root(pool, g, rstd, ve, var, stage):
            pool.wait_ge(dve_s.sem, dve_s.at(g, var))
            nc.gpsimd.tensor_tensor(rstd[:, :], ve[:, :], nhalf[:, 0:R], ALU.pow
                                    ).then_inc(pool_s.sem, pool_s.one(stage))

        def shift(dve, g, nb, mv, rstd, stage, rstage):
            dve.wait_ge(pool_s.sem, pool_s.at(g, rstage))
            nc.vector.scalar_tensor_tensor(out=nb[:, :], in0=mv[:, :, 0], scalar=-1.0, in1=rstd[:, :],
                                           op0=ALU.mult, op1=ALU.mult).then_inc(dve_s.sem, dve_s.one(stage))

        def row(t, r, n=D):
            return t[:, r * n:(r + 1) * n]

        def grow(t, g, r):
            return t[:, ds(g * (R * D) + r * D, D)]

        def cols(t, k, r):
            return t[0][:, k, r * P:(r + 1) * P], t[1][:, k, r * P:(r + 1) * P]

        def transposes(pe, dst, src, ready=None):
            for r in range(R):
                if ready is not None:
                    pe.wait_ge(*ready(r))
                last = nc.tensor.transpose(dst[:, r * P:(r + 1) * P], src(r), ident[:, :])
            return last

        def stats_tiles(mem, name):
            return (sb(mem, f"st_{name}", [P, R, 6], F32), sb(mem, f"mv_{name}", [P, R, 2], F32),
                    sb(mem, f"ve_{name}", [P, R], F32), sb(mem, f"rstd_{name}", [P, R], F32))

        def finish_layer0():
            with ExitStack() as mem, nc.Block() as block:
                hsg = sb(mem, "hsg", [P, R * D], F32)
                wg = sb(mem, "wg", [P, R * D], F32)
                ag = sb(mem, "ag", [P, R * D], F32)
                xg = sb(mem, "xg2", [P, R * D], F32)
                cT = [sb(mem, f"cT_{p}", [P, 2 * K, GW], F16) for p in ("hi", "lo")]
                gy = sb(mem, "gy", [P, HK, GW], F32)
                sT = [sb(mem, f"sT_{p}", [P, HK, GW], F16) for p in ("hi", "lo")]
                th = sb(mem, "th", [P, R * D], F32)
                dl = sb(mem, "dl", [P, R * D], F32)
                f = sb(mem, "f", [P, R * D], F32)
                stg, mvg, veg, rsg = stats_tiles(mem, "g")
                stf, mvf, vef, rsf = stats_tiles(mem, "f")
                stx, mvx, vex, rsx = stats_tiles(mem, "x")
                nb = sb(mem, "nb2", [P, R], F32)
                pe_s.plan(("cT", 2 * K), ("g1", R), ("gT", HK), ("g2", R))
                act_s.plan(("cT", 2 * K), ("silu", HK), ("sT", HK), ("tanh", R), ("h", R), ("V", R))
                dve_s.plan(("cT", 2 * K), ("dl", R), ("gs", R), ("gm", R), ("gv", 1), ("gy", R), ("sT", HK),
                           ("u", R), ("f", R), ("fs", R), ("fm", R), ("fv", 1), ("fn", R), ("fg", R), ("fb", R),
                           ("x", R), ("xs", R), ("xm", R), ("xv", 1), ("nb", 1), ("V", R))
                pool_s.plan(("g", 1), ("f", 1), ("x", 1))
                first_in = 16 * (G + 1)

                @block.sync
                def _(sp):
                    with sp.Fori(0, G) as g:
                        sp.wait_ge(dve_s.sem, dve_s.before(g, "x", R - 1))
                        for dst, src in ((hsg, hs_d), (wg, w_d), (xg, a["x"])):
                            sp.dma_start(dst[:, :], src[ds(g * P, P), :]).then_inc(s_xin, 16)
                        sp.dma_start(ag[:, :], agg[:, ds(g * (R * D), R * D)]).then_inc(s_xin, 16)

                @block.gpsimd
                def _(pool):
                    with pool.Fori(0, G) as g:
                        inverse_root(pool, g, rsg, veg, "gv", "g")
                        inverse_root(pool, g, rsf, vef, "fv", "f")
                        inverse_root(pool, g, rsx, vex, "xv", "x")

                @block.scalar
                def _(act):
                    with act.Fori(0, G) as g:
                        for k in range(2 * K):
                            act.wait_ge(pe_s.sem, pe_s.at(g, "cT", k))
                            nc.scalar.copy(cT[0][:, k, :], bank[k][:, :]).then_inc(act_s.sem, act_s.one("cT", k))
                        act.wait_ge(pe_s.sem, pe_s.at(g, "gT", HK - 1))
                        for k in range(HK):
                            nc.scalar.activation(gy[:, k, :], bank[k][:, :], ACT.Silu,
                                                 bias=col_b[:, GB + k:GB + k + 1], scale=col_b[:, GG + k:GG + k + 1]
                                                 ).then_inc(act_s.sem, act_s.one("silu", k))
                        for k in range(HK):
                            act.wait_ge(act_s.sem, act_s.at(g, "silu", k))
                            nc.scalar.copy(sT[0][:, k, :], gy[:, k, :]).then_inc(act_s.sem, act_s.one("sT", k))
                        for r in range(R):
                            act.wait_ge(pe_s.sem, pe_s.at(g, "g2", r))
                            nc.scalar.activation(row(th, r), bank[4 + r][:, 0:D], ACT.Tanh, scale=0.5
                                                 ).then_inc(act_s.sem, act_s.one("tanh", r))
                        act.wait_ge(dve_s.sem, dve_s.at(g, "nb"))
                        for r in range(R):
                            nc.scalar.activation(row(dl, r), grow(rows, g, r), ACT.Relu, bias=nb[:, r:r + 1],
                                                 scale=rsx[:, r:r + 1]).then_inc(act_s.sem, act_s.one("h", r))
                        for r in range(R):
                            act.wait_ge(act_s.sem, act_s.at(g, "h", r))
                            nc.scalar.copy(v_row(0, g * R + r, D), row(dl, r)
                                           ).then_inc(act_s.sem, act_s.one("V", r))

                @block.vector
                def _(dve):
                    nc.vector.memset(value_columns(0), 1.0)
                    nc.vector.memset(value_columns(1), 0.0)

                    def each(stage, op):
                        for r in range(R):
                            op(r).then_inc(dve_s.sem, dve_s.one(stage, r))

                    def after(g, stage, r):
                        dve.wait_ge(dve_s.sem, dve_s.at(g, stage, r))

                    with dve.Fori(0, G) as g:
                        for k in range(2 * K):
                            dve.wait_ge(act_s.sem, act_s.at(g, "cT", k))
                            nc.vector.tensor_tensor(cT[1][:, k, :], bank[k][:, :], cT[0][:, k, :], ALU.subtract
                                                    ).then_inc(dve_s.sem, dve_s.one("cT", k))
                        dve.wait_ge(dve_s.sem, dve_s.before(g, "V", R - 1))
                        each("dl", lambda r: nc.vector.tensor_tensor(row(dl, r), grow(agg, g, r), row(hsg, r),
                                                                     ALU.subtract))
                        moments(dve, g, [(bank[4 + r][:, :], (pe_s.sem, pe_s.at(g, "g1", r))) for r in range(R)],
                                stg, mvg, veg, ("gs", "gm", "gv"))
                        dve.wait_ge(pool_s.sem, pool_s.at(g, "g"))
                        each("gy", lambda r: nc.vector.tensor_scalar(gy[:, r, :], bank[4 + r][:, :], mvg[:, r, 0:1],
                                                                     rsg[:, r:r + 1], ALU.subtract, ALU.mult))
                        for k in range(HK):
                            dve.wait_ge(act_s.sem, act_s.at(g, "sT", k))
                            nc.vector.tensor_tensor(sT[1][:, k, :], gy[:, k, :], sT[0][:, k, :], ALU.subtract
                                                    ).then_inc(dve_s.sem, dve_s.one("sT", k))
                        for r in range(R):
                            dve.wait_ge(act_s.sem, act_s.at(g, "tanh", r))
                            nc.vector.scalar_tensor_tensor(out=row(th, r), in0=row(th, r), scalar=1.0,
                                                           in1=row(dl, r), op0=ALU.add, op1=ALU.mult
                                                           ).then_inc(dve_s.sem, dve_s.one("u", r))
                        for r in range(R):
                            after(g, "u", r)
                            nc.vector.scalar_tensor_tensor(out=row(f, r), in0=row(th, r), scalar=0.5,
                                                           in1=row(wg, r), op0=ALU.mult, op1=ALU.add
                                                           ).then_inc(dve_s.sem, dve_s.one("f", r))
                        moments(dve, g, [(row(f, r), (dve_s.sem, dve_s.at(g, "f", r))) for r in range(R)],
                                stf, mvf, vef, ("fs", "fm", "fv"))
                        dve.wait_ge(pool_s.sem, pool_s.at(g, "f"))
                        each("fn", lambda r: nc.vector.tensor_scalar(row(f, r), row(f, r), mvf[:, r, 0:1],
                                                                     rsf[:, r:r + 1], ALU.subtract, ALU.mult))
                        for stage, prior, other, op in (("fg", "fn", lng, ALU.mult), ("fb", "fg", lnb, ALU.add)):
                            for r in range(R):
                                after(g, prior, r)
                                nc.vector.tensor_tensor(row(f, r), row(f, r), other[:, :], op
                                                        ).then_inc(dve_s.sem, dve_s.one(stage, r))
                        for r in range(R):
                            after(g, "fb", r)
                            nc.vector.tensor_tensor(grow(rows, g, r), row(f, r), row(xg, r), ALU.add
                                                    ).then_inc(dve_s.sem, dve_s.one("x", r))
                        moments(dve, g, [(grow(rows, g, r), None) for r in range(R)], stx, mvx, vex,
                                ("xs", "xm", "xv"), (dve_s.sem, dve_s.at(g, "x", R - 1)))
                        shift(dve, g, nb, mvx, rsx, "nb", "x")
                        for r in range(R):
                            dve.wait_ge(act_s.sem, act_s.at(g, "V", r))
                            nc.vector.tensor_tensor(v_row(1, g * R + r, D), row(dl, r), v_row(0, g * R + r, D),
                                                    ALU.subtract).then_inc(dve_s.sem, dve_s.one("V", r))

                @block.tensor
                def _(pe):
                    with pe.Fori(0, G) as g:
                        pe.wait_ge(s_xin, g * 64 + (first_in + 64))
                        for k in range(K):
                            transposes(pe, bank[k], lambda r: ag[:, r * D + k * P:r * D + (k + 1) * P]
                                       ).then_inc(pe_s.sem, pe_s.one("cT", k))
                        for k in range(K):
                            transposes(pe, bank[K + k], lambda r: hsg[:, r * D + k * P:r * D + (k + 1) * P]
                                       ).then_inc(pe_s.sem, pe_s.one("cT", K + k))
                        pe.wait_ge(dve_s.sem, dve_s.at(g, "cT", 2 * K - 1))
                        for r in range(R):
                            products(pe, bank[4 + r][:, :],
                                     [(cols(cT, k, r), w("g1", k)) for k in range(2 * K)], "g1"
                                     ).then_inc(pe_s.sem, pe_s.one("g1", r))
                        pe.wait_ge(dve_s.sem, dve_s.at(g, "gy", R - 1))
                        for k in range(HK):
                            transposes(pe, bank[k], lambda r: gy[:, r, k * P:(k + 1) * P]
                                       ).then_inc(pe_s.sem, pe_s.one("gT", k))
                        pe.wait_ge(dve_s.sem, dve_s.at(g, "sT", HK - 1))
                        for r in range(R):
                            products(pe, bank[4 + r][:, 0:D],
                                     [(cols(sT, k, r), w("g2", k)) for k in range(HK)], "g2"
                                     ).then_inc(pe_s.sem, pe_s.one("g2", r))
            for x_ in (pe_s, act_s, dve_s, pool_s):
                x_.close(G)

        def finish_layer1():
            with ExitStack() as mem, nc.Block() as block:
                ag = sb(mem, "ag1", [P, R * D], F32)
                aT = [sb(mem, f"aT_{p}", [P, K, GW], F16) for p in ("hi", "lo")]
                h = sb(mem, "h1", [P, R * D], F32)
                hT = [sb(mem, f"h1T_{p}", [P, K, GW], F16) for p in ("hi", "lo")]
                stx, mvx, vex, rsx = stats_tiles(mem, "x1")
                nb = sb(mem, "nb3", [P, R], F32)
                pe_s.plan(("aT", K), ("lin", R), ("hT", K), ("wh", R))
                act_s.plan(("aT", K), ("h", R), ("hT", K), ("wh", R))
                dve_s.plan(("aT", K), ("x", R), ("xs", R), ("xm", R), ("xv", 1), ("nb", 1), ("hT", K), ("sd", R))
                pool_s.plan(("x", 1))
                first_in = 16 * (G + 1) + 64 * G

                @block.sync
                def _(sp):
                    with sp.Fori(0, G) as g:
                        sp.wait_ge(pe_s.sem, pe_s.before(g, "aT", K - 1))
                        sp.dma_start(ag[:, :], agg[:, ds(g * (R * D), R * D)]).then_inc(s_xin, 16)

                @block.gpsimd
                def _(pool):
                    with pool.Fori(0, G) as g:
                        inverse_root(pool, g, rsx, vex, "xv", "x")

                @block.scalar
                def _(act):
                    with act.Fori(0, G) as g:
                        for k in range(K):
                            act.wait_ge(pe_s.sem, pe_s.at(g, "aT", k))
                            nc.scalar.copy(aT[0][:, k, :], bank[k][:, :]).then_inc(act_s.sem, act_s.one("aT", k))
                        act.wait_ge(dve_s.sem, dve_s.at(g, "nb"))
                        for r in range(R):
                            nc.scalar.activation(row(h, r), grow(rows, g, r), ACT.Relu, bias=nb[:, r:r + 1],
                                                 scale=rsx[:, r:r + 1]).then_inc(act_s.sem, act_s.one("h", r))
                        for k in range(K):
                            act.wait_ge(pe_s.sem, pe_s.at(g, "hT", k))
                            nc.scalar.copy(hT[0][:, k, :], bank[k][:, :]).then_inc(act_s.sem, act_s.one("hT", k))
                        for r in range(R):
                            act.wait_ge(pe_s.sem, pe_s.at(g, "wh", r))
                            nc.scalar.copy(grow(agg, g, r), bank[4 + r][:, 0:D]
                                           ).then_inc(act_s.sem, act_s.one("wh", r))

                @block.vector
                def _(dve):
                    with dve.Fori(0, G) as g:
                        for k in range(K):
                            dve.wait_ge(act_s.sem, act_s.at(g, "aT", k))
                            nc.vector.tensor_tensor(aT[1][:, k, :], bank[k][:, :], aT[0][:, k, :], ALU.subtract
                                                    ).then_inc(dve_s.sem, dve_s.one("aT", k))
                        for r in range(R):
                            dve.wait_ge(pe_s.sem, pe_s.at(g, "lin", r))
                            nc.vector.tensor_tensor(grow(rows, g, r), bank[4 + r][:, 0:D], grow(rows, g, r), ALU.add
                                                    ).then_inc(dve_s.sem, dve_s.one("x", r))
                        moments(dve, g, [(grow(rows, g, r), None) for r in range(R)], stx, mvx, vex,
                                ("xs", "xm", "xv"), (dve_s.sem, dve_s.at(g, "x", R - 1)))
                        shift(dve, g, nb, mvx, rsx, "nb", "x")
                        for k in range(K):
                            dve.wait_ge(act_s.sem, act_s.at(g, "hT", k))
                            nc.vector.tensor_tensor(hT[1][:, k, :], bank[k][:, :], hT[0][:, k, :], ALU.subtract
                                                    ).then_inc(dve_s.sem, dve_s.one("hT", k))
                        for r in range(R):
                            dve.wait_ge(act_s.sem, act_s.at(g, "wh", r))
                            nc.vector.tensor_copy(s_col[:, ds(g * R + r, 1)], bank[4 + r][:, D:D + 1])
                            nc.vector.tensor_copy(d_col[:, ds(g * R + r, 1)], bank[4 + r][:, D + 1:D + 2]
                                                  ).then_inc(dve_s.sem, dve_s.one("sd", r))

                @block.tensor
                def _(pe):
                    with pe.Fori(0, G) as g:
                        pe.wait_ge(s_xin, g * 16 + (first_in + 16))
                        for k in range(K):
                            transposes(pe, bank[k], lambda r: ag[:, r * D + k * P:r * D + (k + 1) * P]
                                       ).then_inc(pe_s.sem, pe_s.one("aT", k))
                        pe.wait_ge(dve_s.sem, dve_s.at(g, "aT", K - 1))
                        for r in range(R):
                            pe.wait_ge(dve_s.sem, dve_s.before(g, "sd", r))
                            products(pe, bank[4 + r][:, 0:D], [(cols(aT, k, r), w("W1", k)) for k in range(K)],
                                     "W1").then_inc(pe_s.sem, pe_s.one("lin", r))
                        for k in range(K):
                            transposes(pe, bank[k], lambda r: h[:, r * D + k * P:r * D + (k + 1) * P],
                                       lambda r: (act_s.sem, act_s.at(g, "h", r))
                                       ).then_inc(pe_s.sem, pe_s.one("hT", k))
                        pe.wait_ge(dve_s.sem, dve_s.at(g, "hT", K - 1))
                        for r in range(R):
                            products(pe, bank[4 + r][:, 0:D + 2], [(cols(hT, k, r), w("W2", k)) for k in range(K)]
                                     ).then_inc(pe_s.sem, pe_s.one("wh", r))
            for x_ in (pe_s, act_s, dve_s, pool_s):
                x_.close(G)

        def finish_layer2():
            with ExitStack() as mem, nc.Block() as block:
                e = sb(mem, "e", [P, R * D], F32)
                h = sb(mem, "h2", [P, R * D], F32)
                hT = [sb(mem, f"h2T_{p}", [P, K, GW], F16) for p in ("hi", "lo")]
                qT = sb(mem, "qTg", [P, 2, K, GW], F16)
                stx, mvx, vex, rsx = stats_tiles(mem, "x2")
                nb = sb(mem, "nb4", [P, R], F32)
                VB = (6, 7, 0, 1)
                pe_s.plan(("hT", K), ("qT", K), ("kT", K), ("v", R))
                act_s.plan(("e", R), ("h", R), ("hT", K), ("qT", K), ("kT", K), ("v", R))
                dve_s.plan(("mn", R), ("pos", R), ("x", R), ("xs", R), ("xm", R), ("xv", 1), ("nb", 1), ("hT", K),
                           ("qT", K), ("kT", K), ("v", R))
                pool_s.plan(("x", 1))

                @block.sync
                def _(sp):
                    with sp.Fori(0, G) as g:
                        sp.wait_ge(dve_s.sem, dve_s.at(g, "qT", K - 1))
                        sp.dma_start(qT_d[ds(g * P, P), :], qT[:, :, :, :].rearrange("p a k n -> p (a k n)")
                                     ).then_inc(s_store, 16)
                    sp.wait_ge(s_store, stored + 16 * G)

                @block.gpsimd
                def _(pool):
                    with pool.Fori(0, G) as g:
                        inverse_root(pool, g, rsx, vex, "xv", "x")

                @block.scalar
                def _(act):
                    with act.Fori(0, G) as g:
                        for r in range(R):
                            act.wait_ge(dve_s.sem, dve_s.at(g, "mn", r))
                            nc.scalar.activation(row(e, r), row(e, r), ACT.Exp
                                                 ).then_inc(act_s.sem, act_s.one("e", r))
                        act.wait_ge(dve_s.sem, dve_s.at(g, "nb"))
                        for r in range(R):
                            nc.scalar.activation(row(h, r), grow(rows, g, r), ACT.Relu, bias=nb[:, r:r + 1],
                                                 scale=rsx[:, r:r + 1]).then_inc(act_s.sem, act_s.one("h", r))
                        for k in range(K):
                            act.wait_ge(pe_s.sem, pe_s.at(g, "hT", k))
                            nc.scalar.copy(hT[0][:, k, :], bank[k][:, :]).then_inc(act_s.sem, act_s.one("hT", k))
                        act.wait_ge(s_store, g * 16 + stored)
                        for k in range(K):
                            act.wait_ge(pe_s.sem, pe_s.at(g, "qT", k))
                            nc.scalar.copy(qT[:, 0, k, :], bank[2 + k][:, :]
                                           ).then_inc(act_s.sem, act_s.one("qT", k))
                        for k in range(K):
                            act.wait_ge(pe_s.sem, pe_s.at(g, "kT", k))
                            nc.scalar.copy(kT[0][:, k, ds(g * GW, GW)], bank[4 + k][:, :]
                                           ).then_inc(act_s.sem, act_s.one("kT", k))
                        for r in range(R):
                            act.wait_ge(pe_s.sem, pe_s.at(g, "v", r))
                            nc.scalar.copy(v_row(0, g * R + r, D), bank[VB[r]][:, 0:D]
                                           ).then_inc(act_s.sem, act_s.one("v", r))

                @block.vector
                def _(dve):
                    nc.vector.memset(value_columns(0), 1.0)
                    nc.vector.memset(value_columns(1), 0.0)
                    with dve.Fori(0, G) as g:
                        for r in range(R):
                            nc.vector.tensor_scalar(row(e, r), grow(agg, g, r), 0.0, None, ALU.min
                                                    ).then_inc(dve_s.sem, dve_s.one("mn", r))
                        for r in range(R):
                            nc.vector.scalar_tensor_tensor(out=grow(rows, g, r), in0=grow(agg, g, r), scalar=0.0,
                                                           in1=grow(rows, g, r), op0=ALU.max, op1=ALU.add
                                                           ).then_inc(dve_s.sem, dve_s.one("pos", r))
                        for r in range(R):
                            dve.wait_ge(act_s.sem, act_s.at(g, "e", r))
                            dve.wait_ge(dve_s.sem, dve_s.at(g, "pos", r))
                            nc.vector.scalar_tensor_tensor(out=grow(rows, g, r), in0=row(e, r), scalar=-1.0,
                                                           in1=grow(rows, g, r), op0=ALU.add, op1=ALU.add
                                                           ).then_inc(dve_s.sem, dve_s.one("x", r))
                        moments(dve, g, [(grow(rows, g, r), None) for r in range(R)], stx, mvx, vex,
                                ("xs", "xm", "xv"), (dve_s.sem, dve_s.at(g, "x", R - 1)))
                        shift(dve, g, nb, mvx, rsx, "nb", "x")
                        for k in range(K):
                            dve.wait_ge(act_s.sem, act_s.at(g, "hT", k))
                            nc.vector.tensor_tensor(hT[1][:, k, :], bank[k][:, :], hT[0][:, k, :], ALU.subtract
                                                    ).then_inc(dve_s.sem, dve_s.one("hT", k))
                        for k in range(K):
                            dve.wait_ge(act_s.sem, act_s.at(g, "qT", k))
                            nc.vector.tensor_tensor(qT[:, 1, k, :], bank[2 + k][:, :], qT[:, 0, k, :], ALU.subtract
                                                    ).then_inc(dve_s.sem, dve_s.one("qT", k))
                        for k in range(K):
                            dve.wait_ge(act_s.sem, act_s.at(g, "kT", k))
                            c = ds(g * GW, GW)
                            nc.vector.tensor_tensor(kT[1][:, k, c], bank[4 + k][:, :], kT[0][:, k, c], ALU.subtract
                                                    ).then_inc(dve_s.sem, dve_s.one("kT", k))
                        for r in range(R):
                            dve.wait_ge(act_s.sem, act_s.at(g, "v", r))
                            nc.vector.tensor_tensor(v_row(1, g * R + r, D), bank[VB[r]][:, 0:D],
                                                    v_row(0, g * R + r, D), ALU.subtract
                                                    ).then_inc(dve_s.sem, dve_s.one("v", r))

                @block.tensor
                def _(pe):
                    with pe.Fori(0, G) as g:
                        for k in range(K):
                            transposes(pe, bank[k], lambda r: h[:, r * D + k * P:r * D + (k + 1) * P],
                                       lambda r: (act_s.sem, act_s.at(g, "h", r))
                                       ).then_inc(pe_s.sem, pe_s.one("hT", k))
                        pe.wait_ge(dve_s.sem, dve_s.at(g, "hT", K - 1))
                        for name, b in (("qT", 2), ("kT", 4)):
                            for m in range(K):
                                products(pe, bank[b + m][:, :],
                                         [(w("Wq" if b == 2 else "Wk", k, m * P, (m + 1) * P),
                                           (hT[0][:, k, :], hT[1][:, k, :])) for k in range(K)]
                                         ).then_inc(pe_s.sem, pe_s.one(name, m))
                        for r in range(R):
                            products(pe, bank[VB[r]][:, 0:D], [(cols(hT, k, r), w("Wv", k)) for k in range(K)]
                                     ).then_inc(pe_s.sem, pe_s.one("v", r))
            for x_ in (pe_s, act_s, dve_s, pool_s):
                x_.close(G)

        def row_maxima():
            with ExitStack() as mem, nc.Block() as block:
                mask = sb(mem, "mask", [P, 2, T * GW], U8)
                q_hi = spare[:, 0:2 * K * GW].rearrange("p (h k n) -> p h k n", h=2, k=K)
                m16 = sb(mem, "m16", [P, R, GW], F16)
                top_of = sb(mem, "top_of", [P, R, GW], F32)
                onto = sb(mem, "onto", [P, R, P], F32)
                Q = T // R
                pe_q.plan(("s", R))
                act_q.plan(("m16", R))
                dve_q.plan(("max", R))
                pe_s.plan(("turn", 1), ("spread", 1))
                dve_s.plan(("clear", R), ("own", R), ("loop", R), ("diag", R), ("join", 3), ("col", 1),
                           ("m", 1), ("onto", R), ("row", 1))
                masks = 16 * loaded[0]

                @block.sync
                def _(sp):
                    with sp.Fori(0, G // 2) as b:
                        for half in range(2):
                            sp.wait_ge(dve_s.sem, dve_s.before(b * 2 + half, "row", 0, 2))
                            at = ds(b * (2 * P) + half * P, P)
                            sp.dma_start(mask[:, half, :], mask_d[at, :]).then_inc(s_mask[half], 16)
                            sp.dma_start(q_hi[:, half, :, :].rearrange("p k n -> p (k n)"), qT_d[at, 0:K * GW]
                                         ).then_inc(s_qin[half], 16)

                @block.scalar
                def _(act):
                    with act.Fori(0, G // 2) as b:
                        for half in range(2):
                            g = b * 2 + half
                            act.wait_ge(dve_s.sem, dve_s.at(g, "diag", R - 1))
                            with act.Fori(0, Q) as q:
                                n = g * Q + q
                                for r in range(R):
                                    act.wait_ge(pe_q.sem, pe_q.before(n, "s", r))
                                    nc.scalar.copy(m16[:, r, :], mask[:, half, ds(q * (R * GW) + r * GW, GW)]
                                                   ).then_inc(act_q.sem, act_q.one("m16", r))

                @block.vector
                def _(dve):
                    with dve.Fori(0, G // 2) as b:
                        for half in range(2):
                            g = b * 2 + half

                            def own(r):
                                return mask[:, half, ds(g * (R * GW) + (r * GW + r * P), P)]

                            for r in range(R):
                                nc.vector.memset(top_of[:, r, :], -3.0e38
                                                 ).then_inc(dve_s.sem, dve_s.one("clear", r))
                            dve.wait_ge(s_mask[half], b * 16 + (masks + 16))
                            for r in range(R):
                                nc.vector.tensor_tensor(onto[:, r, :], own(r), ident8[:, :], ALU.mult
                                                        ).then_inc(dve_s.sem, dve_s.one("own", r))
                            for r in range(R):
                                dve.wait_ge(dve_s.sem, dve_s.at(g, "own", r))
                                nc.vector.tensor_reduce(loop_col[:, ds(g * R + r, 1)], onto[:, r, :], AX_X, ALU.max
                                                        ).then_inc(dve_s.sem, dve_s.one("loop", r))
                            for r in range(R):
                                nc.vector.tensor_tensor(own(r), own(r), ident8[:, :], ALU.max
                                                        ).then_inc(dve_s.sem, dve_s.one("diag", r))
                            dve.wait_ge(dve_s.sem, dve_s.at(g, "diag", R - 1))
                            dve.sem_inc(s_pass[0], 1)
                            with dve.Fori(0, Q) as q:
                                n = g * Q + q
                                for r in range(R):
                                    dve.wait_ge(pe_q.sem, pe_q.at(n, "s", r))
                                    dve.wait_ge(dve_q.sem, dve_q.before(n, "max", r))
                                    nc.vector.tensor_tensor(top_of[:, r, :], bank[r][:, :], top_of[:, r, :], ALU.max
                                                            ).then_inc(dve_q.sem, dve_q.one("max", r))
                            dve.wait_ge(dve_q.sem, dve_q.at(g * Q + (Q - 1), "max", R - 1))
                            nc.vector.tensor_tensor(top_of[:, 0, :], top_of[:, 0, :], top_of[:, 1, :], ALU.max
                                                    ).then_inc(dve_s.sem, dve_s.one("join", 0))
                            nc.vector.tensor_tensor(top_of[:, 2, :], top_of[:, 2, :], top_of[:, 3, :], ALU.max
                                                    ).then_inc(dve_s.sem, dve_s.one("join", 1))
                            dve.wait_ge(dve_s.sem, dve_s.at(g, "join", 1))
                            nc.vector.tensor_tensor(top_of[:, 0, :], top_of[:, 0, :], top_of[:, 2, :], ALU.max
                                                    ).then_inc(dve_s.sem, dve_s.one("join", 2))
                            dve.wait_ge(pe_s.sem, pe_s.at(g, "turn"))
                            nc.vector.tensor_reduce(m_col[:, ds(g * R, R)],
                                                    bank[4][:, :].rearrange("p (r n) -> p r n", r=R), AX_X, ALU.max
                                                    ).then_inc(dve_s.sem, dve_s.one("col"))
                            dve.wait_ge(dve_s.sem, dve_s.at(g, "col"))
                            nc.vector.tensor_scalar(m_col[:, ds(g * R, R)], m_col[:, ds(g * R, R)], BIG, None,
                                                    ALU.subtract).then_inc(dve_s.sem, dve_s.one("m"))
                            dve.wait_ge(dve_s.sem, dve_s.at(g, "m"))
                            for r in range(R):
                                nc.vector.tensor_scalar(onto[:, r, :], ident[:, :], m_col[:, ds(g * R + r, 1)], None,
                                                        ALU.mult).then_inc(dve_s.sem, dve_s.one("onto", r))
                            dve.wait_ge(pe_s.sem, pe_s.at(g, "spread"))
                            nc.vector.tensor_copy(m_row[:, ds(g * GW, GW)], bank[5][:, :]
                                                  ).then_inc(dve_s.sem, dve_s.one("row"))

                @block.tensor
                def _(pe):
                    with pe.Fori(0, G // 2) as b:
                        for half in range(2):
                            g = b * 2 + half
                            pe.wait_ge(s_qin[half], b * 16 + 16)
                            pe.sem_inc(s_pass[2], 1)
                            with pe.Fori(0, Q) as q:
                                n = g * Q + q
                                for r in range(R):
                                    pe.wait_ge(dve_q.sem, dve_q.before(n, "max", r))
                                    c = ds(q * (R * P) + r * P, P)
                                    for k in range(K):
                                        nc.tensor.matmul(bank[r][:, :], kT[0][:, k, c], q_hi[:, half, k, :],
                                                         start=(k == 0), stop=False)
                                    pe.wait_ge(act_q.sem, act_q.at(n, "m16", r))
                                    nc.tensor.matmul(bank[r][:, :], big16[:, :], m16[:, r, :], start=False,
                                                     stop=True).then_inc(pe_q.sem, pe_q.one("s", r))
                            pe.wait_ge(dve_s.sem, dve_s.at(g, "join", 2))
                            transposes(pe, bank[4], lambda r: top_of[:, 0, r * P:(r + 1) * P]
                                       ).then_inc(pe_s.sem, pe_s.one("turn"))
                            for r in range(R):
                                pe.wait_ge(dve_s.sem, dve_s.at(g, "onto", r))
                                last = nc.tensor.matmul(bank[5][:, r * P:(r + 1) * P], ones[:, :], onto[:, r, :],
                                                        start=True, stop=True)
                            last.then_inc(pe_s.sem, pe_s.one("spread"))
            loaded[0] += G // 2
            for x_ in (dve_s, pe_s):
                x_.close(G)
            for x_ in (pe_q, act_q, dve_q):
                x_.close(G * Q)

        def attend():
            with ExitStack() as mem, nc.Block() as block:
                mask = sb(mem, "mask", [P, 2, T * GW], U8)
                qh = spare[:, 0:4 * K * GW].rearrange("p (h a k n) -> p h a k n", h=2, a=2, k=K)
                p32 = sb(mem, "p32", [P, R, GW], F32)
                ph = sb(mem, "ph", [P, R, GW], F16)
                pl = sb(mem, "pl", [P, R, GW], F16)
                rden = sb(mem, "rden", [P, R], F32)
                res = w_gate[0][:, 0:2 * R * D].bitcast(F32)
                gap = w_gate[1][:, 0:2 * R * D].bitcast(F32)
                Q = T // R
                pe_l.plan(("s", R))
                pe_q.plan(("pv", R))
                act_q.plan(("exp", R), ("hi", R))
                dve_q.plan(("z", R), ("p", R), ("lo", R))
                pe_s.plan(("block", 1))
                act_s.plan(("res", R))
                dve_s.plan(("diag", R), ("rden", R), ("gap", R), ("gap2", R), ("sel", R), ("out", R))
                masks = 16 * loaded[0]
                qs = 16 * (G // 2)

                @block.sync
                def _(sp):
                    with sp.Fori(0, G // 2) as b:
                        for half in range(2):
                            g = b * 2 + half
                            sp.wait_ge(pe_s.sem, pe_s.before(g, "block", 0, 2))
                            at = ds(b * (2 * P) + half * P, P)
                            sp.dma_start(mask[:, half, :], mask_d[at, :]).then_inc(s_mask[half], 16)
                            sp.dma_start(qh[:, half, :, :, :].rearrange("p a k n -> p (a k n)"), qT_d[at, :]
                                         ).then_inc(s_qin[half], 16)
                    sp.wait_ge(s_out, 16 * G)

                @block.gpsimd
                def _(pool):
                    with pool.Fori(0, G) as g:
                        pool.wait_ge(dve_s.sem, dve_s.at(g, "out", R - 1))
                        pool.sem_inc(s_pass[1], 1)
                        nc.gpsimd.dma_start(out[ds(g * P, P), :], rows[:, ds(g * (R * D), R * D)]
                                            ).then_inc(s_out, 16)

                @block.scalar
                def _(act):
                    with act.Fori(0, G // 2) as b:
                        for half in range(2):
                            g = b * 2 + half
                            with act.Fori(0, Q) as q:
                                n = g * Q + q
                                for r in range(R):
                                    act.wait_ge(dve_q.sem, dve_q.at(n, "z", r))
                                    nc.scalar.activation(p32[:, r, :], p32[:, r, :], ACT.Exp
                                                         ).then_inc(act_q.sem, act_q.one("exp", r))
                                for r in range(R):
                                    act.wait_ge(dve_q.sem, dve_q.at(n, "p", r))
                                    act.wait_ge(pe_q.sem, pe_q.before(n, "pv", r))
                                    nc.scalar.copy(ph[:, r, :], p32[:, r, :]
                                                   ).then_inc(act_q.sem, act_q.one("hi", r))
                            for r in range(R):
                                act.wait_ge(dve_s.sem, dve_s.at(g, "rden", r))
                                nc.scalar.mul(row(res, r), bank[4 + r][:, 0:D], rden[:, r:r + 1]
                                              ).then_inc(act_s.sem, act_s.one("res", r))

                @block.vector
                def _(dve):
                    with dve.Fori(0, G // 2) as b:
                        for half in range(2):
                            g = b * 2 + half
                            dve.wait_ge(s_mask[half], b * 16 + (masks + 16))
                            for r in range(R):
                                own = mask[:, half, ds(g * (R * GW) + (r * GW + r * P), P)]
                                nc.vector.tensor_tensor(own, own, ident8[:, :], ALU.max
                                                        ).then_inc(dve_s.sem, dve_s.one("diag", r))
                            dve.wait_ge(dve_s.sem, dve_s.at(g, "diag", R - 1))
                            dve.sem_inc(s_pass[0], 1)
                            with dve.Fori(0, Q) as q:
                                n = g * Q + q
                                for r in range(R):
                                    dve.wait_ge(pe_l.sem, pe_l.at(n, "s", r))
                                    dve.wait_ge(dve_q.sem, dve_q.before(n, "lo", r))
                                    nc.vector.tensor_tensor(p32[:, r, :], bank[r][:, :], m_row[:, ds(g * GW, GW)],
                                                            ALU.subtract).then_inc(dve_q.sem, dve_q.one("z", r))
                                for r in range(R):
                                    dve.wait_ge(act_q.sem, act_q.at(n, "exp", r))
                                    nc.vector.scalar_tensor_tensor(
                                        out=p32[:, r, :], in0=p32[:, r, :], scalar=TOP,
                                        in1=mask[:, half, ds(q * (R * GW) + r * GW, GW)], op0=ALU.min, op1=ALU.mult
                                        ).then_inc(dve_q.sem, dve_q.one("p", r))
                                for r in range(R):
                                    dve.wait_ge(act_q.sem, act_q.at(n, "hi", r))
                                    nc.vector.tensor_tensor(pl[:, r, :], p32[:, r, :], ph[:, r, :], ALU.subtract
                                                            ).then_inc(dve_q.sem, dve_q.one("lo", r))
                            dve.wait_ge(pe_s.sem, pe_s.at(g, "block"))
                            for r in range(R):
                                nc.vector.reciprocal(rden[:, r:r + 1], bank[4 + r][:, D:D + 1]
                                                     ).then_inc(dve_s.sem, dve_s.one("rden", r))
                            for r in range(R):
                                dve.wait_ge(act_s.sem, act_s.at(g, "res", r))
                                nc.vector.tensor_tensor(row(gap, r), v_row(0, g * R + r, D), row(res, r), ALU.subtract
                                                        ).then_inc(dve_s.sem, dve_s.one("gap", r))
                            for r in range(R):
                                dve.wait_ge(dve_s.sem, dve_s.at(g, "gap", r))
                                nc.vector.tensor_tensor(row(gap, r), row(gap, r), v_row(1, g * R + r, D), ALU.add
                                                        ).then_inc(dve_s.sem, dve_s.one("gap2", r))
                            for r in range(R):
                                dve.wait_ge(dve_s.sem, dve_s.at(g, "gap2", r))
                                nc.vector.scalar_tensor_tensor(out=row(res, r), in0=row(gap, r),
                                                               scalar=loop_col[:, ds(g * R + r, 1)],
                                                               in1=row(res, r), op0=ALU.mult, op1=ALU.add
                                                               ).then_inc(dve_s.sem, dve_s.one("sel", r))
                            for r in range(R):
                                dve.wait_ge(dve_s.sem, dve_s.at(g, "sel", r))
                                nc.vector.tensor_tensor(grow(rows, g, r), row(res, r), grow(rows, g, r), ALU.add
                                                        ).then_inc(dve_s.sem, dve_s.one("out", r))

                @block.tensor
                def _(pe):
                    def logits(g, q, half):
                        n = g * Q + q
                        for r in range(R):
                            pe.wait_ge(dve_q.sem, dve_q.before(n, "z", r))
                            c = ds(q * (R * P) + r * P, P)
                            products(pe, bank[r][:, :],
                                     [((kT[0][:, k, c], kT[1][:, k, c]), (qh[:, half, 0, k, :], qh[:, half, 1, k, :]))
                                      for k in range(K)]).then_inc(pe_l.sem, pe_l.one("s", r))

                    def values(g, q, edge=0):
                        n = g * Q + q
                        for r in range(R):
                            pe.wait_ge(dve_q.sem, dve_q.at(n, "lo", r))
                            first, final = edge == -1 and r == 0, edge == 1 and r == R - 1
                            t = q * R + r
                            for i in range(R):
                                acc = bank[4 + i][:, 0:D + 1]
                                c = slice(i * P, (i + 1) * P)
                                nc.tensor.matmul(acc, ph[:, r, c], v_row(0, t), start=first, stop=False)
                                nc.tensor.matmul(acc, ph[:, r, c], v_row(1, t), start=False, stop=False)
                                last = nc.tensor.matmul(acc, pl[:, r, c], v_row(0, t), start=False, stop=final)
                            last.then_inc(pe_q.sem, pe_q.one("pv", r))

                    with pe.Fori(0, G // 2) as b:
                        for half in range(2):
                            g = b * 2 + half
                            pe.wait_ge(s_qin[half], b * 16 + (qs + 16))
                            logits(g, 0, half)
                            logits(g, 1, half)
                            pe.wait_ge(act_s.sem, act_s.before(g, "res", R - 1))
                            values(g, 0, -1)
                            with pe.Fori(1, Q - 1) as q:
                                logits(g, q + 1, half)
                                values(g, q)
                            values(g, Q - 1, 1)
                            pe.wait_ge(pe_q.sem, pe_q.at(g * Q + (Q - 1), "pv", R - 1))
                            pe.sem_inc(pe_s.sem, pe_s.one("block"))
            loaded[0] += G // 2
            for x_ in (dve_s, pe_s, act_s):
                x_.close(G)
            for x_ in (pe_q, act_q, dve_q, pe_l):
                x_.close(G * Q)

        def with_gamma(slope, wh):
            nonlocal gamma
            with ExitStack() as mem:
                gamma = sb(mem, "gamma", [P, N], F32)
                weights_and_values(slope, wh)
                aggregate(agg, True)

        gamma = None
        with_gamma(0.2, rows)
        finish_layer0()
        aggregate(agg, False)
        finish_layer1()
        with_gamma(0.01, agg)
        kT = [sb(top, f"kT_{p}", [P, K, N], F16) for p in ("hi", "lo")]
        finish_layer2()
        m_row = agg[:, 0:N]
        spare = agg[:, N:2 * N].bitcast(F16)
        row_maxima()
        attend()


_NAMES = ["L0_gnn_W", "L0_gnn_a_src", "L0_gnn_a_dst", "L0_gnn_W_bcdt", "L0_gnn_b_bcdt", "L0_gnn_abp_w",
          "L0_gnn_abp_b", "L0_gnn_cp_w", "L0_gnn_cp_b", "L0_gnn_W_hz", "L0_gnn_b_hz", "L0_gnn_out_w",
          "L0_gnn_out_b", "L0_gnn_fe1_w", "L0_gnn_fe1_b", "L0_gnn_fe_ln_g", "L0_gnn_fe_ln_b", "L0_gnn_fe2_w",
          "L0_gnn_fe2_b", "L0_gnn_A", "L0_gnn_D", "L0_gnn_g1_w", "L0_gnn_g1_b", "L0_gnn_g_ln_g",
          "L0_gnn_g_ln_b", "L0_gnn_g2_w", "L0_gnn_g2_b", "L0_gnn_ln_g", "L0_gnn_ln_b", "L1_gnn_b",
          "L2_gnn_W", "L2_gnn_a", "L3_gnn_Wq", "L3_gnn_Wk", "L3_gnn_Wv"]
_FLAT = ("L0_gnn_a_src", "L0_gnn_a_dst", "L0_gnn_cp_w", "L2_gnn_a")


def kernel(**inputs):
    import numpy as np
    import concourse.bacc as bacc
    from concourse.bass_utils import run_bass_kernel_spmd

    x, adj = np.asarray(inputs["x"]), np.asarray(inputs["adj"])
    arrays = {name: np.ascontiguousarray(inputs[name]) for name in _NAMES}
    for name in _FLAT:
        arrays[name] = arrays[name].reshape(-1)
    arrays["L1_gnn_WT"] = np.ascontiguousarray(np.asarray(inputs["L1_gnn_W"]).T)
    arrays["x"] = np.ascontiguousarray(x.reshape(G, R, P, D).transpose(0, 2, 1, 3)).reshape(G * P, R * D)
    arrays["adj"] = np.ascontiguousarray(adj.reshape(G, GW, T, P).transpose(0, 3, 2, 1)).reshape(G * P, T * GW)

    nc = bacc.Bacc("TRN2", target_bir_lowering=False, num_devices=1)
    aps = {name: nc.dram_tensor(f"in_{name}", v.shape, mybir.dt.from_np(v.dtype), kind="ExternalInput").ap()
           for name, v in arrays.items()}
    out = nc.dram_tensor("out_x", (G * P, R * D), F32, kind="ExternalOutput").ap()
    build(nc, aps, out)
    result = run_bass_kernel_spmd(nc, [{f"in_{name}": v for name, v in arrays.items()}], core_ids=[0])
    got = result.results[0]["out_x"]
    return np.ascontiguousarray(got.reshape(G, P, R, D).transpose(0, 2, 1, 3)).reshape(N, D)
```

```python
from contextlib import ExitStack

import concourse.bass as bass
from concourse import mybir

F32 = mybir.dt.float32
F16 = mybir.dt.float16
U8 = mybir.dt.uint8
I32 = mybir.dt.int32
ALU = mybir.AluOpType
ACT = mybir.ActivationFunctionType
AX_X = mybir.AxisListType.X
RMAX = bass.bass_isa.ReduceOp.max
ds = bass.ds

P = 128
N = 4096
D = 256
T = N // P
R = 4
G = T // R
GW = R * P
K = D // P
S = 128
H = 512
HK = H // P
VW = D + 2
EPS = 1e-5
BIG = 32768.0
PSCALE = 16384.0
START = 128
TOP = 60000.0


class Steps:

    def __init__(self, sem):
        self.sem, self.base = sem, START

    def plan(self, *stages):
        self.first, self.per, self.made = {}, 0, 0
        for name, n in stages:
            self.first[name] = self.per
            self.per += n

    def at(self, rnd, stage, i=0):
        return self.base + rnd * self.per + (self.first[stage] + i + 1)

    def before(self, rnd, stage, i=0, back=1):
        assert self.base >= back * self.per
        return self.at(rnd - back, stage, i)

    def one(self, stage, i=0):
        assert self.first[stage] + i == self.made % self.per, (stage, i, self.made % self.per)
        self.made += 1
        return 1

    def close(self, rounds):
        assert self.made % self.per == 0 and self.made
        self.base += rounds * self.per


def layout():
    dense = [("W0", K, D + 1), ("fe1", K, H), ("bcdt", K, 2 * S + 1), ("abp", 1, D), ("hz", K, 2 * H),
             ("out", HK, D), ("fe2", HK, D)]
    gate = [("g1", 2 * K, H), ("g2", HK, D)]
    later = [("W1", K, D), ("W2", K, D + 1), ("Wq", K, D), ("Wk", K, D), ("Wv", K, D)]
    where = {}
    sizes = []
    for pack, group in enumerate((dense, gate, later)):
        at = 0
        for name, k, n in group:
            where[name] = (pack, at, k, n)
            at += k * n
        sizes.append(at)
    bias, at = {}, 0
    for name, n in [("bcdt", 2 * S + 1), ("fe1", H), ("fe2", D), ("out", D), ("g1", H), ("g2", D), ("W1", D)]:
        bias[name] = (at, n)
        at += n
    return where, sizes, bias, at


def build(nc, a, out):
    where, sizes, bias_at, bias_n = layout()
    top = ExitStack()

    mask_d = nc.dram_tensor("mask_d", [G * P, T * GW], U8, kind="Internal").ap()
    x1_d, x2_d, x3_d = (nc.dram_tensor(n, [G * P, R * D], F32, kind="Internal").ap() for n in ("x1", "x2", "x3"))
    hs_d = nc.dram_tensor("hs_d", [G * P, R * D], F32, kind="Internal").ap()
    w_d = nc.dram_tensor("w_d", [G * P, R * D], F32, kind="Internal").ap()
    qT_d = nc.dram_tensor("qT_d", [G * P, 2 * K * GW], F16, kind="Internal").ap()

    named = set()

    def sb(stack, name, shape, dt):
        n = sum(x.split(".")[0] == name for x in named)
        named.add(f"{name}.{n}")
        return stack.enter_context(nc.sbuf_tensor(f"{name}_{n}" if n else name, shape, dt))

    def sem(name):
        return top.enter_context(nc.semaphore(name))

    with top:
        bank = [top.enter_context(nc.psum_tensor(f"bank{i}", [P, 512], F32)) for i in range(8)]
        pe_s, act_s, dve_s, pool_s = (Steps(sem(n)) for n in ("pe_done", "act_done", "dve_done", "pool_done"))
        pe_q, act_q, dve_q = (Steps(sem(n)) for n in ("pe_quad_done", "act_quad_done", "dve_quad_done"))
        pe_l = Steps(sem("pe_logits_done"))
        pre_s, act_v, dve_v = (Steps(sem(n)) for n in ("bounds_done", "act_values_done", "dve_values_done"))
        next_pe, next_act, next_dve, next_pool = (Steps(sem(f"{n}_next_done")) for n in ("pe", "act", "dve", "pool"))
        steps = (pe_s, act_s, dve_s, pool_s, pe_q, act_q, dve_q, pe_l, pre_s, act_v, dve_v,
                 next_pe, next_act, next_dve, next_pool)
        s_in = sem("inputs_loaded")
        s_mst = sem("mask_stored")
        s_xin = sem("x_loaded")
        s_mask = [sem(f"mask_quad_loaded_{i}") for i in range(4)]
        s_whole = [sem("mask_loaded_0"), sem("mask_loaded_1")]
        s_qin = [sem("q_loaded_0"), sem("q_loaded_1")]
        s_store = sem("rows_stored")
        s_xout = sem("x_stored")
        s_out = sem("out_stored")
        s_pass = [sem("dve_passed"), sem("pool_passed"), sem("pe_passed"), sem("sp_passed")]

        ident = sb(top, "ident", [P, P], F32)
        ident8 = sb(top, "ident8", [P, P], U8)
        ones = sb(top, "ones", [P, P], F32)
        ones16 = sb(top, "ones16", [P, P], F16)
        big16 = sb(top, "big16", [P, P], F16)
        bias3 = sb(top, "bias3", [P, bias_n], F16)
        col_b = sb(top, "col_b", [P, 30], F32)
        lng = sb(top, "lng", [P, D], F32)
        lnb = sb(top, "lnb", [P, D], F32)
        nhalf = sb(top, "nhalf", [P, 8], F32)
        Dcol = sb(top, "Dcol", [P, 1], F32)
        w_src = sb(top, "w_src", [P, 2, K, 2, P], F16)
        d_col = sb(top, "d_col", [P, T], F32)
        omega = sb(top, "omega", [P, T], F32)
        vprime = sb(top, "vprime", [P, T], F32)
        m_col = sb(top, "m_col", [P, T], F32)
        loop_col = sb(top, "loop_col", [P, T], F32)
        dmax = sb(top, "dmax", [P, 2], F32)
        w_later = [sb(top, f"w_later_{p}", [P, sizes[2]], F16) for p in ("hi", "lo")]

        w_gate = [sb(top, f"w_gate_{p}", [P, sizes[1]], F16) for p in ("hi", "lo")]
        VA = sb(top, "VA", [P, 2 * T * VW], F16)
        VB = sb(top, "VB", [P, 2 * T * VW], F16)
        s_row = sb(top, "s_row", [P, N], F32)

        def value(t):
            return t[:, :]

        def rows_of(t):
            return t[:, 0:2 * T * D].bitcast(F32)

        dense_mem = ExitStack()
        w_dense = [sb(dense_mem, f"w_dense_{p}", [P, sizes[0]], F16) for p in ("hi", "lo")]
        packs = (w_dense, w_gate, w_later)
        BZ, BH, BABP, FEG, FEB, GG, GB = 0, 4, 8, 10, 14, 18, 22

        def w(name, k, c0=0, c1=None):
            pack, at, _, n = where[name]
            at += k * n
            c1 = n if c1 is None else c1
            return packs[pack][0][:, at + c0:at + c1], packs[pack][1][:, at + c0:at + c1]

        def products(pe, out_ap, pairs, bias=None):
            todo = []
            for (sh, sl), (mh, ml) in pairs:
                todo += [(sh, mh), (sh, ml), (sl, mh)]
            if bias is not None:
                at, n = bias_at[bias]
                todo.append((ones16[:, :], bias3[:, at:at + n]))
            for i, (st, mv) in enumerate(todo):
                last = nc.tensor.matmul(out_ap, st, mv, start=(i == 0), stop=(i == len(todo) - 1))
            return last

        def source_rows(pe, layer, hT, out_bank):
            return products(pe, out_bank[:, :],
                            [((w_src[:, layer, k, 0, :], w_src[:, layer, k, 1, :]), (hT[0][:, k, :], hT[1][:, k, :]))
                             for k in range(K)])

        with ExitStack() as mem, nc.Block() as block:
            stage = [VA[:, 0:2 * sizes[0]].bitcast(F32), VB[:, 0:2 * sizes[1]].bitcast(F32),
                     VB[:, 2 * sizes[1]:2 * (sizes[1] + sizes[2])].bitcast(F32)]
            src_col = sb(mem, "src_col", [P, 2, K], F32)
            wc = sb(mem, "wc", [P, K, S], F32)
            junk = sb(mem, "junk", [P, 11, D], F32)
            vecs = sb(mem, "vecs", [P, 4 * D], F32)
            cpw = sb(mem, "cpw", [P, S], F32)
            bc = sb(mem, "bc", [P, S], F32)
            arow = sb(mem, "arow", [P, S], F32)
            cpb = sb(mem, "cpb", [P, 2], F32)
            brow = sb(mem, "brow", [P, bias_n], F32)
            part = sb(mem, "part", [P, bias_n], F16)
            acc3 = sb(mem, "acc3", [P, bias_n], F32)
            loads = []

            def stage_w(name, src, c0=0, n=None):
                pack, at, k, width = where[name]
                view = stage[pack][:, at:at + k * width].rearrange("p (k n) -> p k n", k=k)
                n = src.shape[1] if n is None else n
                loads.append((view[:, :, c0:c0 + n], src.rearrange("(k p) n -> p k n", p=P)))

            stage_w("W0", a["L0_gnn_W"])
            stage_w("fe1", a["L0_gnn_fe1_w"])
            stage_w("bcdt", a["L0_gnn_W_bcdt"][:, 0:S], 0)
            stage_w("bcdt", a["L0_gnn_W_bcdt"][:, 2 * S:3 * S], S)
            stage_w("abp", a["L0_gnn_abp_w"])
            stage_w("hz", a["L0_gnn_W_hz"])
            stage_w("out", a["L0_gnn_out_w"])
            stage_w("fe2", a["L0_gnn_fe2_w"])
            stage_w("g1", a["L0_gnn_g1_w"])
            stage_w("g2", a["L0_gnn_g2_w"])
            stage_w("W1", a["L1_gnn_WT"])
            stage_w("W2", a["L2_gnn_W"])
            stage_w("Wq", a["L3_gnn_Wq"])
            stage_w("Wk", a["L3_gnn_Wk"])
            stage_w("Wv", a["L3_gnn_Wv"])
            loads.append((wc[:, :, :], a["L0_gnn_W_bcdt"][:, S:2 * S].rearrange("(k p) n -> p k n", p=P)))

            def spread(dst, vec):
                loads.append((dst, vec.partition_broadcast(P)))

            spread(vecs[:, 0:D], a["L0_gnn_a_src"])
            spread(vecs[:, D:2 * D], a["L0_gnn_a_dst"])
            spread(vecs[:, 2 * D:4 * D], a["L2_gnn_a"])
            spread(cpw[:, :], a["L0_gnn_cp_w"])
            spread(bc[:, :], a["L0_gnn_b_bcdt"][S:2 * S])
            spread(arow[:, :], a["L0_gnn_A"])
            spread(cpb[:, 0:1], a["L0_gnn_cp_b"])
            spread(Dcol[:, :], a["L0_gnn_D"])
            spread(lng[:, :], a["L0_gnn_ln_g"])
            spread(lnb[:, :], a["L0_gnn_ln_b"])
            spread(brow[:, 0:S], a["L0_gnn_b_bcdt"][0:S])
            spread(brow[:, S:2 * S], a["L0_gnn_b_bcdt"][2 * S:3 * S])
            for name, vec in (("fe1", "L0_gnn_fe1_b"), ("fe2", "L0_gnn_fe2_b"), ("out", "L0_gnn_out_b"),
                              ("g1", "L0_gnn_g1_b"), ("g2", "L0_gnn_g2_b"), ("W1", "L1_gnn_b")):
                at, n = bias_at[name]
                spread(brow[:, at:at + n], a[vec])
            for at, vec in ((BH, a["L0_gnn_b_hz"][0:H]), (BZ, a["L0_gnn_b_hz"][H:2 * H]), (BABP, a["L0_gnn_abp_b"]),
                            (FEG, a["L0_gnn_fe_ln_g"]), (FEB, a["L0_gnn_fe_ln_b"]),
                            (GG, a["L0_gnn_g_ln_g"]), (GB, a["L0_gnn_g_ln_b"])):
                n = vec.shape[0] // P
                loads.append((col_b[:, at:at + n], vec.rearrange("(k p) -> p k", p=P)))

            dve_s.plan(("fold", 9), ("src", 4), ("ones", 1), ("split", 3), ("big", 1), ("parts", 8))
            pool_s.plan(("zero", 3), ("ident", 2), ("one", 1))
            act_s.plan(("hi", 3))

            @block.sync
            def _(sp):
                for x_ in steps:
                    sp.sem_inc(x_.sem, START)
                for dst, src in loads:
                    with nc.allow_non_contiguous_dma(reason="small vectors"):
                        sp.dma_start(dst, src).then_inc(s_in, 16)

            @block.gpsimd
            def _(pool):
                nc.gpsimd.memset(ident[:, :], 0.0).then_inc(pool_s.sem, pool_s.one("zero", 0))
                nc.gpsimd.memset(ones[:, :], 1.0).then_inc(pool_s.sem, pool_s.one("zero", 1))
                nc.gpsimd.memset(nhalf[:, :], -0.5).then_inc(pool_s.sem, pool_s.one("zero", 2))
                pool.wait_ge(pool_s.sem, pool_s.at(0, "zero", 0))
                nc.gpsimd.affine_select(out=ident[:, :], in_=ident[:, :], compare_op=ALU.not_equal, fill=1.0,
                                        base=0, pattern=[[-1, P]], channel_multiplier=1
                                        ).then_inc(pool_s.sem, pool_s.one("ident", 0))
                pool.wait_ge(pool_s.sem, pool_s.at(0, "ident", 0))
                nc.gpsimd.tensor_copy(ident8[:, :], ident[:, :]).then_inc(pool_s.sem, pool_s.one("ident", 1))
                nc.gpsimd.tensor_copy(ones16[:, :], ones[:, :]).then_inc(pool_s.sem, pool_s.one("one", 0))

            @block.scalar
            def _(act):
                for i in range(3):
                    act.wait_ge(s_in, 16 * len(loads))
                    act.wait_ge(dve_s.sem, dve_s.at(0, "fold", 8))
                    nc.scalar.copy(packs[i][0][:, :], stage[i][:, :]).then_inc(act_s.sem, act_s.one("hi", i))

            @block.vector
            def _(dve):
                dve.wait_ge(s_in, 16 * len(loads))
                n = 0
                for layer, (name, off) in enumerate((("W0", 0), ("W2", 2 * D))):
                    pack, at, k_, width = where[name]
                    for k in range(K):
                        for j in range(2):
                            base = at + k * width
                            ins = nc.vector.tensor_tensor_reduce(
                                out=junk[:, n, :], in0=stage[pack][:, base:base + D],
                                in1=vecs[:, off + j * D:off + (j + 1) * D], scale=1.0, scalar=0.0,
                                op0=ALU.mult, op1=ALU.add, accum_out=stage[pack][:, base + D:base + D + 1] if j else
                                src_col[:, layer, k:k + 1])
                            ins.then_inc(dve_s.sem, dve_s.one("fold", n))
                            n += 1
                pack, at, k_, width = where["bcdt"]
                for k in range(K):
                    last = nc.vector.tensor_tensor_reduce(
                        out=junk[:, 8 + k, 0:S], in0=wc[:, k, :], in1=cpw[:, :], scale=1.0, scalar=0.0, op0=ALU.mult,
                        op1=ALU.add, accum_out=stage[pack][:, at + k * width + 2 * S:at + k * width + 2 * S + 1])
                last.then_inc(dve_s.sem, dve_s.one("fold", 8))
                dve.wait_ge(dve_s.sem, dve_s.at(0, "fold", 8))
                dve.wait_ge(pool_s.sem, pool_s.at(0, "one"))
                n = 0
                for layer in range(2):
                    for k in range(K):
                        col, (hi_part, lo_part) = src_col[:, layer, k:k + 1], (w_src[:, layer, k, i, :] for i in range(2))
                        nc.vector.tensor_scalar(hi_part, ones[:, :], col, None, ALU.mult
                                                ).then_inc(dve_s.sem, dve_s.one("src", n))
                        dve.wait_ge(dve_s.sem, dve_s.at(0, "src", n))
                        last = nc.vector.scalar_tensor_tensor(out=lo_part, in0=ones[:, :], scalar=col, in1=hi_part,
                                                              op0=ALU.mult, op1=ALU.subtract)
                        n += 1
                nc.vector.tensor_tensor_reduce(
                    out=junk[:, 10, 0:S], in0=bc[:, :], in1=cpw[:, :], scale=1.0, scalar=1.0, op0=ALU.mult,
                    op1=ALU.add, accum_out=cpb[:, 1:2]).then_inc(dve_s.sem, dve_s.one("ones"))
                for i in range(3):
                    dve.wait_ge(act_s.sem, act_s.at(0, "hi", i))
                    nc.vector.tensor_tensor(packs[i][1][:, :], stage[i][:, :], packs[i][0][:, :], ALU.subtract
                                            ).then_inc(dve_s.sem, dve_s.one("split", i))
                dve.wait_ge(pool_s.sem, pool_s.at(0, "one"))
                nc.vector.tensor_scalar(big16[:, :], ident[:, :], BIG, None, ALU.mult
                                        ).then_inc(dve_s.sem, dve_s.one("big"))
                dve.wait_ge(dve_s.sem, dve_s.at(0, "ones"))
                nc.vector.tensor_tensor(brow[:, 2 * S:2 * S + 1], cpb[:, 0:1], cpb[:, 1:2], ALU.add
                                        ).then_inc(dve_s.sem, dve_s.one("parts", 0))
                nc.vector.tensor_tensor(brow[:, S:2 * S], brow[:, S:2 * S], arow[:, :], ALU.add
                                        ).then_inc(dve_s.sem, dve_s.one("parts", 1))
                for q in range(3):
                    dve.wait_ge(dve_s.sem, dve_s.at(0, "parts", 2 * q + 1))
                    nc.vector.tensor_copy(part[:, :], brow[:, :]).then_inc(dve_s.sem, dve_s.one("parts", 2 * q + 2))
                    dve.wait_ge(dve_s.sem, dve_s.at(0, "parts", 2 * q + 2))
                    if q == 0:
                        nc.vector.tensor_scalar(acc3[:, :], part[:, :], ident[:, 0:1], None, ALU.mult)
                    if q == 1:
                        nc.vector.scalar_tensor_tensor(out=acc3[:, :], in0=part[:, :], scalar=ident[:, 1:2],
                                                       in1=acc3[:, :], op0=ALU.mult, op1=ALU.add)
                    if q == 2:
                        nc.vector.scalar_tensor_tensor(out=bias3[:, :], in0=part[:, :], scalar=ident[:, 2:3],
                                                       in1=acc3[:, :], op0=ALU.mult, op1=ALU.add
                                                       ).then_inc(dve_s.sem, dve_s.one("parts", 7))
                    else:
                        nc.vector.tensor_tensor(brow[:, :], brow[:, :], part[:, :], ALU.subtract
                                                ).then_inc(dve_s.sem, dve_s.one("parts", 2 * q + 3))

        for x_ in (dve_s, pool_s, act_s):
            x_.close(1)

        with ExitStack() as mem, nc.Block() as block:
            wh = rows_of(VB)
            xg = sb(mem, "xg", [P, R * D], F32)
            h = sb(mem, "h", [P, R * D], F32)
            hT = [sb(mem, f"hT_{p}", [P, K, GW], F16) for p in ("hi", "lo")]
            whT = [sb(mem, f"whT_{p}", [P, K, GW], F16) for p in ("hi", "lo")]
            whT32 = sb(mem, "whT32", [P, K, GW], F32)
            ex = sb(mem, "ex", [P, R, S], F32)
            asmbT = [sb(mem, f"asmbT_{p}", [P, GW], F16) for p in ("hi", "lo")]
            hsT32 = sb(mem, "hsT32", [P, K, GW], F32)
            hsT = [sb(mem, f"hsT_{p}", [P, K, GW], F16) for p in ("hi", "lo")]
            hp = sb(mem, "hp", [P, HK, GW], F32)
            part16 = [VA[:, i * HK * GW:(i + 1) * HK * GW] for i in range(8)]
            whole32 = [VA[:, 2 * i * HK * GW:2 * (i + 1) * HK * GW].bitcast(F32) for i in range(2)]
            as_tiles = lambda t: t.rearrange("p (k n) -> p k n", k=HK)
            fey, feT32 = as_tiles(whole32[0]), as_tiles(whole32[1])
            feT = [as_tiles(part16[4]), as_tiles(part16[5])]
            mT = [as_tiles(part16[6]), as_tiles(part16[7])]
            hsr = sb(mem, "hsr", [P, R * D], F32)
            wr = sb(mem, "wr", [P, R * D], F32)
            st = sb(mem, "st", [P, R, 6], F32)
            mv = sb(mem, "mv", [P, R, 2], F32)
            ve = sb(mem, "ve", [P, R], F32)
            rstd = sb(mem, "rstd", [P, R], F32)
            nb = sb(mem, "nb", [P, R], F32)
            st2 = sb(mem, "st2", [P, R, 6], F32)
            mv2 = sb(mem, "mv2", [P, R, 2], F32)
            ve2 = sb(mem, "ve2", [P, R], F32)
            rstd2 = sb(mem, "rstd2", [P, R], F32)
            nmax = sb(mem, "nmax", [P, R], F32)
            esum = sb(mem, "esum", [P, R], F32)
            rsum = sb(mem, "rsum", [P, R], F32)
            c1 = sb(mem, "c1", [P, R], F32)

            pe_s.plan(("whT", K), ("srow", 1), ("wh", R), ("bcdt", R), ("fe1", R), ("asmbT", 1),
                      ("abT", K), ("hz", 2 * HK), ("feT", HK), ("out", R), ("fe2", R))
            act_s.plan(("whT32", K), ("whT", K), ("srow", 1), ("wh", R), ("ex", R), ("asmbT", 1),
                       ("hsT", K), ("hz", 2 * HK), ("mT", HK), ("silu", HK), ("feT", HK))
            dve_s.plan(("whT", K), ("d", R), ("softmax", 2 * R), ("rsum", R), ("asmb", R), ("asmbT", 1),
                       ("hsT32", K), ("hsT", K), ("stats2", R), ("mean2", R), ("var2", 1), ("fey", R),
                       ("mT32", HK), ("mT", HK), ("feT", HK), ("hs", 2), ("w", 2))
            pool_s.plan(("rstd2", 1))
            next_pe.plan(("hT", K))
            next_act.plan(("h", R), ("hT", K))
            next_dve.plan(("stats", R), ("mean", R), ("var", 1), ("nb", 1), ("hT", K))
            next_pool.plan(("rstd", 1))

            @block.sync
            def _(sp):
                sp.dma_start(xg[:, :], a["x"][0:P, :]).then_inc(s_xin, 16)
                sp.wait_ge(next_act.sem, next_act.at(0, "h", R - 1))
                sp.dma_start(xg[:, :], a["x"][P:2 * P, :]).then_inc(s_xin, 16)
                with sp.Fori(0, G) as g:
                    sp.wait_ge(next_act.sem, next_act.at(g + 1, "h", R - 1))
                    sp.sem_inc(s_pass[3], 1)
                    sp.dma_start(xg[:, :], a["x"][ds(((g + 2) % G) * P, P), :]).then_inc(s_xin, 16)
                    sp.wait_ge(dve_s.sem, dve_s.at(g, "w", 1))
                    sp.sem_inc(s_pass[3], 1)
                    sp.dma_start(hs_d[ds(g * P, P), :], hsr[:, :]).then_inc(s_store, 16)
                    sp.dma_start(w_d[ds(g * P, P), :], wr[:, :]).then_inc(s_store, 16)
                sp.wait_ge(s_store, 32 * G)
                sp.wait_ge(s_xin, 16 * (G + 2))

            @block.gpsimd
            def _(pool):
                def next_root(g):
                    pool.wait_ge(next_dve.sem, next_dve.at(g, "var"))
                    nc.gpsimd.tensor_tensor(rstd[:, :], ve[:, :], nhalf[:, 0:R], ALU.pow
                                            ).then_inc(next_pool.sem, next_pool.one("rstd"))

                next_root(0)
                with pool.Fori(0, G) as g:
                    nc.gpsimd.dma_start(mask_d[ds(g * P, P), :], a["adj"][ds(g * P, P), :]).then_inc(s_mst, 16)
                    pool.wait_ge(dve_s.sem, dve_s.at(g, "var2"))
                    nc.gpsimd.tensor_tensor(rstd2[:, :], ve2[:, :], nhalf[:, 0:R], ALU.pow
                                            ).then_inc(pool_s.sem, pool_s.one("rstd2"))
                    next_root(g + 1)
                pool.wait_ge(s_mst, 16 * G)

            @block.scalar
            def _(act):
                def hi(dst, src, stage, i):
                    nc.scalar.copy(dst, src).then_inc(act_s.sem, act_s.one(stage, i))

                def next_h(g):
                    act.wait_ge(next_dve.sem, next_dve.at(g, "nb"))
                    for r in range(R):
                        nc.scalar.activation(h[:, r * D:(r + 1) * D], xg[:, r * D:(r + 1) * D], ACT.Relu,
                                             bias=nb[:, r:r + 1], scale=rstd[:, r:r + 1]
                                             ).then_inc(next_act.sem, next_act.one("h", r))

                def next_hT(g):
                    for k in range(K):
                        act.wait_ge(next_pe.sem, next_pe.at(g, "hT", k))
                        nc.scalar.copy(hT[0][:, k, :], bank[2 + k][:, :]
                                       ).then_inc(next_act.sem, next_act.one("hT", k))

                next_h(0)
                next_hT(0)
                with act.Fori(0, G) as g:
                    for k in range(K):
                        act.wait_ge(pe_s.sem, pe_s.at(g, "whT", k))
                        nc.scalar.copy(whT32[:, k, :], bank[k][:, :]).then_inc(act_s.sem, act_s.one("whT32", k))
                    for k in range(K):
                        act.wait_ge(act_s.sem, act_s.at(g, "whT32", k))
                        hi(whT[0][:, k, :], whT32[:, k, :], "whT", k)
                    act.wait_ge(pe_s.sem, pe_s.at(g, "srow"))
                    nc.scalar.copy(s_row[:, ds(g * GW, GW)], bank[2][:, :]
                                   ).then_inc(act_s.sem, act_s.one("srow"))
                    for r in range(R):
                        act.wait_ge(pe_s.sem, pe_s.at(g, "wh", r))
                        nc.scalar.copy(wh[:, ds(g * (R * D) + r * D, D)], bank[4 + r][:, 0:D]
                                       ).then_inc(act_s.sem, act_s.one("wh", r))
                    for r in range(R):
                        act.wait_ge(dve_s.sem, dve_s.at(g, "softmax", 2 * r + 1))
                        nc.scalar.activation(ex[:, r, :], bank[r][:, S:2 * S], ACT.Exp, bias=nmax[:, r:r + 1],
                                             scale=1.0, accum_out=esum[:, r:r + 1]
                                             ).then_inc(act_s.sem, act_s.one("ex", r))
                    act.wait_ge(pe_s.sem, pe_s.at(g, "asmbT"))
                    hi(asmbT[0][:, :], bank[0][:, :], "asmbT", 0)
                    for k in range(K):
                        act.wait_ge(dve_s.sem, dve_s.at(g, "hsT32", k))
                        hi(hsT[0][:, k, :], hsT32[:, k, :], "hsT", k)
                    for m in range(HK):
                        act.wait_ge(pe_s.sem, pe_s.at(g, "hz", 2 * m))
                        nc.scalar.activation(hp[:, m, :], bank[(0, 1)[m % 2]][:, :], ACT.Identity,
                                             bias=col_b[:, BH + m:BH + m + 1], scale=1.0
                                             ).then_inc(act_s.sem, act_s.one("hz", 2 * m))
                        act.wait_ge(pe_s.sem, pe_s.at(g, "hz", 2 * m + 1))
                        nc.scalar.activation(feT32[:, m, :], bank[(3, 2)[m % 2]][:, :], ACT.Silu,
                                             bias=col_b[:, BZ + m:BZ + m + 1], scale=1.0
                                             ).then_inc(act_s.sem, act_s.one("hz", 2 * m + 1))
                    for m in range(HK):
                        act.wait_ge(dve_s.sem, dve_s.at(g, "mT32", m))
                        hi(mT[0][:, m, :], hp[:, m, :], "mT", m)
                    for k in range(HK):
                        act.wait_ge(pe_s.sem, pe_s.at(g, "feT", k))
                        nc.scalar.activation(feT32[:, k, :], bank[4 + k][:, :], ACT.Silu,
                                             bias=col_b[:, FEB + k:FEB + k + 1], scale=col_b[:, FEG + k:FEG + k + 1]
                                             ).then_inc(act_s.sem, act_s.one("silu", k))
                    for k in range(HK):
                        act.wait_ge(act_s.sem, act_s.at(g, "silu", k))
                        hi(feT[0][:, k, :], feT32[:, k, :], "feT", k)
                    next_h(g + 1)
                    next_hT(g + 1)

            @block.vector
            def _(dve):
                def lo(dst, src, hi_part, stage, i):
                    nc.vector.tensor_tensor(dst, src, hi_part, ALU.subtract).then_inc(dve_s.sem, dve_s.one(stage, i))

                def next_moments(g):
                    dve.wait_ge(s_xin, g * 16 + 16)
                    dve.sem_inc(s_pass[0], 1)
                    for r in range(R):
                        nc.vector.bn_stats(st[:, r, :], xg[:, r * D:(r + 1) * D]
                                           ).then_inc(next_dve.sem, next_dve.one("stats", r))
                    dve.wait_ge(next_dve.sem, next_dve.at(g, "stats", R - 1))
                    dve.sem_inc(s_pass[0], 1)
                    for r in range(R):
                        nc.vector.bn_aggr(mv[:, r, :], st[:, r, :]).then_inc(next_dve.sem, next_dve.one("mean", r))
                    dve.wait_ge(next_dve.sem, next_dve.at(g, "mean", R - 1))
                    nc.vector.tensor_scalar(ve[:, :], mv[:, :, 1], EPS, None, ALU.add
                                            ).then_inc(next_dve.sem, next_dve.one("var"))

                def next_nb(g):
                    dve.wait_ge(next_pool.sem, next_pool.at(g, "rstd"))
                    nc.vector.scalar_tensor_tensor(out=nb[:, :], in0=mv[:, :, 0], scalar=-1.0, in1=rstd[:, :],
                                                   op0=ALU.mult, op1=ALU.mult
                                                   ).then_inc(next_dve.sem, next_dve.one("nb"))

                def next_hT(g):
                    for k in range(K):
                        dve.wait_ge(next_act.sem, next_act.at(g, "hT", k))
                        nc.vector.tensor_tensor(hT[1][:, k, :], bank[2 + k][:, :], hT[0][:, k, :], ALU.subtract
                                                ).then_inc(next_dve.sem, next_dve.one("hT", k))

                next_moments(0)
                next_nb(0)
                next_hT(0)
                with dve.Fori(0, G) as g:
                    for k in range(K):
                        dve.wait_ge(act_s.sem, act_s.at(g, "whT", k))
                        lo(whT[1][:, k, :], whT32[:, k, :], whT[0][:, k, :], "whT", k)
                    for r in range(R):
                        dve.wait_ge(act_s.sem, act_s.at(g, "wh", r))
                        nc.vector.tensor_copy(d_col[:, ds(g * R + r, 1)], bank[4 + r][:, D:D + 1]
                                              ).then_inc(dve_s.sem, dve_s.one("d", r))
                    for r in range(R):
                        dve.wait_ge(pe_s.sem, pe_s.at(g, "bcdt", r))
                        nc.vector.tensor_copy(c1[:, r:r + 1], bank[r][:, 2 * S:2 * S + 1]
                                              ).then_inc(dve_s.sem, dve_s.one("softmax", 2 * r))
                        nc.vector.tensor_reduce(nmax[:, r:r + 1], bank[r][:, S:2 * S], AX_X, ALU.max, negate=True
                                                ).then_inc(dve_s.sem, dve_s.one("softmax", 2 * r + 1))
                    for r in range(R):
                        dve.wait_ge(act_s.sem, act_s.at(g, "ex", r))
                        nc.vector.reciprocal(rsum[:, r:r + 1], esum[:, r:r + 1]
                                             ).then_inc(dve_s.sem, dve_s.one("rsum", r))
                    for r in range(R):
                        dve.wait_ge(dve_s.sem, dve_s.at(g, "rsum", r))
                        nc.vector.scalar_tensor_tensor(out=ex[:, r, :], in0=ex[:, r, :], scalar=rsum[:, r:r + 1],
                                                       in1=bank[r][:, 0:S], op0=ALU.mult, op1=ALU.mult
                                                       ).then_inc(dve_s.sem, dve_s.one("asmb", r))
                    dve.wait_ge(act_s.sem, act_s.at(g, "asmbT"))
                    lo(asmbT[1][:, :], bank[0][:, :], asmbT[0][:, :], "asmbT", 0)
                    for k in range(K):
                        dve.wait_ge(pe_s.sem, pe_s.at(g, "abT", k))
                        nc.vector.scalar_tensor_tensor(out=hsT32[:, k, :], in0=bank[1 + k][:, :],
                                                       scalar=col_b[:, BABP + k:BABP + k + 1], in1=whT32[:, k, :],
                                                       op0=ALU.add, op1=ALU.mult
                                                       ).then_inc(dve_s.sem, dve_s.one("hsT32", k))
                    for k in range(K):
                        dve.wait_ge(act_s.sem, act_s.at(g, "hsT", k))
                        lo(hsT[1][:, k, :], hsT32[:, k, :], hsT[0][:, k, :], "hsT", k)
                    for r in range(R):
                        dve.wait_ge(pe_s.sem, pe_s.at(g, "fe1", r))
                        nc.vector.bn_stats(st2[:, r, :], bank[4 + r][:, :]
                                           ).then_inc(dve_s.sem, dve_s.one("stats2", r))
                    dve.wait_ge(dve_s.sem, dve_s.at(g, "stats2", R - 1))
                    dve.sem_inc(s_pass[0], 1)
                    for r in range(R):
                        nc.vector.bn_aggr(mv2[:, r, :], st2[:, r, :]).then_inc(dve_s.sem, dve_s.one("mean2", r))
                    dve.wait_ge(dve_s.sem, dve_s.at(g, "mean2", R - 1))
                    nc.vector.tensor_scalar(ve2[:, :], mv2[:, :, 1], EPS, None, ALU.add
                                            ).then_inc(dve_s.sem, dve_s.one("var2"))
                    next_moments(g + 1)
                    dve.wait_ge(pool_s.sem, pool_s.at(g, "rstd2"))
                    for r in range(R):
                        nc.vector.tensor_scalar(fey[:, r, :], bank[4 + r][:, :], mv2[:, r, 0:1], rstd2[:, r:r + 1],
                                                ALU.subtract, ALU.mult).then_inc(dve_s.sem, dve_s.one("fey", r))
                    next_nb(g + 1)
                    for m in range(HK):
                        dve.wait_ge(act_s.sem, act_s.at(g, "hz", 2 * m + 1))
                        nc.vector.scalar_tensor_tensor(out=hp[:, m, :], in0=feT32[:, m, :], scalar=Dcol[:, :],
                                                       in1=hp[:, m, :], op0=ALU.add, op1=ALU.mult
                                                       ).then_inc(dve_s.sem, dve_s.one("mT32", m))
                    for m in range(HK):
                        dve.wait_ge(act_s.sem, act_s.at(g, "mT", m))
                        lo(mT[1][:, m, :], hp[:, m, :], mT[0][:, m, :], "mT", m)
                    for k in range(HK):
                        dve.wait_ge(act_s.sem, act_s.at(g, "feT", k))
                        lo(feT[1][:, k, :], feT32[:, k, :], feT[0][:, k, :], "feT", k)
                    dve.wait_ge(s_store, g * 32)
                    for j in range(2):
                        dve.wait_ge(pe_s.sem, pe_s.at(g, "out", 2 * j + 1))
                        for r in (2 * j, 2 * j + 1):
                            last = nc.vector.tensor_scalar(hsr[:, r * D:(r + 1) * D],
                                                           bank[j][:, (r % 2) * D:(r % 2 + 1) * D], c1[:, r:r + 1],
                                                           None, ALU.mult)
                        last.then_inc(dve_s.sem, dve_s.one("hs", j))
                    next_hT(g + 1)
                    for j in range(2):
                        dve.wait_ge(dve_s.sem, dve_s.at(g, "hs", j))
                        dve.wait_ge(pe_s.sem, pe_s.at(g, "fe2", 2 * j + 1))
                        nc.vector.tensor_tensor(wr[:, j * 2 * D:(j + 1) * 2 * D], bank[4 + j][:, :],
                                                hsr[:, j * 2 * D:(j + 1) * 2 * D], ALU.add
                                                ).then_inc(dve_s.sem, dve_s.one("w", j))

            @block.tensor
            def _(pe):
                def cols(t, k, r):
                    return t[0][:, k, r * P:(r + 1) * P], t[1][:, k, r * P:(r + 1) * P]

                def next_hT(g):
                    for k in range(K):
                        for r in range(R):
                            if k == 0:
                                pe.wait_ge(next_act.sem, next_act.at(g, "h", r))
                            last = nc.tensor.transpose(bank[2 + k][:, r * P:(r + 1) * P],
                                                       h[:, r * D + k * P:r * D + (k + 1) * P], ident[:, :])
                        last.then_inc(next_pe.sem, next_pe.one("hT", k))

                def fe1(g, r):
                    pe.wait_ge(act_s.sem, act_s.at(g, "wh", r))
                    pe.wait_ge(dve_s.sem, dve_s.at(g, "d", r))
                    products(pe, bank[4 + r][:, :], [(cols(whT, k, r), w("fe1", k)) for k in range(K)], "fe1"
                             ).then_inc(pe_s.sem, pe_s.one("fe1", r))

                next_hT(0)
                with pe.Fori(0, G) as g:
                    pe.wait_ge(next_dve.sem, next_dve.at(g, "hT", K - 1))
                    pe.wait_ge(dve_s.sem, dve_s.before(g, "hs", 1))
                    for m in range(K):
                        products(pe, bank[m][:, :],
                                 [(w("W0", k, m * P, (m + 1) * P), (hT[0][:, k, :], hT[1][:, k, :]))
                                  for k in range(K)]).then_inc(pe_s.sem, pe_s.one("whT", m))
                    source_rows(pe, 0, hT, bank[2]).then_inc(pe_s.sem, pe_s.one("srow"))
                    pe.wait_ge(dve_s.sem, dve_s.before(g, "w", 1))
                    for r in range(R):
                        products(pe, bank[4 + r][:, 0:D + 1],
                                 [(cols(hT, k, r), w("W0", k)) for k in range(K)]
                                 ).then_inc(pe_s.sem, pe_s.one("wh", r))
                    pe.wait_ge(dve_s.sem, dve_s.at(g, "whT", K - 1))
                    pe.wait_ge(act_s.sem, act_s.at(g, "srow"))
                    for r in range(R):
                        products(pe, bank[r][:, 0:2 * S + 1],
                                 [(cols(whT, k, r), w("bcdt", k)) for k in range(K)], "bcdt"
                                 ).then_inc(pe_s.sem, pe_s.one("bcdt", r))
                    for r in range(R):
                        fe1(g, r)
                    pe.wait_ge(dve_s.sem, dve_s.at(g, "asmb", R - 1))
                    for r in range(R):
                        last = nc.tensor.transpose(bank[0][:, r * P:(r + 1) * P], ex[:, r, :], ident[:, :])
                    last.then_inc(pe_s.sem, pe_s.one("asmbT"))
                    pe.wait_ge(dve_s.sem, dve_s.at(g, "asmbT"))
                    for m in range(K):
                        products(pe, bank[1 + m][:, :],
                                 [(w("abp", 0, m * P, (m + 1) * P), (asmbT[0][:, :], asmbT[1][:, :]))]
                                 ).then_inc(pe_s.sem, pe_s.one("abT", m))
                    pe.wait_ge(dve_s.sem, dve_s.at(g, "hsT", K - 1))
                    for m in range(HK):
                        if m >= 2:
                            pe.wait_ge(act_s.sem, act_s.at(g, "hz", 2 * (m - 2) + 1))
                        for j, b in ((0, (0, 1)[m % 2]), (1, (3, 2)[m % 2])):
                            c0 = j * H + m * P
                            products(pe, bank[b][:, :],
                                     [(w("hz", k, c0, c0 + P), (hsT[0][:, k, :], hsT[1][:, k, :]))
                                      for k in range(K)]).then_inc(pe_s.sem, pe_s.one("hz", 2 * m + j))
                    pe.wait_ge(dve_s.sem, dve_s.at(g, "fey", R - 1))
                    for k in range(HK):
                        for r in range(R):
                            last = nc.tensor.transpose(bank[4 + k][:, r * P:(r + 1) * P],
                                                       fey[:, r, k * P:(k + 1) * P], ident[:, :])
                        last.then_inc(pe_s.sem, pe_s.one("feT", k))
                    pe.wait_ge(dve_s.sem, dve_s.at(g, "mT", HK - 1))
                    for r in range(R):
                        products(pe, bank[r // 2][:, (r % 2) * D:(r % 2 + 1) * D],
                                 [(cols(mT, m, r), w("out", m)) for m in range(HK)], "out"
                                 ).then_inc(pe_s.sem, pe_s.one("out", r))
                    next_hT(g + 1)
                    pe.wait_ge(dve_s.sem, dve_s.at(g, "feT", HK - 1))
                    for r in range(R):
                        products(pe, bank[4 + r // 2][:, (r % 2) * D:(r % 2 + 1) * D],
                                 [(cols(feT, k, r), w("fe2", k)) for k in range(HK)], "fe2"
                                 ).then_inc(pe_s.sem, pe_s.one("fe2", r))
        for x_ in (pe_s, act_s, dve_s, pool_s):
            x_.close(G)
        for x_ in (next_pe, next_act, next_dve, next_pool):
            x_.close(G + 1)
        stored = [0]
        dense_mem.close()

        def v_row(V, part, t, n=D + 1):
            return V[:, ds(t * VW + part * (T * VW), n)]

        def moments(dve, g, srcs, st, mv, ve, names, ready_all=None):
            if ready_all is not None:
                dve.wait_ge(*ready_all)
                dve.sem_inc(s_pass[0], 1)
            for r, (src, ready) in enumerate(srcs):
                if ready is not None:
                    dve.wait_ge(*ready)
                nc.vector.bn_stats(st[:, r, :], src).then_inc(dve_s.sem, dve_s.one(names[0], r))
            dve.wait_ge(dve_s.sem, dve_s.at(g, names[0], R - 1))
            dve.sem_inc(s_pass[0], 1)
            for r in range(R):
                nc.vector.bn_aggr(mv[:, r, :], st[:, r, :]).then_inc(dve_s.sem, dve_s.one(names[1], r))
            dve.wait_ge(dve_s.sem, dve_s.at(g, names[1], R - 1))
            nc.vector.tensor_scalar(ve[:, :], mv[:, :, 1], EPS, None, ALU.add
                                    ).then_inc(dve_s.sem, dve_s.one(names[2]))

        def inverse_root(pool, g, rstd, ve, var, stage):
            pool.wait_ge(dve_s.sem, dve_s.at(g, var))
            nc.gpsimd.tensor_tensor(rstd[:, :], ve[:, :], nhalf[:, 0:R], ALU.pow
                                    ).then_inc(pool_s.sem, pool_s.one(stage))

        def shift(dve, g, nb, mv, rstd, stage, rstage):
            dve.wait_ge(pool_s.sem, pool_s.at(g, rstage))
            nc.vector.scalar_tensor_tensor(out=nb[:, :], in0=mv[:, :, 0], scalar=-1.0, in1=rstd[:, :],
                                           op0=ALU.mult, op1=ALU.mult).then_inc(dve_s.sem, dve_s.one(stage))

        def row(t, r, n=D):
            return t[:, r * n:(r + 1) * n]

        def cols(t, k, r):
            return t[0][:, k, r * P:(r + 1) * P], t[1][:, k, r * P:(r + 1) * P]

        def transposes(pe, dst, src, ready=None):
            for r in range(R):
                if ready is not None:
                    pe.wait_ge(*ready(r))
                last = nc.tensor.transpose(dst[:, r * P:(r + 1) * P], src(r), ident[:, :])
            return last

        def stats_tiles(mem, name):
            return (sb(mem, f"st_{name}", [P, R, 6], F32), sb(mem, f"mv_{name}", [P, R, 2], F32),
                    sb(mem, f"ve_{name}", [P, R], F32), sb(mem, f"rstd_{name}", [P, R], F32))


        loaded = [0]
        MS = 4
        Q = T // R

        def aggregate(V, side, slope=None, wh=None):
            weighted = slope is not None
            with ExitStack() as mem, nc.Block() as block:
                mask = sb(mem, "mask", [P, MS, R * GW], U8)
                ph = sb(mem, "ph", [P, 2 * R, GW], F16)
                ag = sb(mem, "ag", [P, R * D], F32)
                rden = sb(mem, "rden", [P, R], F32)
                if weighted:
                    p32 = sb(mem, "p32", [P, R, GW], F32)
                    pl = sb(mem, "pl", [P, 2 * R, GW], F16)
                    v32 = sb(mem, "v32", [P, R, D + 1], F32)
                    dtil = sb(mem, "dtil", [P, T], F32)
                    red = sb(mem, "red", [P, 1], F32)
                work = side(mem, ag)
                pe_q.plan(("pv", R))
                act_q.plan(("hi", R))
                dve_q.plan(("p32", R), ("lo", R))
                pre_s.plan(("red", 1), ("dmax", 1), ("dtil", 1), ("omega", 1), ("vprime", 1), ("scale", 1))
                act_v.plan(("gam", 1), ("v32", R), ("hi", R))
                dve_v.plan(("relu", 1), ("scaled", 1), ("lo", R))
                masks = 16 * loaded[0]

                def slot(q, r):
                    return (q % 2) * R + r

                def gam(j):
                    return s_row[:, j * GW:(j + 1) * GW]

                def mask_here(g, q):
                    return s_mask[q % MS], g * (16 * Q // MS) + (masks + 16 * (q // MS + 1))

                def one_columns():
                    for part, value in ((0, 1.0), (1, 0.0)):
                        view = work["V"][:, part * (T * VW):(part + 1) * (T * VW)]
                        nc.vector.memset(view.rearrange("p (t w) -> p t w", w=VW)[:, :, D:D + 1], value)

                def groups(eng, quad, part, make=None, between=None):
                    for q in range(Q):
                        if make is not None:
                            make(q)
                        quad(0, q)
                    if between is not None:
                        between()
                    with eng.Fori(1, G) as g:
                        for q in range(Q):
                            quad(g, q)
                            part(eng, g - 1, q)
                    for q in range(Q):
                        part(eng, G - 1, q)

                @block.sync
                def _(sp):
                    def quad(g, q):
                        eng, stage = (dve_q, "p32") if weighted else (act_q, "hi")
                        sp.wait_ge(eng.sem, eng.before(g * Q + q, stage, R - 1, MS))
                        sp.sem_inc(s_pass[3], 1)
                        sp.dma_start(mask[:, q % MS, :], mask_d[ds(g * P, P), q * (R * GW):(q + 1) * (R * GW)]
                                     ).then_inc(s_mask[q % MS], 16)

                    groups(sp, quad, work["sync"])

                @block.gpsimd
                def _(pool):
                    if weighted:
                        pool.wait_ge(pre_s.sem, pre_s.at(0, "red"))
                        nc.gpsimd.partition_all_reduce(dmax[:, 0:1], red[:, :], P, RMAX).then_inc(pre_s.sem, 1)
                    with pool.Fori(0, G) as g:
                        work["pool"](pool, g)
                    work["end"](pool)

                @block.scalar
                def _(act):
                    def quad(g, q):
                        if not weighted:
                            act.wait_ge(*mask_here(g, q))
                        for r in range(R):
                            if weighted:
                                act.wait_ge(dve_q.sem, dve_q.at(g * Q + q, "p32", r))
                            act.wait_ge(pe_q.sem, pe_q.before(g * Q + q, "pv", r, 2))
                            nc.scalar.copy(ph[:, slot(q, r), :], p32[:, r, :] if weighted else
                                           mask[:, q % MS, r * GW:(r + 1) * GW]
                                           ).then_inc(act_q.sem, act_q.one("hi", r))

                    def make(q):
                        act.wait_ge(dve_v.sem, dve_v.at(q, "relu"))
                        nc.scalar.activation(gam(q), gam(q), ACT.Exp, scale=slope - 1.0
                                             ).then_inc(act_v.sem, act_v.one("gam"))
                        for r in range(R):
                            act.wait_ge(dve_v.sem, dve_v.before(q, "lo", r))
                            t = q * R + r
                            nc.scalar.mul(v32[:, r, 0:D], wh[:, t * D:(t + 1) * D], vprime[:, t:t + 1])
                            nc.scalar.copy(v32[:, r, D:D + 1], vprime[:, t:t + 1]
                                           ).then_inc(act_v.sem, act_v.one("v32", r))
                        for r in range(R):
                            act.wait_ge(act_v.sem, act_v.at(q, "v32", r))
                            nc.scalar.copy(v_row(V, 0, q * R + r), v32[:, r, :]
                                           ).then_inc(act_v.sem, act_v.one("hi", r))

                    def part(act, g, q):
                        if q == 0:
                            work["sums_free"](act, g)
                            for r in range(R):
                                act.wait_ge(dve_s.sem, dve_s.at(g, "rden", r))
                                nc.scalar.mul(row(ag, r), bank[r][:, 0:D], rden[:, r:r + 1]
                                              ).then_inc(act_s.sem, act_s.one("ag", r))
                        work["act"](act, g, q)

                    if weighted:
                        act.wait_ge(pre_s.sem, pre_s.at(0, "dtil"))
                        nc.scalar.activation(omega[:, :], dtil[:, :], ACT.Exp, scale=1.0 - slope
                                             ).then_inc(pre_s.sem, 1)
                        act.wait_ge(pre_s.sem, pre_s.at(0, "omega"))
                        nc.scalar.activation(vprime[:, :], dtil[:, :], ACT.Exp, scale=slope).then_inc(pre_s.sem, 1)
                        act.wait_ge(pre_s.sem, pre_s.at(0, "vprime"))
                    groups(act, quad, part, make if weighted else None)

                @block.vector
                def _(dve):
                    def quad(g, q):
                        if not weighted:
                            return
                        n = g * Q + q
                        dve.wait_ge(*mask_here(g, q))
                        for r in range(R):
                            dve.wait_ge(dve_q.sem, dve_q.before(n, "lo", r))
                            nc.vector.scalar_tensor_tensor(
                                out=p32[:, r, :], in0=s_row[:, ds(g * GW, GW)],
                                scalar=omega[:, q * R + r:q * R + r + 1],
                                in1=mask[:, q % MS, r * GW:(r + 1) * GW], op0=ALU.max, op1=ALU.mult
                                ).then_inc(dve_q.sem, dve_q.one("p32", r))
                        for r in range(R):
                            dve.wait_ge(act_q.sem, act_q.at(n, "hi", r))
                            nc.vector.tensor_tensor(pl[:, slot(q, r), :], p32[:, r, :], ph[:, slot(q, r), :],
                                                    ALU.subtract).then_inc(dve_q.sem, dve_q.one("lo", r))
                        if isinstance(g, int):
                            for r in range(R):
                                dve.wait_ge(act_v.sem, act_v.at(q, "hi", r))
                                nc.vector.tensor_tensor(v_row(V, 1, q * R + r), v32[:, r, :],
                                                        v_row(V, 0, q * R + r), ALU.subtract
                                                        ).then_inc(dve_v.sem, dve_v.one("lo", r))

                    def make(q):
                        nc.vector.tensor_scalar(gam(q), gam(q), dmax[:, 0:1], 0.0, ALU.add, ALU.max
                                                ).then_inc(dve_v.sem, dve_v.one("relu"))
                        dve.wait_ge(act_v.sem, act_v.at(q, "gam"))
                        nc.vector.tensor_scalar(gam(q), gam(q), PSCALE, None, ALU.mult
                                                ).then_inc(dve_v.sem, dve_v.one("scaled"))
                        dve.wait_ge(dve_v.sem, dve_v.at(q, "scaled"))

                    def part(dve, g, q):
                        if q == 0:
                            dve.wait_ge(pe_q.sem, pe_q.at(g * Q + (Q - 1), "pv", R - 1))
                            dve.wait_ge(act_s.sem, act_s.before(g, "ag", R - 1))
                            for r in range(R):
                                nc.vector.reciprocal(rden[:, r:r + 1], bank[r][:, D:D + 1]
                                                     ).then_inc(dve_s.sem, dve_s.one("rden", r))
                        work["dve"](dve, g, q)

                    if weighted:
                        nc.vector.tensor_reduce(red[:, :], d_col[:, :], AX_X, ALU.max).then_inc(pre_s.sem, 1)
                        dve.wait_ge(pre_s.sem, pre_s.at(0, "dmax"))
                        nc.vector.tensor_scalar(dtil[:, :], d_col[:, :], dmax[:, 0:1], None, ALU.subtract
                                                ).then_inc(pre_s.sem, 1)
                        dve.wait_ge(pre_s.sem, pre_s.at(0, "vprime"))
                        nc.vector.tensor_scalar(omega[:, :], omega[:, :], PSCALE, None, ALU.mult
                                                ).then_inc(pre_s.sem, 1)
                        dve.wait_ge(pre_s.sem, pre_s.at(0, "scale"))
                    groups(dve, quad, part, make if weighted else None, one_columns if weighted else None)

                @block.tensor
                def _(pe):
                    def quad(g, q):
                        n = g * Q + q
                        for r in range(R):
                            if weighted:
                                pe.wait_ge(dve_q.sem, dve_q.at(n, "lo", r))
                                if isinstance(g, int):
                                    pe.wait_ge(dve_v.sem, dve_v.at(q, "lo", r))
                            else:
                                pe.wait_ge(act_q.sem, act_q.at(n, "hi", r))
                            first, final = q == 0 and r == 0, q == Q - 1 and r == R - 1
                            t = q * R + r
                            for i in range(R):
                                if first:
                                    pe.wait_ge(act_s.sem, act_s.before(g, "ag", i))
                                acc = bank[i][:, 0:D + 1]
                                c = slice(i * P, (i + 1) * P)
                                p_hi = ph[:, slot(q, r), c]
                                nc.tensor.matmul(acc, p_hi, v_row(V, 0, t), start=first, stop=False)
                                last = nc.tensor.matmul(acc, p_hi, v_row(V, 1, t), start=False,
                                                        stop=final and not weighted)
                                if weighted:
                                    last = nc.tensor.matmul(acc, pl[:, slot(q, r), c], v_row(V, 0, t),
                                                            start=False, stop=final)
                            last.then_inc(pe_q.sem, pe_q.one("pv", r))

                    groups(pe, quad, work["pe"])
            loaded[0] += G * Q // MS
            for x_ in (pe_s, act_s, dve_s, pool_s):
                x_.close(G)
            for x_ in (pe_q, act_q) + ((dve_q,) if weighted else ()):
                x_.close(G * Q)
            if weighted:
                pre_s.base += 6
                act_v.close(Q)
                dve_v.close(Q)

        def lo(dst, src, hi_part, stage, i):
            return nc.vector.tensor_tensor(dst, src, hi_part, ALU.subtract).then_inc(dve_s.sem, dve_s.one(stage, i))

        def hi(dst, src, stage, i):
            return nc.scalar.copy(dst, src).then_inc(act_s.sem, act_s.one(stage, i))

        def normal(act, g, h, x, nb, rs, stage="h"):
            act.wait_ge(dve_s.sem, dve_s.at(g, "nb"))
            for r in range(R):
                nc.scalar.activation(row(h, r), row(x, r), ACT.Relu, bias=nb[:, r:r + 1], scale=rs[:, r:r + 1]
                                     ).then_inc(act_s.sem, act_s.one(stage, r))

        def finish_layer0(mem, ag):
            hsg = sb(mem, "hsg", [P, R * D], F32)
            wg = sb(mem, "wg", [P, R * D], F32)
            xg = sb(mem, "xg2", [P, R * D], F32)
            xo = sb(mem, "xo", [P, R * D], F32)
            cT = [sb(mem, f"cT_{p}", [P, 2 * K, GW], F16) for p in ("hi", "lo")]
            gy = sb(mem, "gy", [P, HK, GW], F32)
            sT = [sb(mem, f"sT_{p}", [P, HK, GW], F16) for p in ("hi", "lo")]
            th = sb(mem, "th", [P, R * D], F32)
            dl = sb(mem, "dl", [P, R * D], F32)
            f = sb(mem, "f", [P, R * D], F32)
            h = th
            stg, mvg, veg, rsg = stats_tiles(mem, "g")
            stf, mvf, vef, rsf = stats_tiles(mem, "f")
            stx, mvx, vex, rsx = stats_tiles(mem, "x")
            nbg = sb(mem, "nbg", [P, R], F32)
            nbf = sb(mem, "nbf", [P, R], F32)
            nb = sb(mem, "nb2", [P, R], F32)
            pe_s.plan(("cT", 2 * K), ("g1", R), ("gT", HK), ("g2", R))
            act_s.plan(("ag", R), ("cT", 2 * K), ("gy", R), ("silu", HK), ("sT", HK), ("tanh", 2), ("fn", R),
                       ("h", R), ("V", R))
            dve_s.plan(("rden", R), ("cT", 2 * K), ("gs", R), ("gm", R), ("gv", 1), ("nbg", 1), ("sT", HK),
                       ("u", 1), ("f", 1), ("fs", R), ("fm", R), ("fv", 1), ("nbf", 1),
                       ("xs", R), ("xm", R), ("xv", 1), ("nb", 1), ("V", R))
            pool_s.plan(("dl", 1), ("g", 1), ("f", 1), ("fg", R), ("fb", R), ("x", 1), ("rx", 1))
            first_in, stores = 16 * (G + 2), stored[0]
            stored[0] += 16 * G
            V = value(VB)

            def sync(sp, g, q):
                if q == 3:
                    sp.wait_ge(pool_s.sem, pool_s.before(g, "x"))
                    sp.wait_ge(pe_s.sem, pe_s.before(g, "cT", 2 * K - 1))
                    sp.wait_ge(dve_s.sem, dve_s.before(g, "f"))
                    sp.sem_inc(s_pass[3], 1)
                    for dst, src in ((hsg, hs_d), (wg, w_d), (xg, a["x"])):
                        sp.dma_start(dst[:, :], src[ds(g * P, P), :]).then_inc(s_xin, 16)

            def end(pool):
                pool.wait_ge(s_xout, stores + 16 * G)

            def sums_free(act, g):
                act.wait_ge(pool_s.sem, pool_s.before(g, "dl"))

            def pool_part(pool, g):
                pool.wait_ge(s_xin, g * 48 + (first_in + 48))
                pool.wait_ge(act_s.sem, act_s.at(g, "ag", R - 1))
                pool.wait_ge(dve_s.sem, dve_s.before(g, "u"))
                pool.sem_inc(s_pass[1], 1)
                nc.gpsimd.tensor_tensor(dl[:, :], ag[:, :], hsg[:, :], ALU.subtract
                                        ).then_inc(pool_s.sem, pool_s.one("dl"))
                inverse_root(pool, g, rsg, veg, "gv", "g")
                inverse_root(pool, g, rsf, vef, "fv", "f")
                for stage, other, op in (("fg", lng, ALU.mult), ("fb", lnb, ALU.add)):
                    for r in range(R):
                        if stage == "fg":
                            pool.wait_ge(act_s.sem, act_s.at(g, "fn", r))
                        else:
                            pool.wait_ge(pool_s.sem, pool_s.at(g, "fg", r))
                        nc.gpsimd.tensor_tensor(row(f, r), row(f, r), other[:, :], op
                                                ).then_inc(pool_s.sem, pool_s.one(stage, r))
                pool.wait_ge(pool_s.sem, pool_s.at(g, "fb", R - 1))
                pool.wait_ge(s_xout, g * 16 + stores)
                pool.wait_ge(act_s.sem, act_s.before(g, "h", R - 1))
                pool.sem_inc(s_pass[1], 1)
                nc.gpsimd.tensor_tensor(xo[:, :], f[:, :], xg[:, :], ALU.add
                                        ).then_inc(pool_s.sem, pool_s.one("x"))
                pool.wait_ge(pool_s.sem, pool_s.at(g, "x"))
                pool.sem_inc(s_pass[1], 1)
                nc.gpsimd.dma_start(x1_d[ds(g * P, P), :], xo[:, :]).then_inc(s_xout, 16)
                inverse_root(pool, g, rsx, vex, "xv", "rx")

            def act_part(act, g, q):
                if q == 1:
                    for k in range(2 * K):
                        act.wait_ge(pe_s.sem, pe_s.at(g, "cT", k))
                        hi(cT[0][:, k, :], bank[4 + k][:, :], "cT", k)
                if q == 3:
                    act.wait_ge(dve_s.sem, dve_s.at(g, "nbg"))
                    for r in range(R):
                        nc.scalar.activation(gy[:, r, :], bank[4 + r][:, :], ACT.Identity, bias=nbg[:, r:r + 1],
                                             scale=rsg[:, r:r + 1]).then_inc(act_s.sem, act_s.one("gy", r))
                if q == 4:
                    act.wait_ge(pe_s.sem, pe_s.at(g, "gT", HK - 1))
                    for k in range(HK):
                        nc.scalar.activation(gy[:, k, :], bank[4 + k][:, :], ACT.Silu,
                                             bias=col_b[:, GB + k:GB + k + 1], scale=col_b[:, GG + k:GG + k + 1]
                                             ).then_inc(act_s.sem, act_s.one("silu", k))
                    for k in range(HK):
                        act.wait_ge(act_s.sem, act_s.at(g, "silu", k))
                        hi(sT[0][:, k, :], gy[:, k, :], "sT", k)
                if q == 5:
                    act.wait_ge(dve_s.sem, dve_s.before(g, "V", R - 1))
                    for j in range(2):
                        act.wait_ge(pe_s.sem, pe_s.at(g, "g2", 2 * j + 1))
                        nc.scalar.activation(row(th, j, 2 * D), bank[4 + j][:, :], ACT.Tanh, scale=0.5
                                             ).then_inc(act_s.sem, act_s.one("tanh", j))
                if q == 6:
                    act.wait_ge(dve_s.sem, dve_s.at(g, "nbf"))
                    for r in range(R):
                        nc.scalar.activation(row(f, r), row(f, r), ACT.Identity, bias=nbf[:, r:r + 1],
                                             scale=rsf[:, r:r + 1]).then_inc(act_s.sem, act_s.one("fn", r))
                if q == 7:
                    normal(act, g, h, xo, nb, rsx)
                    for r in range(R):
                        act.wait_ge(act_s.sem, act_s.at(g, "h", r))
                        hi(v_row(V, 0, g * R + r, D), row(h, r), "V", r)

            def dve_part(dve, g, q):
                if q == 1:
                    for k in range(2 * K):
                        dve.wait_ge(act_s.sem, act_s.at(g, "cT", k))
                        lo(cT[1][:, k, :], bank[4 + k][:, :], cT[0][:, k, :], "cT", k)
                if q == 3:
                    moments(dve, g, [(bank[4 + r][:, :], (pe_s.sem, pe_s.at(g, "g1", r))) for r in range(R)],
                            stg, mvg, veg, ("gs", "gm", "gv"))
                    shift(dve, g, nbg, mvg, rsg, "nbg", "g")
                if q == 4:
                    for k in range(HK):
                        dve.wait_ge(act_s.sem, act_s.at(g, "sT", k))
                        lo(sT[1][:, k, :], gy[:, k, :], sT[0][:, k, :], "sT", k)
                if q == 5:
                    dve.wait_ge(act_s.sem, act_s.at(g, "tanh", 1))
                    dve.wait_ge(pool_s.sem, pool_s.at(g, "dl"))
                    nc.vector.scalar_tensor_tensor(out=th[:, :], in0=th[:, :], scalar=1.0, in1=dl[:, :],
                                                   op0=ALU.add, op1=ALU.mult
                                                   ).then_inc(dve_s.sem, dve_s.one("u"))
                    dve.wait_ge(dve_s.sem, dve_s.at(g, "u"))
                    dve.wait_ge(s_xin, g * 48 + (first_in + 48))
                    nc.vector.scalar_tensor_tensor(out=f[:, :], in0=th[:, :], scalar=0.5, in1=wg[:, :],
                                                   op0=ALU.mult, op1=ALU.add
                                                   ).then_inc(dve_s.sem, dve_s.one("f"))
                    moments(dve, g, [(row(f, r), None) for r in range(R)], stf, mvf, vef, ("fs", "fm", "fv"),
                            (dve_s.sem, dve_s.at(g, "f")))
                    shift(dve, g, nbf, mvf, rsf, "nbf", "f")
                if q == 7:
                    moments(dve, g, [(row(xo, r), None) for r in range(R)], stx, mvx, vex, ("xs", "xm", "xv"),
                            (pool_s.sem, pool_s.at(g, "x")))
                    shift(dve, g, nb, mvx, rsx, "nb", "rx")
                    for r in range(R):
                        dve.wait_ge(act_s.sem, act_s.at(g, "V", r))
                        lo(v_row(V, 1, g * R + r, D), row(h, r), v_row(V, 0, g * R + r, D), "V", r)

            def pe_part(pe, g, q):
                if q == 0:
                    pe.wait_ge(s_xin, g * 48 + (first_in + 48))
                    for j, src in enumerate((hsg, ag)):
                        for k in range(K):
                            transposes(pe, bank[4 + j * K + k], lambda r: src[:, r * D + k * P:r * D + (k + 1) * P],
                                       (lambda r: (act_s.sem, act_s.at(g, "ag", r))) if j and not k else None
                                       ).then_inc(pe_s.sem, pe_s.one("cT", j * K + k))
                if q == 1:
                    pe.wait_ge(dve_s.sem, dve_s.at(g, "cT", 2 * K - 1))
                    for r in range(R):
                        products(pe, bank[4 + r][:, :],
                                 [(cols(cT, (k + K) % (2 * K), r), w("g1", k)) for k in range(2 * K)], "g1"
                                 ).then_inc(pe_s.sem, pe_s.one("g1", r))
                if q == 2:
                    pe.wait_ge(act_s.sem, act_s.at(g, "gy", R - 1))
                    for k in range(HK):
                        transposes(pe, bank[4 + k], lambda r: gy[:, r, k * P:(k + 1) * P]
                                   ).then_inc(pe_s.sem, pe_s.one("gT", k))
                if q == 3:
                    pe.wait_ge(dve_s.sem, dve_s.at(g, "sT", HK - 1))
                    for r in range(R):
                        products(pe, bank[4 + r // 2][:, (r % 2) * D:(r % 2 + 1) * D],
                                 [(cols(sT, k, r), w("g2", k)) for k in range(HK)], "g2"
                                 ).then_inc(pe_s.sem, pe_s.one("g2", r))

            return {"sync": sync, "pool": pool_part, "act": act_part, "dve": dve_part, "pe": pe_part, "end": end,
                    "sums_free": sums_free, "V": V}

        def finish_layer1(mem, ag):
            xg = sb(mem, "xg3", [P, R * D], F32)
            xo = sb(mem, "xo1", [P, R * D], F32)
            aT = [sb(mem, f"aT_{p}", [P, K, GW], F16) for p in ("hi", "lo")]
            h = sb(mem, "h1", [P, R * D], F32)
            hT = [sb(mem, f"h1T_{p}", [P, K, GW], F16) for p in ("hi", "lo")]
            stx, mvx, vex, rsx = stats_tiles(mem, "x1")
            nb = sb(mem, "nb3", [P, R], F32)
            pe_s.plan(("aT", K), ("lin", R), ("hT", K), ("srow", 1), ("wh", R))
            act_s.plan(("ag", R), ("aT", K), ("h", R), ("hT", K), ("srow", 1), ("wh", R))
            dve_s.plan(("rden", R), ("aT", K), ("x", 2), ("xs", R), ("xm", R), ("xv", 1), ("nb", 1), ("hT", K),
                       ("d", R))
            pool_s.plan(("rx", 1))
            first_in, stores = 16 * (G + 2) + 48 * G, stored[0]
            stored[0] += 16 * G
            wh = rows_of(VA)

            def sync(sp, g, q):
                if q == 3:
                    sp.wait_ge(dve_s.sem, dve_s.before(g, "x", 1))
                    sp.sem_inc(s_pass[3], 1)
                    sp.dma_start(xg[:, :], x1_d[ds(g * P, P), :]).then_inc(s_xin, 16)

            def end(pool):
                pool.wait_ge(s_xout, stores + 16 * G)

            def sums_free(act, g):
                act.wait_ge(pe_s.sem, pe_s.before(g, "aT", K - 1))

            def pool_part(pool, g):
                inverse_root(pool, g, rsx, vex, "xv", "rx")
                pool.wait_ge(dve_s.sem, dve_s.at(g, "x", 1))
                pool.sem_inc(s_pass[1], 1)
                nc.gpsimd.dma_start(x2_d[ds(g * P, P), :], xo[:, :]).then_inc(s_xout, 16)

            def act_part(act, g, q):
                if q == 1:
                    for k in range(K):
                        act.wait_ge(pe_s.sem, pe_s.at(g, "aT", k))
                        hi(aT[0][:, k, :], bank[4 + k][:, :], "aT", k)
                if q == 4:
                    normal(act, g, h, xo, nb, rsx)
                if q == 5:
                    for k in range(K):
                        act.wait_ge(pe_s.sem, pe_s.at(g, "hT", k))
                        hi(hT[0][:, k, :], bank[4 + k][:, :], "hT", k)
                if q == 7:
                    act.wait_ge(pe_s.sem, pe_s.at(g, "srow"))
                    nc.scalar.copy(s_row[:, ds(g * GW, GW)], bank[4][:, :]
                                   ).then_inc(act_s.sem, act_s.one("srow"))
                    for r in range(R):
                        act.wait_ge(pe_s.sem, pe_s.at(g, "wh", r))
                        nc.scalar.copy(wh[:, ds(g * (R * D) + r * D, D)], bank[(5, 6, 7, 4)[r]][:, 0:D]
                                       ).then_inc(act_s.sem, act_s.one("wh", r))

            def dve_part(dve, g, q):
                if q == 1:
                    for k in range(K):
                        dve.wait_ge(act_s.sem, act_s.at(g, "aT", k))
                        lo(aT[1][:, k, :], bank[4 + k][:, :], aT[0][:, k, :], "aT", k)
                if q == 3:
                    dve.wait_ge(s_xin, g * 16 + (first_in + 16))
                    dve.wait_ge(s_xout, g * 16 + stores)
                    dve.sem_inc(s_pass[0], 1)
                    for j in range(2):
                        dve.wait_ge(pe_s.sem, pe_s.at(g, "lin", 2 * j + 1))
                        nc.vector.tensor_tensor(row(xo, j, 2 * D), bank[6 + j][:, :], row(xg, j, 2 * D), ALU.add
                                                ).then_inc(dve_s.sem, dve_s.one("x", j))
                    moments(dve, g, [(row(xo, r), None) for r in range(R)], stx, mvx, vex, ("xs", "xm", "xv"),
                            (dve_s.sem, dve_s.at(g, "x", 1)))
                    shift(dve, g, nb, mvx, rsx, "nb", "rx")
                if q == 5:
                    for k in range(K):
                        dve.wait_ge(act_s.sem, act_s.at(g, "hT", k))
                        lo(hT[1][:, k, :], bank[4 + k][:, :], hT[0][:, k, :], "hT", k)
                if q == 7:
                    for r in range(R):
                        dve.wait_ge(act_s.sem, act_s.at(g, "wh", r))
                        nc.vector.tensor_copy(d_col[:, ds(g * R + r, 1)], bank[(5, 6, 7, 4)[r]][:, D:D + 1]
                                              ).then_inc(dve_s.sem, dve_s.one("d", r))

            def pe_part(pe, g, q):
                if q == 0:
                    pe.wait_ge(dve_s.sem, dve_s.before(g, "d", R - 1))
                    for k in range(K):
                        transposes(pe, bank[4 + k], lambda r: ag[:, r * D + k * P:r * D + (k + 1) * P],
                                   lambda r: (act_s.sem, act_s.at(g, "ag", r))
                                   ).then_inc(pe_s.sem, pe_s.one("aT", k))
                if q == 2:
                    pe.wait_ge(dve_s.sem, dve_s.at(g, "aT", K - 1))
                    for r in range(R):
                        products(pe, bank[6 + r // 2][:, (r % 2) * D:(r % 2 + 1) * D],
                                 [(cols(aT, k, r), w("W1", k)) for k in range(K)], "W1"
                                 ).then_inc(pe_s.sem, pe_s.one("lin", r))
                if q == 4:
                    for k in range(K):
                        transposes(pe, bank[4 + k], lambda r: h[:, r * D + k * P:r * D + (k + 1) * P],
                                   lambda r: (act_s.sem, act_s.at(g, "h", r))
                                   ).then_inc(pe_s.sem, pe_s.one("hT", k))
                if q == 6:
                    pe.wait_ge(dve_s.sem, dve_s.at(g, "hT", K - 1))
                    source_rows(pe, 1, hT, bank[4]).then_inc(pe_s.sem, pe_s.one("srow"))
                    for r in range(R):
                        if r == R - 1:
                            pe.wait_ge(act_s.sem, act_s.at(g, "srow"))
                        products(pe, bank[(5, 6, 7, 4)[r]][:, 0:D + 1],
                                 [(cols(hT, k, r), w("W2", k)) for k in range(K)]
                                 ).then_inc(pe_s.sem, pe_s.one("wh", r))

            return {"sync": sync, "pool": pool_part, "act": act_part, "dve": dve_part, "pe": pe_part, "end": end,
                    "sums_free": sums_free}

        def finish_layer2(mem, ag):
            xg = sb(mem, "xg4", [P, R * D], F32)
            xo = sb(mem, "xo2", [P, R * D], F32)
            e = w_gate[0][:, 0:2 * R * D].bitcast(F32)
            h = w_gate[1][:, 0:2 * R * D].bitcast(F32)
            hT = [sb(mem, f"h2T_{p}", [P, K, GW], F16) for p in ("hi", "lo")]
            qT = sb(mem, "qTg", [P, 2, K, GW], F16)
            stx, mvx, vex, rsx = stats_tiles(mem, "x2")
            nb = sb(mem, "nb4", [P, R], F32)
            pe_s.plan(("hT", K), ("qT", K), ("kT", K), ("v", R))
            act_s.plan(("ag", R), ("e", 1), ("h", R), ("hT", K), ("qT", K), ("kT", K), ("v", R))
            dve_s.plan(("rden", R), ("mn", 1), ("pos", 1), ("x", 1), ("xs", R), ("xm", R), ("xv", 1), ("nb", 1),
                       ("hT", K), ("qT", K), ("kT", K), ("v", R))
            pool_s.plan(("rx", 1))
            first_in, stores = 16 * (G + 2) + 64 * G, stored[0]
            stored[0] += 32 * G
            V = value(VA)

            def sync(sp, g, q):
                if q == 3:
                    sp.wait_ge(dve_s.sem, dve_s.before(g, "pos"))
                    sp.sem_inc(s_pass[3], 1)
                    sp.dma_start(xg[:, :], x2_d[ds(g * P, P), :]).then_inc(s_xin, 16)

            def end(pool):
                pool.wait_ge(s_xout, stores + 32 * G)

            def sums_free(act, g):
                act.wait_ge(dve_s.sem, dve_s.before(g, "pos"))

            def pool_part(pool, g):
                inverse_root(pool, g, rsx, vex, "xv", "rx")
                pool.wait_ge(dve_s.sem, dve_s.at(g, "x"))
                pool.sem_inc(s_pass[1], 1)
                nc.gpsimd.dma_start(x3_d[ds(g * P, P), :], xo[:, :]).then_inc(s_xout, 16)
                pool.wait_ge(dve_s.sem, dve_s.at(g, "qT", K - 1))
                pool.sem_inc(s_pass[1], 1)
                nc.gpsimd.dma_start(qT_d[ds(g * P, P), :], qT[:, :, :, :].rearrange("p a k n -> p (a k n)")
                                    ).then_inc(s_xout, 16)

            def act_part(act, g, q):
                if q == 1:
                    act.wait_ge(dve_s.sem, dve_s.at(g, "mn"))
                    nc.scalar.activation(e[:, :], e[:, :], ACT.Exp).then_inc(act_s.sem, act_s.one("e"))
                if q == 2:
                    normal(act, g, h, xo, nb, rsx)
                if q == 3:
                    for k in range(K):
                        act.wait_ge(pe_s.sem, pe_s.at(g, "hT", k))
                        hi(hT[0][:, k, :], bank[4 + k][:, :], "hT", k)
                if q == 5:
                    act.wait_ge(s_xout, g * 32 + stores)
                    for k in range(K):
                        act.wait_ge(pe_s.sem, pe_s.at(g, "qT", k))
                        hi(qT[:, 0, k, :], bank[4 + k][:, :], "qT", k)
                    for k in range(K):
                        act.wait_ge(pe_s.sem, pe_s.at(g, "kT", k))
                        hi(kT[0][:, k, ds(g * GW, GW)], bank[6 + k][:, :], "kT", k)
                if q == 7:
                    for r in range(R):
                        act.wait_ge(pe_s.sem, pe_s.at(g, "v", r))
                        hi(v_row(V, 0, g * R + r, D), bank[4 + r][:, 0:D], "v", r)

            def dve_part(dve, g, q):
                if q == 1:
                    dve.wait_ge(act_s.sem, act_s.at(g, "ag", R - 1))
                    nc.vector.tensor_scalar(e[:, :], ag[:, :], 0.0, None, ALU.min
                                            ).then_inc(dve_s.sem, dve_s.one("mn"))
                    dve.wait_ge(s_xin, g * 16 + (first_in + 16))
                    dve.wait_ge(s_xout, g * 32 + stores)
                    nc.vector.scalar_tensor_tensor(out=xo[:, :], in0=ag[:, :], scalar=0.0, in1=xg[:, :],
                                                   op0=ALU.max, op1=ALU.add
                                                   ).then_inc(dve_s.sem, dve_s.one("pos"))
                    dve.wait_ge(act_s.sem, act_s.at(g, "e"))
                    dve.wait_ge(dve_s.sem, dve_s.at(g, "pos"))
                    nc.vector.scalar_tensor_tensor(out=xo[:, :], in0=e[:, :], scalar=-1.0, in1=xo[:, :],
                                                   op0=ALU.add, op1=ALU.add).then_inc(dve_s.sem, dve_s.one("x"))
                    moments(dve, g, [(row(xo, r), None) for r in range(R)], stx, mvx, vex, ("xs", "xm", "xv"),
                            (dve_s.sem, dve_s.at(g, "x")))
                    shift(dve, g, nb, mvx, rsx, "nb", "rx")
                if q == 3:
                    for k in range(K):
                        dve.wait_ge(act_s.sem, act_s.at(g, "hT", k))
                        lo(hT[1][:, k, :], bank[4 + k][:, :], hT[0][:, k, :], "hT", k)
                if q == 5:
                    for k in range(K):
                        dve.wait_ge(act_s.sem, act_s.at(g, "qT", k))
                        lo(qT[:, 1, k, :], bank[4 + k][:, :], qT[:, 0, k, :], "qT", k)
                    for k in range(K):
                        dve.wait_ge(act_s.sem, act_s.at(g, "kT", k))
                        c = ds(g * GW, GW)
                        lo(kT[1][:, k, c], bank[6 + k][:, :], kT[0][:, k, c], "kT", k)
                if q == 7:
                    for r in range(R):
                        dve.wait_ge(act_s.sem, act_s.at(g, "v", r))
                        lo(v_row(V, 1, g * R + r, D), bank[4 + r][:, 0:D], v_row(V, 0, g * R + r, D), "v", r)

            def pe_part(pe, g, q):
                if q == 2:
                    pe.wait_ge(dve_s.sem, dve_s.before(g, "v", R - 1))
                    for k in range(K):
                        transposes(pe, bank[4 + k], lambda r: h[:, r * D + k * P:r * D + (k + 1) * P],
                                   lambda r: (act_s.sem, act_s.at(g, "h", r))
                                   ).then_inc(pe_s.sem, pe_s.one("hT", k))
                if q == 4:
                    pe.wait_ge(dve_s.sem, dve_s.at(g, "hT", K - 1))
                    for name, b in (("q", 4), ("k", 6)):
                        for m in range(K):
                            products(pe, bank[b + m][:, :],
                                     [(w("W" + name, k, m * P, (m + 1) * P), (hT[0][:, k, :], hT[1][:, k, :]))
                                      for k in range(K)]).then_inc(pe_s.sem, pe_s.one(name + "T", m))
                if q == 6:
                    pe.wait_ge(dve_s.sem, dve_s.at(g, "kT", K - 1))
                    for r in range(R):
                        products(pe, bank[4 + r][:, 0:D], [(cols(hT, k, r), w("Wv", k)) for k in range(K)]
                                 ).then_inc(pe_s.sem, pe_s.one("v", r))

            return {"sync": sync, "pool": pool_part, "act": act_part, "dve": dve_part, "pe": pe_part, "end": end,
                    "sums_free": sums_free, "V": V}

        whole = [0]

        def row_maxima():
            with ExitStack() as mem, nc.Block() as block:
                mask = sb(mem, "mask", [P, 2, T * GW], U8)
                q_hi = spare[:, 0:2 * K * GW].rearrange("p (h k n) -> p h k n", h=2, k=K)
                m16 = sb(mem, "m16", [P, R, GW], F16)
                top_of = sb(mem, "top_of", [P, R, GW], F32)
                onto = sb(mem, "onto", [P, R, P], F32)
                Q = T // R
                pe_q.plan(("s", R))
                act_q.plan(("m16", R))
                dve_q.plan(("max", R))
                pe_s.plan(("turn", 1), ("spread", 1))
                dve_s.plan(("clear", R), ("own", R), ("loop", R), ("diag", R), ("join", 3), ("col", 1),
                           ("m", 1), ("onto", R), ("row", 1))
                masks = 16 * whole[0]

                @block.sync
                def _(sp):
                    with sp.Fori(0, G // 2) as b:
                        for half in range(2):
                            sp.wait_ge(dve_s.sem, dve_s.before(b * 2 + half, "row", 0, 2))
                            at = ds(b * (2 * P) + half * P, P)
                            sp.dma_start(mask[:, half, :], mask_d[at, :]).then_inc(s_whole[half], 16)
                            sp.dma_start(q_hi[:, half, :, :].rearrange("p k n -> p (k n)"), qT_d[at, 0:K * GW]
                                         ).then_inc(s_qin[half], 16)

                @block.scalar
                def _(act):
                    with act.Fori(0, G // 2) as b:
                        for half in range(2):
                            g = b * 2 + half
                            act.wait_ge(dve_s.sem, dve_s.at(g, "diag", R - 1))
                            with act.Fori(0, Q) as q:
                                n = g * Q + q
                                for r in range(R):
                                    act.wait_ge(pe_q.sem, pe_q.before(n, "s", r))
                                    nc.scalar.copy(m16[:, r, :], mask[:, half, ds(q * (R * GW) + r * GW, GW)]
                                                   ).then_inc(act_q.sem, act_q.one("m16", r))

                @block.vector
                def _(dve):
                    with dve.Fori(0, G // 2) as b:
                        for half in range(2):
                            g = b * 2 + half

                            def own(r):
                                return mask[:, half, ds(g * (R * GW) + (r * GW + r * P), P)]

                            for r in range(R):
                                nc.vector.memset(top_of[:, r, :], -3.0e38
                                                 ).then_inc(dve_s.sem, dve_s.one("clear", r))
                            dve.wait_ge(s_whole[half], b * 16 + (masks + 16))
                            for r in range(R):
                                nc.vector.tensor_tensor(onto[:, r, :], own(r), ident8[:, :], ALU.mult
                                                        ).then_inc(dve_s.sem, dve_s.one("own", r))
                            for r in range(R):
                                dve.wait_ge(dve_s.sem, dve_s.at(g, "own", r))
                                nc.vector.tensor_reduce(loop_col[:, ds(g * R + r, 1)], onto[:, r, :], AX_X, ALU.max
                                                        ).then_inc(dve_s.sem, dve_s.one("loop", r))
                            for r in range(R):
                                nc.vector.tensor_tensor(own(r), own(r), ident8[:, :], ALU.max
                                                        ).then_inc(dve_s.sem, dve_s.one("diag", r))
                            dve.wait_ge(dve_s.sem, dve_s.at(g, "diag", R - 1))
                            dve.sem_inc(s_pass[0], 1)
                            with dve.Fori(0, Q) as q:
                                n = g * Q + q
                                for r in range(R):
                                    dve.wait_ge(pe_q.sem, pe_q.at(n, "s", r))
                                    dve.wait_ge(dve_q.sem, dve_q.before(n, "max", r))
                                    nc.vector.tensor_tensor(top_of[:, r, :], bank[r][:, :], top_of[:, r, :], ALU.max
                                                            ).then_inc(dve_q.sem, dve_q.one("max", r))
                            dve.wait_ge(dve_q.sem, dve_q.at(g * Q + (Q - 1), "max", R - 1))
                            nc.vector.tensor_tensor(top_of[:, 0, :], top_of[:, 0, :], top_of[:, 1, :], ALU.max
                                                    ).then_inc(dve_s.sem, dve_s.one("join", 0))
                            nc.vector.tensor_tensor(top_of[:, 2, :], top_of[:, 2, :], top_of[:, 3, :], ALU.max
                                                    ).then_inc(dve_s.sem, dve_s.one("join", 1))
                            dve.wait_ge(dve_s.sem, dve_s.at(g, "join", 1))
                            nc.vector.tensor_tensor(top_of[:, 0, :], top_of[:, 0, :], top_of[:, 2, :], ALU.max
                                                    ).then_inc(dve_s.sem, dve_s.one("join", 2))
                            dve.wait_ge(pe_s.sem, pe_s.at(g, "turn"))
                            nc.vector.tensor_reduce(m_col[:, ds(g * R, R)],
                                                    bank[4][:, :].rearrange("p (r n) -> p r n", r=R), AX_X, ALU.max
                                                    ).then_inc(dve_s.sem, dve_s.one("col"))
                            dve.wait_ge(dve_s.sem, dve_s.at(g, "col"))
                            nc.vector.tensor_scalar(m_col[:, ds(g * R, R)], m_col[:, ds(g * R, R)], BIG, None,
                                                    ALU.subtract).then_inc(dve_s.sem, dve_s.one("m"))
                            dve.wait_ge(dve_s.sem, dve_s.at(g, "m"))
                            for r in range(R):
                                nc.vector.tensor_scalar(onto[:, r, :], ident[:, :], m_col[:, ds(g * R + r, 1)], None,
                                                        ALU.mult).then_inc(dve_s.sem, dve_s.one("onto", r))
                            dve.wait_ge(pe_s.sem, pe_s.at(g, "spread"))
                            nc.vector.tensor_copy(m_row[:, ds(g * GW, GW)], bank[5][:, :]
                                                  ).then_inc(dve_s.sem, dve_s.one("row"))

                @block.tensor
                def _(pe):
                    with pe.Fori(0, G // 2) as b:
                        for half in range(2):
                            g = b * 2 + half
                            pe.wait_ge(s_qin[half], b * 16 + 16)
                            pe.sem_inc(s_pass[2], 1)
                            with pe.Fori(0, Q) as q:
                                n = g * Q + q
                                for r in range(R):
                                    pe.wait_ge(dve_q.sem, dve_q.before(n, "max", r))
                                    c = ds(q * (R * P) + r * P, P)
                                    for k in range(K):
                                        nc.tensor.matmul(bank[r][:, :], kT[0][:, k, c], q_hi[:, half, k, :],
                                                         start=(k == 0), stop=False)
                                    pe.wait_ge(act_q.sem, act_q.at(n, "m16", r))
                                    nc.tensor.matmul(bank[r][:, :], big16[:, :], m16[:, r, :], start=False,
                                                     stop=True).then_inc(pe_q.sem, pe_q.one("s", r))
                            pe.wait_ge(dve_s.sem, dve_s.at(g, "join", 2))
                            transposes(pe, bank[4], lambda r: top_of[:, 0, r * P:(r + 1) * P]
                                       ).then_inc(pe_s.sem, pe_s.one("turn"))
                            for r in range(R):
                                pe.wait_ge(dve_s.sem, dve_s.at(g, "onto", r))
                                last = nc.tensor.matmul(bank[5][:, r * P:(r + 1) * P], ones[:, :], onto[:, r, :],
                                                        start=True, stop=True)
                            last.then_inc(pe_s.sem, pe_s.one("spread"))
            whole[0] += G // 2
            for x_ in (dve_s, pe_s):
                x_.close(G)
            for x_ in (pe_q, act_q, dve_q):
                x_.close(G * Q)

        def attend():
            with ExitStack() as mem, nc.Block() as block:
                mask = sb(mem, "mask", [P, 2, T * GW], U8)
                qh = spare[:, 0:4 * K * GW].rearrange("p (h a k n) -> p h a k n", h=2, a=2, k=K)
                p32 = sb(mem, "p32", [P, R, GW], F32)
                ph = sb(mem, "ph", [P, R, GW], F16)
                pl = sb(mem, "pl", [P, R, GW], F16)
                rden = sb(mem, "rden", [P, R], F32)
                res = w_gate[0][:, 0:2 * R * D].bitcast(F32)
                gap = w_gate[1][:, 0:2 * R * D].bitcast(F32)
                xg = [s_row[:, i * R * D:(i + 1) * R * D] for i in range(2)]
                xo = s_row[:, 2 * R * D:3 * R * D]
                Q = T // R
                pe_l.plan(("s", R))
                pe_q.plan(("pv", R))
                act_q.plan(("exp", R), ("hi", R))
                dve_q.plan(("z", R), ("p", R), ("lo", R))
                pe_s.plan(("block", 1))
                act_s.plan(("res", R))
                dve_s.plan(("diag", R), ("rden", R), ("gap", R), ("gap2", R), ("sel", R), ("out", 1))
                masks = 16 * whole[0]
                qs = 16 * (G // 2)

                @block.sync
                def _(sp):
                    with sp.Fori(0, G // 2) as b:
                        for half in range(2):
                            g = b * 2 + half
                            sp.wait_ge(pe_s.sem, pe_s.before(g, "block", 0, 2))
                            sp.wait_ge(dve_s.sem, dve_s.before(g, "out", 0, 2))
                            at = ds(b * (2 * P) + half * P, P)
                            sp.dma_start(mask[:, half, :], mask_d[at, :]).then_inc(s_whole[half], 16)
                            sp.dma_start(qh[:, half, :, :, :].rearrange("p a k n -> p (a k n)"), qT_d[at, :]
                                         ).then_inc(s_qin[half], 16)
                            sp.dma_start(xg[half], x3_d[at, :]).then_inc(s_qin[half], 16)
                    sp.wait_ge(s_out, 16 * G)

                @block.gpsimd
                def _(pool):
                    with pool.Fori(0, G) as g:
                        pool.wait_ge(dve_s.sem, dve_s.at(g, "out"))
                        pool.sem_inc(s_pass[1], 1)
                        nc.gpsimd.dma_start(out[ds(g * P, P), :], xo
                                            ).then_inc(s_out, 16)

                @block.scalar
                def _(act):
                    with act.Fori(0, G // 2) as b:
                        for half in range(2):
                            g = b * 2 + half
                            with act.Fori(0, Q) as q:
                                n = g * Q + q
                                for r in range(R):
                                    act.wait_ge(dve_q.sem, dve_q.at(n, "z", r))
                                    nc.scalar.activation(p32[:, r, :], p32[:, r, :], ACT.Exp
                                                         ).then_inc(act_q.sem, act_q.one("exp", r))
                                for r in range(R):
                                    act.wait_ge(dve_q.sem, dve_q.at(n, "p", r))
                                    act.wait_ge(pe_q.sem, pe_q.before(n, "pv", r))
                                    nc.scalar.copy(ph[:, r, :], p32[:, r, :]
                                                   ).then_inc(act_q.sem, act_q.one("hi", r))
                            for r in range(R):
                                act.wait_ge(dve_s.sem, dve_s.at(g, "rden", r))
                                nc.scalar.mul(row(res, r), bank[4 + r][:, 0:D], rden[:, r:r + 1]
                                              ).then_inc(act_s.sem, act_s.one("res", r))

                @block.vector
                def _(dve):
                    with dve.Fori(0, G // 2) as b:
                        for half in range(2):
                            g = b * 2 + half
                            dve.wait_ge(s_whole[half], b * 16 + (masks + 16))
                            for r in range(R):
                                own = mask[:, half, ds(g * (R * GW) + (r * GW + r * P), P)]
                                nc.vector.tensor_tensor(own, own, ident8[:, :], ALU.max
                                                        ).then_inc(dve_s.sem, dve_s.one("diag", r))
                            dve.wait_ge(dve_s.sem, dve_s.at(g, "diag", R - 1))
                            dve.sem_inc(s_pass[0], 1)
                            with dve.Fori(0, Q) as q:
                                n = g * Q + q
                                for r in range(R):
                                    dve.wait_ge(pe_l.sem, pe_l.at(n, "s", r))
                                    dve.wait_ge(dve_q.sem, dve_q.before(n, "lo", r))
                                    nc.vector.tensor_tensor(p32[:, r, :], bank[r][:, :], m_row[:, ds(g * GW, GW)],
                                                            ALU.subtract).then_inc(dve_q.sem, dve_q.one("z", r))
                                for r in range(R):
                                    dve.wait_ge(act_q.sem, act_q.at(n, "exp", r))
                                    nc.vector.scalar_tensor_tensor(
                                        out=p32[:, r, :], in0=p32[:, r, :], scalar=TOP,
                                        in1=mask[:, half, ds(q * (R * GW) + r * GW, GW)], op0=ALU.min, op1=ALU.mult
                                        ).then_inc(dve_q.sem, dve_q.one("p", r))
                                for r in range(R):
                                    dve.wait_ge(act_q.sem, act_q.at(n, "hi", r))
                                    nc.vector.tensor_tensor(pl[:, r, :], p32[:, r, :], ph[:, r, :], ALU.subtract
                                                            ).then_inc(dve_q.sem, dve_q.one("lo", r))
                            dve.wait_ge(pe_s.sem, pe_s.at(g, "block"))
                            for r in range(R):
                                nc.vector.reciprocal(rden[:, r:r + 1], bank[4 + r][:, D:D + 1]
                                                     ).then_inc(dve_s.sem, dve_s.one("rden", r))
                            for r in range(R):
                                dve.wait_ge(act_s.sem, act_s.at(g, "res", r))
                                nc.vector.tensor_tensor(row(gap, r), v_row(V, 0, g * R + r, D), row(res, r), ALU.subtract
                                                        ).then_inc(dve_s.sem, dve_s.one("gap", r))
                            for r in range(R):
                                dve.wait_ge(dve_s.sem, dve_s.at(g, "gap", r))
                                nc.vector.tensor_tensor(row(gap, r), row(gap, r), v_row(V, 1, g * R + r, D), ALU.add
                                                        ).then_inc(dve_s.sem, dve_s.one("gap2", r))
                            for r in range(R):
                                dve.wait_ge(dve_s.sem, dve_s.at(g, "gap2", r))
                                nc.vector.scalar_tensor_tensor(out=row(res, r), in0=row(gap, r),
                                                               scalar=loop_col[:, ds(g * R + r, 1)],
                                                               in1=row(res, r), op0=ALU.mult, op1=ALU.add
                                                               ).then_inc(dve_s.sem, dve_s.one("sel", r))
                            dve.wait_ge(dve_s.sem, dve_s.at(g, "sel", R - 1))
                            dve.wait_ge(s_out, g * 16)
                            dve.wait_ge(s_qin[half], b * 32 + (qs + 32))
                            nc.vector.tensor_tensor(xo, res, xg[half], ALU.add
                                                    ).then_inc(dve_s.sem, dve_s.one("out"))

                @block.tensor
                def _(pe):
                    def logits(g, q, half):
                        n = g * Q + q
                        for r in range(R):
                            pe.wait_ge(dve_q.sem, dve_q.before(n, "z", r))
                            c = ds(q * (R * P) + r * P, P)
                            products(pe, bank[r][:, :],
                                     [((kT[0][:, k, c], kT[1][:, k, c]), (qh[:, half, 0, k, :], qh[:, half, 1, k, :]))
                                      for k in range(K)]).then_inc(pe_l.sem, pe_l.one("s", r))

                    def values(g, q, edge=0):
                        n = g * Q + q
                        for r in range(R):
                            pe.wait_ge(dve_q.sem, dve_q.at(n, "lo", r))
                            first, final = edge == -1 and r == 0, edge == 1 and r == R - 1
                            t = q * R + r
                            for i in range(R):
                                acc = bank[4 + i][:, 0:D + 1]
                                c = slice(i * P, (i + 1) * P)
                                nc.tensor.matmul(acc, ph[:, r, c], v_row(V, 0, t), start=first, stop=False)
                                nc.tensor.matmul(acc, ph[:, r, c], v_row(V, 1, t), start=False, stop=False)
                                last = nc.tensor.matmul(acc, pl[:, r, c], v_row(V, 0, t), start=False, stop=final)
                            last.then_inc(pe_q.sem, pe_q.one("pv", r))

                    with pe.Fori(0, G // 2) as b:
                        for half in range(2):
                            g = b * 2 + half
                            pe.wait_ge(s_qin[half], b * 32 + (qs + 32))
                            logits(g, 0, half)
                            logits(g, 1, half)
                            pe.wait_ge(act_s.sem, act_s.before(g, "res", R - 1))
                            values(g, 0, -1)
                            with pe.Fori(1, Q - 1) as q:
                                logits(g, q + 1, half)
                                values(g, q)
                            values(g, Q - 1, 1)
                            pe.wait_ge(pe_q.sem, pe_q.at(g * Q + (Q - 1), "pv", R - 1))
                            pe.sem_inc(pe_s.sem, pe_s.one("block"))
            whole[0] += G // 2
            for x_ in (dve_s, pe_s, act_s):
                x_.close(G)
            for x_ in (pe_q, act_q, dve_q, pe_l):
                x_.close(G * Q)

        aggregate(value(VA), finish_layer0, 0.2, rows_of(VB))
        aggregate(value(VB), finish_layer1)
        kT = [sb(top, f"kT_{p}", [P, K, N], F16) for p in ("hi", "lo")]
        aggregate(value(VB), finish_layer2, 0.01, rows_of(VA))
        m_row = VB[:, 0:2 * N].bitcast(F32)
        spare = VB[:, 2 * N:4 * N]
        V = value(VA)
        row_maxima()
        attend()


_NAMES = ["L0_gnn_W", "L0_gnn_a_src", "L0_gnn_a_dst", "L0_gnn_W_bcdt", "L0_gnn_b_bcdt", "L0_gnn_abp_w",
          "L0_gnn_abp_b", "L0_gnn_cp_w", "L0_gnn_cp_b", "L0_gnn_W_hz", "L0_gnn_b_hz", "L0_gnn_out_w",
          "L0_gnn_out_b", "L0_gnn_fe1_w", "L0_gnn_fe1_b", "L0_gnn_fe_ln_g", "L0_gnn_fe_ln_b", "L0_gnn_fe2_w",
          "L0_gnn_fe2_b", "L0_gnn_A", "L0_gnn_D", "L0_gnn_g1_w", "L0_gnn_g1_b", "L0_gnn_g_ln_g",
          "L0_gnn_g_ln_b", "L0_gnn_g2_w", "L0_gnn_g2_b", "L0_gnn_ln_g", "L0_gnn_ln_b", "L1_gnn_b",
          "L2_gnn_W", "L2_gnn_a", "L3_gnn_Wq", "L3_gnn_Wk", "L3_gnn_Wv"]
_FLAT = ("L0_gnn_a_src", "L0_gnn_a_dst", "L0_gnn_cp_w", "L2_gnn_a")


def kernel(**inputs):
    import numpy as np
    import concourse.bacc as bacc
    from concourse.bass_utils import run_bass_kernel_spmd

    x, adj = np.asarray(inputs["x"]), np.asarray(inputs["adj"])
    arrays = {name: np.ascontiguousarray(inputs[name]) for name in _NAMES}
    for name in _FLAT:
        arrays[name] = arrays[name].reshape(-1)
    arrays["L1_gnn_WT"] = np.ascontiguousarray(np.asarray(inputs["L1_gnn_W"]).T)
    arrays["x"] = np.ascontiguousarray(x.reshape(G, R, P, D).transpose(0, 2, 1, 3)).reshape(G * P, R * D)
    arrays["adj"] = np.ascontiguousarray(adj.reshape(G, GW, T, P).transpose(0, 3, 2, 1)).reshape(G * P, T * GW)

    nc = bacc.Bacc("TRN2", target_bir_lowering=False, num_devices=1)
    aps = {name: nc.dram_tensor(f"in_{name}", v.shape, mybir.dt.from_np(v.dtype), kind="ExternalInput").ap()
           for name, v in arrays.items()}
    out = nc.dram_tensor("out_x", (G * P, R * D), F32, kind="ExternalOutput").ap()
    build(nc, aps, out)
    result = run_bass_kernel_spmd(nc, [{f"in_{name}": v for name, v in arrays.items()}], core_ids=[0])
    got = result.results[0]["out_x"]
    return np.ascontiguousarray(got.reshape(G, P, R, D).transpose(0, 2, 1, 3)).reshape(N, D)
```

```python
from contextlib import ExitStack

import concourse.bass as bass
from concourse import mybir

F32 = mybir.dt.float32
F16 = mybir.dt.float16
U8 = mybir.dt.uint8
ALU = mybir.AluOpType
ACT = mybir.ActivationFunctionType
AX_X = mybir.AxisListType.X
RMAX = bass.bass_isa.ReduceOp.max
ds = bass.ds

P = 128
N = 4096
D = 256
T = N // P
R = 4
G = T // R
GW = R * P
K = D // P
S = 128
H = 512
HK = H // P
VW = D + 2
EPS = 1e-5
BIG = 32768.0
PSCALE = 16384.0
START = 128
TOP = 60000.0


class Steps:

    def __init__(self, sem):
        self.sem, self.base = sem, START

    def plan(self, *stages):
        self.first, self.per, self.made = {}, 0, 0
        for name, n in stages:
            self.first[name] = self.per
            self.per += n

    def at(self, rnd, stage, i=0):
        return self.base + rnd * self.per + (self.first[stage] + i + 1)

    def before(self, rnd, stage, i=0, back=1):
        assert self.base >= back * self.per
        return self.at(rnd - back, stage, i)

    def one(self, stage, i=0):
        assert self.first[stage] + i == self.made % self.per, (stage, i, self.made % self.per)
        self.made += 1
        return 1

    def close(self, rounds):
        assert self.made % self.per == 0 and self.made
        self.base += rounds * self.per


def layout():
    dense = [("W0", K, D + 1), ("fe1", K, H), ("bcdt", K, 2 * S + 1), ("abp", 1, D), ("hz", K, 2 * H),
             ("out", HK, D), ("fe2", HK, D)]
    gate = [("g1", 2 * K, H), ("g2", HK, D)]
    later = [("W1", K, D), ("W2", K, D + 1), ("Wq", K, D), ("Wk", K, D), ("Wv", K, D)]
    where = {}
    sizes = []
    for pack, group in enumerate((dense, gate, later)):
        at = 0
        for name, k, n in group:
            where[name] = (pack, at, k, n)
            at += k * n
        sizes.append(at)
    bias, at = {}, 0
    for name, n in [("bcdt", 2 * S + 1), ("fe1", H), ("fe2", D), ("out", D), ("g1", H), ("g2", D), ("W1", D)]:
        bias[name] = (at, n)
        at += n
    return where, sizes, bias, at


def build(nc, a, out):
    where, sizes, bias_at, bias_n = layout()
    top = ExitStack()

    mask_d = nc.dram_tensor("mask_d", [G * P, T * GW], U8, kind="Internal").ap()
    x1_d, x2_d, x3_d = (nc.dram_tensor(n, [G * P, R * D], F32, kind="Internal").ap() for n in ("x1", "x2", "x3"))
    hs_d = nc.dram_tensor("hs_d", [G * P, R * D], F32, kind="Internal").ap()
    w_d = nc.dram_tensor("w_d", [G * P, R * D], F32, kind="Internal").ap()
    qT_d = nc.dram_tensor("qT_d", [G * P, 2 * K * GW], F16, kind="Internal").ap()

    named = set()

    def sb(stack, name, shape, dt):
        n = sum(x.split(".")[0] == name for x in named)
        named.add(f"{name}.{n}")
        return stack.enter_context(nc.sbuf_tensor(f"{name}_{n}" if n else name, shape, dt))

    def sem(name):
        return top.enter_context(nc.semaphore(name))

    with top:
        bank = [top.enter_context(nc.psum_tensor(f"bank{i}", [P, 512], F32)) for i in range(8)]
        pe_s, act_s, dve_s, pool_s = (Steps(sem(n)) for n in ("pe_done", "act_done", "dve_done", "pool_done"))
        pe_q, act_q, dve_q = (Steps(sem(n)) for n in ("pe_quad_done", "act_quad_done", "dve_quad_done"))
        pe_l = Steps(sem("pe_logits_done"))
        pre_s, act_v, dve_v = (Steps(sem(n)) for n in ("bounds_done", "act_values_done", "dve_values_done"))
        next_pe, next_act, next_dve, next_pool = (Steps(sem(f"{n}_next_done")) for n in ("pe", "act", "dve", "pool"))
        steps = (pe_s, act_s, dve_s, pool_s, pe_q, act_q, dve_q, pe_l, pre_s, act_v, dve_v,
                 next_pe, next_act, next_dve, next_pool)
        s_in = [sem(f"inputs_loaded_{i}") for i in range(4)]
        s_mst = sem("mask_stored")
        s_xin = sem("x_loaded")
        s_mask = [sem(f"mask_quad_loaded_{i}") for i in range(4)]
        s_whole = [sem("mask_loaded_0"), sem("mask_loaded_1")]
        s_qin = [sem("q_loaded_0"), sem("q_loaded_1")]
        s_store = sem("rows_stored")
        s_xout = sem("x_stored")
        s_out = sem("out_stored")
        s_pass = [sem("dve_passed"), sem("pool_passed"), sem("pe_passed"), sem("sp_passed")]

        ident = sb(top, "ident", [P, P], F32)
        ident8 = sb(top, "ident8", [P, P], U8)
        ones = sb(top, "ones", [P, P], F32)
        ones16 = sb(top, "ones16", [P, P], F16)
        big16 = sb(top, "big16", [P, P], F16)
        bias3 = sb(top, "bias3", [P, bias_n], F16)
        col_b = sb(top, "col_b", [P, 30], F32)
        lng = sb(top, "lng", [P, D], F32)
        lnb = sb(top, "lnb", [P, D], F32)
        nhalf = sb(top, "nhalf", [P, 8], F32)
        Dcol = sb(top, "Dcol", [P, 1], F32)
        w_src = sb(top, "w_src", [P, 2, K, 2, P], F16)
        d_col = sb(top, "d_col", [P, T], F32)
        omega = sb(top, "omega", [P, T], F32)
        vprime = sb(top, "vprime", [P, T], F32)
        m_col = sb(top, "m_col", [P, T], F32)
        loop_col = sb(top, "loop_col", [P, T], F32)
        dmax = sb(top, "dmax", [P, 2], F32)
        w_later = [sb(top, f"w_later_{p}", [P, sizes[2]], F16) for p in ("hi", "lo")]

        w_gate = [sb(top, f"w_gate_{p}", [P, sizes[1]], F16) for p in ("hi", "lo")]
        VA = sb(top, "VA", [P, 2 * T * VW], F16)
        VB = sb(top, "VB", [P, 2 * T * VW], F16)
        s_row = sb(top, "s_row", [P, N], F32)

        def value(t):
            return t[:, :]

        def rows_of(t):
            return t[:, 0:2 * T * D].bitcast(F32)

        dense_mem = ExitStack()
        w_dense = [sb(dense_mem, f"w_dense_{p}", [P, sizes[0]], F16) for p in ("hi", "lo")]
        packs = (w_dense, w_gate, w_later)
        BZ, BH, BABP, FEG, FEB, GG, GB = 0, 4, 8, 10, 14, 18, 22

        def w(name, k, c0=0, c1=None):
            pack, at, _, n = where[name]
            at += k * n
            c1 = n if c1 is None else c1
            return packs[pack][0][:, at + c0:at + c1], packs[pack][1][:, at + c0:at + c1]

        def products(pe, out_ap, pairs, bias=None):
            todo = []
            for (sh, sl), (mh, ml) in pairs:
                todo += [(sh, mh), (sh, ml), (sl, mh)]
            if bias is not None:
                at, n = bias_at[bias]
                todo.append((ones16[:, :], bias3[:, at:at + n]))
            for i, (st, mv) in enumerate(todo):
                last = nc.tensor.matmul(out_ap, st, mv, start=(i == 0), stop=(i == len(todo) - 1))
            return last

        def source_rows(pe, layer, hT, out_bank):
            return products(pe, out_bank[:, :],
                            [((w_src[:, layer, k, 0, :], w_src[:, layer, k, 1, :]), (hT[0][:, k, :], hT[1][:, k, :]))
                             for k in range(K)])

        xg = sb(dense_mem, "xg", [P, R * D], F32)
        h = sb(dense_mem, "h", [P, R * D], F32)
        hT = [sb(dense_mem, f"hT_{p}", [P, K, GW], F16) for p in ("hi", "lo")]
        st = sb(dense_mem, "st", [P, R, 6], F32)
        mv = sb(dense_mem, "mv", [P, R, 2], F32)
        ve = sb(dense_mem, "ve", [P, R], F32)
        rstd = sb(dense_mem, "rstd", [P, R], F32)
        nb = sb(dense_mem, "nb", [P, R], F32)
        next_pe.plan(("hT", K))
        next_act.plan(("h", R), ("hT", K))
        next_dve.plan(("stats", R), ("mean", R), ("var", 1), ("nb", 1), ("hT", K))
        next_pool.plan(("rstd", 1))

        def next_root(pool, g):
            pool.wait_ge(next_dve.sem, next_dve.at(g, "var"))
            nc.gpsimd.tensor_tensor(rstd[:, :], ve[:, :], nhalf[:, 0:R], ALU.pow
                                    ).then_inc(next_pool.sem, next_pool.one("rstd"))

        def next_h(act, g):
            act.wait_ge(next_dve.sem, next_dve.at(g, "nb"))
            for r in range(R):
                nc.scalar.activation(h[:, r * D:(r + 1) * D], xg[:, r * D:(r + 1) * D], ACT.Relu,
                                     bias=nb[:, r:r + 1], scale=rstd[:, r:r + 1]
                                     ).then_inc(next_act.sem, next_act.one("h", r))

        def next_hT_hi(act, g):
            for k in range(K):
                act.wait_ge(next_pe.sem, next_pe.at(g, "hT", k))
                nc.scalar.copy(hT[0][:, k, :], bank[2 + k][:, :]
                               ).then_inc(next_act.sem, next_act.one("hT", k))

        def next_moments(dve, g):
            dve.wait_ge(s_xin, g * 16 + 16)
            dve.sem_inc(s_pass[0], 1)
            for r in range(R):
                nc.vector.bn_stats(st[:, r, :], xg[:, r * D:(r + 1) * D]
                                   ).then_inc(next_dve.sem, next_dve.one("stats", r))
            dve.wait_ge(next_dve.sem, next_dve.at(g, "stats", R - 1))
            dve.sem_inc(s_pass[0], 1)
            for r in range(R):
                nc.vector.bn_aggr(mv[:, r, :], st[:, r, :]).then_inc(next_dve.sem, next_dve.one("mean", r))
            dve.wait_ge(next_dve.sem, next_dve.at(g, "mean", R - 1))
            nc.vector.tensor_scalar(ve[:, :], mv[:, :, 1], EPS, None, ALU.add
                                    ).then_inc(next_dve.sem, next_dve.one("var"))

        def next_nb(dve, g):
            dve.wait_ge(next_pool.sem, next_pool.at(g, "rstd"))
            nc.vector.scalar_tensor_tensor(out=nb[:, :], in0=mv[:, :, 0], scalar=-1.0, in1=rstd[:, :],
                                           op0=ALU.mult, op1=ALU.mult
                                           ).then_inc(next_dve.sem, next_dve.one("nb"))

        def next_hT_lo(dve, g):
            for k in range(K):
                dve.wait_ge(next_act.sem, next_act.at(g, "hT", k))
                nc.vector.tensor_tensor(hT[1][:, k, :], bank[2 + k][:, :], hT[0][:, k, :], ALU.subtract
                                        ).then_inc(next_dve.sem, next_dve.one("hT", k))

        def next_hT(pe, g):
            for k in range(K):
                for r in range(R):
                    if k == 0:
                        pe.wait_ge(next_act.sem, next_act.at(g, "h", r))
                    last = nc.tensor.transpose(bank[2 + k][:, r * P:(r + 1) * P],
                                               h[:, r * D + k * P:r * D + (k + 1) * P], ident[:, :])
                last.then_inc(next_pe.sem, next_pe.one("hT", k))

        with ExitStack() as mem, nc.Block() as block:
            stage = [VA[:, 0:2 * sizes[0]].bitcast(F32), VB[:, 0:2 * sizes[1]].bitcast(F32),
                     VB[:, 2 * sizes[1]:2 * (sizes[1] + sizes[2])].bitcast(F32)]
            src_col = sb(mem, "src_col", [P, 2, K], F32)
            wc = sb(mem, "wc", [P, K, S], F32)
            junk = sb(mem, "junk", [P, 11, D], F32)
            vecs = sb(mem, "vecs", [P, 4 * D], F32)
            cpw = sb(mem, "cpw", [P, S], F32)
            bc = sb(mem, "bc", [P, S], F32)
            arow = sb(mem, "arow", [P, S], F32)
            cpb = sb(mem, "cpb", [P, 2], F32)
            brow = sb(mem, "brow", [P, bias_n], F32)
            part = sb(mem, "part", [P, bias_n], F16)
            acc3 = sb(mem, "acc3", [P, bias_n], F32)
            early, dense_in, later_in = [], [], []

            def stage_w(loads, name, src, c0=0, n=None):
                pack, at, k, width = where[name]
                view = stage[pack][:, at:at + k * width].rearrange("p (k n) -> p k n", k=k)
                n = src.shape[1] if n is None else n
                loads.append((view[:, :, c0:c0 + n], src.rearrange("(k p) n -> p k n", p=P)))

            def spread(dst, vec):
                early.append((dst, vec.partition_broadcast(P)))

            spread(cpw[:, :], a["L0_gnn_cp_w"])
            spread(bc[:, :], a["L0_gnn_b_bcdt"][S:2 * S])
            spread(arow[:, :], a["L0_gnn_A"])
            spread(cpb[:, 0:1], a["L0_gnn_cp_b"])
            spread(brow[:, 0:S], a["L0_gnn_b_bcdt"][0:S])
            spread(brow[:, S:2 * S], a["L0_gnn_b_bcdt"][2 * S:3 * S])
            for name, vec in (("fe1", "L0_gnn_fe1_b"), ("fe2", "L0_gnn_fe2_b"), ("out", "L0_gnn_out_b"),
                              ("g1", "L0_gnn_g1_b"), ("g2", "L0_gnn_g2_b"), ("W1", "L1_gnn_b")):
                at, n = bias_at[name]
                spread(brow[:, at:at + n], a[vec])
            bias_loads = len(early)
            spread(vecs[:, 0:D], a["L0_gnn_a_src"])
            spread(vecs[:, D:2 * D], a["L0_gnn_a_dst"])
            spread(vecs[:, 2 * D:4 * D], a["L2_gnn_a"])
            early.append((wc[:, :, :], a["L0_gnn_W_bcdt"][:, S:2 * S].rearrange("(k p) n -> p k n", p=P)))
            stage_w(early, "W0", a["L0_gnn_W"])
            stage_w(early, "W2", a["L2_gnn_W"])

            stage_w(dense_in, "bcdt", a["L0_gnn_W_bcdt"][:, 0:S], 0)
            stage_w(dense_in, "bcdt", a["L0_gnn_W_bcdt"][:, 2 * S:3 * S], S)
            stage_w(dense_in, "fe1", a["L0_gnn_fe1_w"])
            stage_w(dense_in, "abp", a["L0_gnn_abp_w"])
            stage_w(dense_in, "hz", a["L0_gnn_W_hz"])
            stage_w(dense_in, "out", a["L0_gnn_out_w"])
            stage_w(dense_in, "fe2", a["L0_gnn_fe2_w"])
            stage_w(later_in, "g1", a["L0_gnn_g1_w"])
            stage_w(later_in, "g2", a["L0_gnn_g2_w"])
            stage_w(later_in, "W1", a["L1_gnn_WT"])
            stage_w(later_in, "Wq", a["L3_gnn_Wq"])
            stage_w(later_in, "Wk", a["L3_gnn_Wk"])
            stage_w(later_in, "Wv", a["L3_gnn_Wv"])
            later_in += [(t[:, :], a[vec].partition_broadcast(P))
                         for t, vec in ((Dcol, "L0_gnn_D"), (lng, "L0_gnn_ln_g"), (lnb, "L0_gnn_ln_b"))]
            for at, vec in ((BH, a["L0_gnn_b_hz"][0:H]), (BZ, a["L0_gnn_b_hz"][H:2 * H]), (BABP, a["L0_gnn_abp_b"]),
                            (FEG, a["L0_gnn_fe_ln_g"]), (FEB, a["L0_gnn_fe_ln_b"]),
                            (GG, a["L0_gnn_g_ln_g"]), (GB, a["L0_gnn_g_ln_b"])):
                n = vec.shape[0] // P
                later_in.append((col_b[:, at:at + n], vec.rearrange("(k p) -> p k", p=P)))

            def load(eng, loads, sem_of):
                for i, (dst, src) in enumerate(loads):
                    with nc.allow_non_contiguous_dma(reason="small vectors"):
                        eng.dma_start(dst, src).then_inc(sem_of(i), 16)

            dve_s.plan(("ones", 1), ("row", 2), ("acc0", 1), ("rest0", 1), ("acc1", 1), ("rest1", 1), ("fold", 9),
                       ("src", 4), ("bias", 1), ("big", 1), ("split", 3))
            pool_s.plan(("zero", 3), ("ident", 2), ("one", 1))
            act_s.plan(("part", 3), ("hi", 3))

            @block.sync
            def _(sp):
                for x_ in steps:
                    sp.sem_inc(x_.sem, START)
                sp.dma_start(xg[:, :], a["x"][0:P, :]).then_inc(s_xin, 16)
                load(sp, early, lambda i: s_in[0] if i < bias_loads else s_in[1])
                load(sp, later_in, lambda i: s_in[3])

            @block.gpsimd
            def _(pool):
                nc.gpsimd.memset(ident[:, :], 0.0).then_inc(pool_s.sem, pool_s.one("zero", 0))
                nc.gpsimd.memset(ones[:, :], 1.0).then_inc(pool_s.sem, pool_s.one("zero", 1))
                nc.gpsimd.memset(nhalf[:, :], -0.5).then_inc(pool_s.sem, pool_s.one("zero", 2))
                pool.wait_ge(pool_s.sem, pool_s.at(0, "zero", 0))
                nc.gpsimd.affine_select(out=ident[:, :], in_=ident[:, :], compare_op=ALU.not_equal, fill=1.0,
                                        base=0, pattern=[[-1, P]], channel_multiplier=1
                                        ).then_inc(pool_s.sem, pool_s.one("ident", 0))
                pool.wait_ge(pool_s.sem, pool_s.at(0, "ident", 0))
                nc.gpsimd.tensor_copy(ident8[:, :], ident[:, :]).then_inc(pool_s.sem, pool_s.one("ident", 1))
                nc.gpsimd.tensor_copy(ones16[:, :], ones[:, :]).then_inc(pool_s.sem, pool_s.one("one", 0))
                pool.wait_ge(pool_s.sem, pool_s.at(0, "zero", 2))
                next_root(pool, 0)

            @block.scalar
            def _(act):
                load(act, dense_in, lambda i: s_in[2])
                next_h(act, 0)
                for q, ready in enumerate((("row", 1), ("rest0", 0), ("rest1", 0))):
                    act.wait_ge(dve_s.sem, dve_s.at(0, *ready))
                    nc.scalar.copy(part[:, :], brow[:, :]).then_inc(act_s.sem, act_s.one("part", q))
                    if q == 0:
                        next_hT_hi(act, 0)
                act.wait_ge(s_in[1], 16 * (len(early) - bias_loads))
                act.wait_ge(dve_s.sem, dve_s.at(0, "fold", 8))
                for i in range(3):
                    act.wait_ge(*((s_in[2], 16 * len(dense_in)) if i == 0 else (s_in[3], 16 * len(later_in))))
                    nc.scalar.copy(packs[i][0][:, :], stage[i][:, :]).then_inc(act_s.sem, act_s.one("hi", i))

            @block.tensor
            def _(pe):
                pe.wait_ge(pool_s.sem, pool_s.at(0, "ident", 0))
                next_hT(pe, 0)

            @block.vector
            def _(dve):
                next_moments(dve, 0)
                next_nb(dve, 0)
                dve.wait_ge(s_in[0], 16 * bias_loads)
                dve.wait_ge(pool_s.sem, pool_s.at(0, "one"))
                nc.vector.tensor_tensor_reduce(
                    out=junk[:, 10, 0:S], in0=bc[:, :], in1=cpw[:, :], scale=1.0, scalar=1.0, op0=ALU.mult,
                    op1=ALU.add, accum_out=cpb[:, 1:2]).then_inc(dve_s.sem, dve_s.one("ones"))
                dve.wait_ge(dve_s.sem, dve_s.at(0, "ones"))
                nc.vector.tensor_tensor(brow[:, 2 * S:2 * S + 1], cpb[:, 0:1], cpb[:, 1:2], ALU.add
                                        ).then_inc(dve_s.sem, dve_s.one("row", 0))
                nc.vector.tensor_tensor(brow[:, S:2 * S], brow[:, S:2 * S], arow[:, :], ALU.add
                                        ).then_inc(dve_s.sem, dve_s.one("row", 1))
                dve.wait_ge(act_s.sem, act_s.at(0, "part", 0))
                nc.vector.tensor_scalar(acc3[:, :], part[:, :], ident[:, 0:1], None, ALU.mult
                                        ).then_inc(dve_s.sem, dve_s.one("acc0"))
                nc.vector.tensor_tensor(brow[:, :], brow[:, :], part[:, :], ALU.subtract
                                        ).then_inc(dve_s.sem, dve_s.one("rest0"))
                next_hT_lo(dve, 0)
                dve.wait_ge(act_s.sem, act_s.at(0, "part", 1))
                dve.wait_ge(dve_s.sem, dve_s.at(0, "rest0"))
                nc.vector.scalar_tensor_tensor(out=acc3[:, :], in0=part[:, :], scalar=ident[:, 1:2], in1=acc3[:, :],
                                               op0=ALU.mult, op1=ALU.add).then_inc(dve_s.sem, dve_s.one("acc1"))
                nc.vector.tensor_tensor(brow[:, :], brow[:, :], part[:, :], ALU.subtract
                                        ).then_inc(dve_s.sem, dve_s.one("rest1"))
                dve.wait_ge(s_in[1], 16 * (len(early) - bias_loads))
                n = 0
                for layer, (name, off) in enumerate((("W0", 0), ("W2", 2 * D))):
                    pack, at, k_, width = where[name]
                    for k in range(K):
                        for j in range(2):
                            base = at + k * width
                            ins = nc.vector.tensor_tensor_reduce(
                                out=junk[:, n, :], in0=stage[pack][:, base:base + D],
                                in1=vecs[:, off + j * D:off + (j + 1) * D], scale=1.0, scalar=0.0,
                                op0=ALU.mult, op1=ALU.add, accum_out=stage[pack][:, base + D:base + D + 1] if j else
                                src_col[:, layer, k:k + 1])
                            ins.then_inc(dve_s.sem, dve_s.one("fold", n))
                            n += 1
                pack, at, k_, width = where["bcdt"]
                for k in range(K):
                    last = nc.vector.tensor_tensor_reduce(
                        out=junk[:, 8 + k, 0:S], in0=wc[:, k, :], in1=cpw[:, :], scale=1.0, scalar=0.0, op0=ALU.mult,
                        op1=ALU.add, accum_out=stage[pack][:, at + k * width + 2 * S:at + k * width + 2 * S + 1])
                last.then_inc(dve_s.sem, dve_s.one("fold", 8))
                dve.wait_ge(dve_s.sem, dve_s.at(0, "fold", 8))
                n = 0
                for layer in range(2):
                    for k in range(K):
                        col, (hi_part, lo_part) = src_col[:, layer, k:k + 1], (w_src[:, layer, k, i, :] for i in range(2))
                        nc.vector.tensor_scalar(hi_part, ones[:, :], col, None, ALU.mult
                                                ).then_inc(dve_s.sem, dve_s.one("src", n))
                        dve.wait_ge(dve_s.sem, dve_s.at(0, "src", n))
                        nc.vector.scalar_tensor_tensor(out=lo_part, in0=ones[:, :], scalar=col, in1=hi_part,
                                                       op0=ALU.mult, op1=ALU.subtract)
                        n += 1
                dve.wait_ge(act_s.sem, act_s.at(0, "part", 2))
                nc.vector.scalar_tensor_tensor(out=bias3[:, :], in0=part[:, :], scalar=ident[:, 2:3], in1=acc3[:, :],
                                               op0=ALU.mult, op1=ALU.add).then_inc(dve_s.sem, dve_s.one("bias"))
                nc.vector.tensor_scalar(big16[:, :], ident[:, :], BIG, None, ALU.mult
                                        ).then_inc(dve_s.sem, dve_s.one("big"))
                for i in range(3):
                    dve.wait_ge(act_s.sem, act_s.at(0, "hi", i))
                    nc.vector.tensor_tensor(packs[i][1][:, :], stage[i][:, :], packs[i][0][:, :], ALU.subtract
                                            ).then_inc(dve_s.sem, dve_s.one("split", i))

        for x_ in (dve_s, pool_s, act_s):
            x_.close(1)

        with ExitStack() as mem, nc.Block() as block:
            wh = rows_of(VB)
            whT = [sb(mem, f"whT_{p}", [P, K, GW], F16) for p in ("hi", "lo")]
            whT32 = sb(mem, "whT32", [P, K, GW], F32)
            ex = sb(mem, "ex", [P, R, S], F32)
            asmbT = [sb(mem, f"asmbT_{p}", [P, GW], F16) for p in ("hi", "lo")]
            hsT32 = sb(mem, "hsT32", [P, K, GW], F32)
            hsT = [sb(mem, f"hsT_{p}", [P, K, GW], F16) for p in ("hi", "lo")]
            hp = sb(mem, "hp", [P, HK, GW], F32)
            part16 = [VA[:, i * HK * GW:(i + 1) * HK * GW] for i in range(8)]
            whole32 = [VA[:, 2 * i * HK * GW:2 * (i + 1) * HK * GW].bitcast(F32) for i in range(2)]
            as_tiles = lambda t: t.rearrange("p (k n) -> p k n", k=HK)
            fey, feT32 = as_tiles(whole32[0]), as_tiles(whole32[1])
            feT = [as_tiles(part16[4]), as_tiles(part16[5])]
            mT = [as_tiles(part16[6]), as_tiles(part16[7])]
            hsr = sb(mem, "hsr", [P, R * D], F32)
            wr = sb(mem, "wr", [P, R * D], F32)
            st2 = sb(mem, "st2", [P, R, 6], F32)
            mv2 = sb(mem, "mv2", [P, R, 2], F32)
            ve2 = sb(mem, "ve2", [P, R], F32)
            rstd2 = sb(mem, "rstd2", [P, R], F32)
            nmax = sb(mem, "nmax", [P, R], F32)
            esum = sb(mem, "esum", [P, R], F32)
            rsum = sb(mem, "rsum", [P, R], F32)
            c1 = sb(mem, "c1", [P, R], F32)

            pe_s.plan(("whT", K), ("srow", 1), ("wh", R), ("bcdt", R), ("fe1", R), ("asmbT", 1),
                      ("abT", K), ("hz", 2 * HK), ("feT", HK), ("out", R), ("fe2", R))
            act_s.plan(("whT32", K), ("whT", K), ("srow", 1), ("wh", R), ("ex", R), ("asmbT", 1),
                       ("hsT", K), ("hz", 2 * HK), ("mT", HK), ("silu", HK), ("feT", HK))
            dve_s.plan(("whT", K), ("d", R), ("softmax", 2 * R), ("rsum", R), ("asmb", R), ("asmbT", 1),
                       ("hsT32", K), ("hsT", K), ("stats2", R), ("mean2", R), ("var2", 1), ("fey", R),
                       ("mT32", HK), ("mT", HK), ("feT", HK), ("hs", 2), ("w", 2))
            pool_s.plan(("rstd2", 1))

            @block.sync
            def _(sp):
                sp.wait_ge(next_act.sem, next_act.at(0, "h", R - 1))
                sp.dma_start(xg[:, :], a["x"][P:2 * P, :]).then_inc(s_xin, 16)
                with sp.Fori(0, G) as g:
                    sp.wait_ge(next_act.sem, next_act.at(g + 1, "h", R - 1))
                    sp.sem_inc(s_pass[3], 1)
                    sp.dma_start(xg[:, :], a["x"][ds(((g + 2) % G) * P, P), :]).then_inc(s_xin, 16)
                    sp.wait_ge(dve_s.sem, dve_s.at(g, "w", 1))
                    sp.sem_inc(s_pass[3], 1)
                    sp.dma_start(hs_d[ds(g * P, P), :], hsr[:, :]).then_inc(s_store, 16)
                    sp.dma_start(w_d[ds(g * P, P), :], wr[:, :]).then_inc(s_store, 16)
                sp.wait_ge(s_store, 32 * G)
                sp.wait_ge(s_xin, 16 * (G + 2))

            @block.gpsimd
            def _(pool):
                with pool.Fori(0, G) as g:
                    nc.gpsimd.dma_start(mask_d[ds(g * P, P), :], a["adj"][ds(g * P, P), :]).then_inc(s_mst, 16)
                    pool.wait_ge(dve_s.sem, dve_s.at(g, "var2"))
                    nc.gpsimd.tensor_tensor(rstd2[:, :], ve2[:, :], nhalf[:, 0:R], ALU.pow
                                            ).then_inc(pool_s.sem, pool_s.one("rstd2"))
                    next_root(pool, g + 1)
                pool.wait_ge(s_mst, 16 * G)

            @block.scalar
            def _(act):
                def hi(dst, src, stage, i):
                    nc.scalar.copy(dst, src).then_inc(act_s.sem, act_s.one(stage, i))

                with act.Fori(0, G) as g:
                    for k in range(K):
                        act.wait_ge(pe_s.sem, pe_s.at(g, "whT", k))
                        nc.scalar.copy(whT32[:, k, :], bank[k][:, :]).then_inc(act_s.sem, act_s.one("whT32", k))
                    for k in range(K):
                        act.wait_ge(act_s.sem, act_s.at(g, "whT32", k))
                        hi(whT[0][:, k, :], whT32[:, k, :], "whT", k)
                    act.wait_ge(pe_s.sem, pe_s.at(g, "srow"))
                    nc.scalar.copy(s_row[:, ds(g * GW, GW)], bank[2][:, :]
                                   ).then_inc(act_s.sem, act_s.one("srow"))
                    for r in range(R):
                        act.wait_ge(pe_s.sem, pe_s.at(g, "wh", r))
                        nc.scalar.copy(wh[:, ds(g * (R * D) + r * D, D)], bank[4 + r][:, 0:D]
                                       ).then_inc(act_s.sem, act_s.one("wh", r))
                    for r in range(R):
                        act.wait_ge(dve_s.sem, dve_s.at(g, "softmax", 2 * r + 1))
                        nc.scalar.activation(ex[:, r, :], bank[r][:, S:2 * S], ACT.Exp, bias=nmax[:, r:r + 1],
                                             scale=1.0, accum_out=esum[:, r:r + 1]
                                             ).then_inc(act_s.sem, act_s.one("ex", r))
                    act.wait_ge(pe_s.sem, pe_s.at(g, "asmbT"))
                    hi(asmbT[0][:, :], bank[0][:, :], "asmbT", 0)
                    for k in range(K):
                        act.wait_ge(dve_s.sem, dve_s.at(g, "hsT32", k))
                        hi(hsT[0][:, k, :], hsT32[:, k, :], "hsT", k)
                    for m in range(HK):
                        act.wait_ge(pe_s.sem, pe_s.at(g, "hz", 2 * m))
                        nc.scalar.activation(hp[:, m, :], bank[(0, 1)[m % 2]][:, :], ACT.Identity,
                                             bias=col_b[:, BH + m:BH + m + 1], scale=1.0
                                             ).then_inc(act_s.sem, act_s.one("hz", 2 * m))
                        act.wait_ge(pe_s.sem, pe_s.at(g, "hz", 2 * m + 1))
                        nc.scalar.activation(feT32[:, m, :], bank[(3, 2)[m % 2]][:, :], ACT.Silu,
                                             bias=col_b[:, BZ + m:BZ + m + 1], scale=1.0
                                             ).then_inc(act_s.sem, act_s.one("hz", 2 * m + 1))
                    for m in range(HK):
                        act.wait_ge(dve_s.sem, dve_s.at(g, "mT32", m))
                        hi(mT[0][:, m, :], hp[:, m, :], "mT", m)
                    for k in range(HK):
                        act.wait_ge(pe_s.sem, pe_s.at(g, "feT", k))
                        nc.scalar.activation(feT32[:, k, :], bank[4 + k][:, :], ACT.Silu,
                                             bias=col_b[:, FEB + k:FEB + k + 1], scale=col_b[:, FEG + k:FEG + k + 1]
                                             ).then_inc(act_s.sem, act_s.one("silu", k))
                    for k in range(HK):
                        act.wait_ge(act_s.sem, act_s.at(g, "silu", k))
                        hi(feT[0][:, k, :], feT32[:, k, :], "feT", k)
                    next_h(act, g + 1)
                    next_hT_hi(act, g + 1)

            @block.vector
            def _(dve):
                def lo(dst, src, hi_part, stage, i):
                    nc.vector.tensor_tensor(dst, src, hi_part, ALU.subtract).then_inc(dve_s.sem, dve_s.one(stage, i))

                with dve.Fori(0, G) as g:
                    for k in range(K):
                        dve.wait_ge(act_s.sem, act_s.at(g, "whT", k))
                        lo(whT[1][:, k, :], whT32[:, k, :], whT[0][:, k, :], "whT", k)
                    for r in range(R):
                        dve.wait_ge(act_s.sem, act_s.at(g, "wh", r))
                        nc.vector.tensor_copy(d_col[:, ds(g * R + r, 1)], bank[4 + r][:, D:D + 1]
                                              ).then_inc(dve_s.sem, dve_s.one("d", r))
                    for r in range(R):
                        dve.wait_ge(pe_s.sem, pe_s.at(g, "bcdt", r))
                        nc.vector.tensor_copy(c1[:, r:r + 1], bank[r][:, 2 * S:2 * S + 1]
                                              ).then_inc(dve_s.sem, dve_s.one("softmax", 2 * r))
                        nc.vector.tensor_reduce(nmax[:, r:r + 1], bank[r][:, S:2 * S], AX_X, ALU.max, negate=True
                                                ).then_inc(dve_s.sem, dve_s.one("softmax", 2 * r + 1))
                    for r in range(R):
                        dve.wait_ge(act_s.sem, act_s.at(g, "ex", r))
                        nc.vector.reciprocal(rsum[:, r:r + 1], esum[:, r:r + 1]
                                             ).then_inc(dve_s.sem, dve_s.one("rsum", r))
                    for r in range(R):
                        dve.wait_ge(dve_s.sem, dve_s.at(g, "rsum", r))
                        nc.vector.scalar_tensor_tensor(out=ex[:, r, :], in0=ex[:, r, :], scalar=rsum[:, r:r + 1],
                                                       in1=bank[r][:, 0:S], op0=ALU.mult, op1=ALU.mult
                                                       ).then_inc(dve_s.sem, dve_s.one("asmb", r))
                    dve.wait_ge(act_s.sem, act_s.at(g, "asmbT"))
                    lo(asmbT[1][:, :], bank[0][:, :], asmbT[0][:, :], "asmbT", 0)
                    for k in range(K):
                        dve.wait_ge(pe_s.sem, pe_s.at(g, "abT", k))
                        nc.vector.scalar_tensor_tensor(out=hsT32[:, k, :], in0=bank[1 + k][:, :],
                                                       scalar=col_b[:, BABP + k:BABP + k + 1], in1=whT32[:, k, :],
                                                       op0=ALU.add, op1=ALU.mult
                                                       ).then_inc(dve_s.sem, dve_s.one("hsT32", k))
                    for k in range(K):
                        dve.wait_ge(act_s.sem, act_s.at(g, "hsT", k))
                        lo(hsT[1][:, k, :], hsT32[:, k, :], hsT[0][:, k, :], "hsT", k)
                    for r in range(R):
                        dve.wait_ge(pe_s.sem, pe_s.at(g, "fe1", r))
                        nc.vector.bn_stats(st2[:, r, :], bank[4 + r][:, :]
                                           ).then_inc(dve_s.sem, dve_s.one("stats2", r))
                    dve.wait_ge(dve_s.sem, dve_s.at(g, "stats2", R - 1))
                    dve.sem_inc(s_pass[0], 1)
                    for r in range(R):
                        nc.vector.bn_aggr(mv2[:, r, :], st2[:, r, :]).then_inc(dve_s.sem, dve_s.one("mean2", r))
                    dve.wait_ge(dve_s.sem, dve_s.at(g, "mean2", R - 1))
                    nc.vector.tensor_scalar(ve2[:, :], mv2[:, :, 1], EPS, None, ALU.add
                                            ).then_inc(dve_s.sem, dve_s.one("var2"))
                    next_moments(dve, g + 1)
                    dve.wait_ge(pool_s.sem, pool_s.at(g, "rstd2"))
                    for r in range(R):
                        nc.vector.tensor_scalar(fey[:, r, :], bank[4 + r][:, :], mv2[:, r, 0:1], rstd2[:, r:r + 1],
                                                ALU.subtract, ALU.mult).then_inc(dve_s.sem, dve_s.one("fey", r))
                    next_nb(dve, g + 1)
                    for m in range(HK):
                        dve.wait_ge(act_s.sem, act_s.at(g, "hz", 2 * m + 1))
                        nc.vector.scalar_tensor_tensor(out=hp[:, m, :], in0=feT32[:, m, :], scalar=Dcol[:, :],
                                                       in1=hp[:, m, :], op0=ALU.add, op1=ALU.mult
                                                       ).then_inc(dve_s.sem, dve_s.one("mT32", m))
                    for m in range(HK):
                        dve.wait_ge(act_s.sem, act_s.at(g, "mT", m))
                        lo(mT[1][:, m, :], hp[:, m, :], mT[0][:, m, :], "mT", m)
                    for k in range(HK):
                        dve.wait_ge(act_s.sem, act_s.at(g, "feT", k))
                        lo(feT[1][:, k, :], feT32[:, k, :], feT[0][:, k, :], "feT", k)
                    dve.wait_ge(s_store, g * 32)
                    for j in range(2):
                        dve.wait_ge(pe_s.sem, pe_s.at(g, "out", 2 * j + 1))
                        for r in (2 * j, 2 * j + 1):
                            last = nc.vector.tensor_scalar(hsr[:, r * D:(r + 1) * D],
                                                           bank[j][:, (r % 2) * D:(r % 2 + 1) * D], c1[:, r:r + 1],
                                                           None, ALU.mult)
                        last.then_inc(dve_s.sem, dve_s.one("hs", j))
                    next_hT_lo(dve, g + 1)
                    for j in range(2):
                        dve.wait_ge(dve_s.sem, dve_s.at(g, "hs", j))
                        dve.wait_ge(pe_s.sem, pe_s.at(g, "fe2", 2 * j + 1))
                        nc.vector.tensor_tensor(wr[:, j * 2 * D:(j + 1) * 2 * D], bank[4 + j][:, :],
                                                hsr[:, j * 2 * D:(j + 1) * 2 * D], ALU.add
                                                ).then_inc(dve_s.sem, dve_s.one("w", j))

            @block.tensor
            def _(pe):
                def cols(t, k, r):
                    return t[0][:, k, r * P:(r + 1) * P], t[1][:, k, r * P:(r + 1) * P]

                def fe1(g, r):
                    pe.wait_ge(act_s.sem, act_s.at(g, "wh", r))
                    pe.wait_ge(dve_s.sem, dve_s.at(g, "d", r))
                    products(pe, bank[4 + r][:, :], [(cols(whT, k, r), w("fe1", k)) for k in range(K)], "fe1"
                             ).then_inc(pe_s.sem, pe_s.one("fe1", r))

                with pe.Fori(0, G) as g:
                    pe.wait_ge(next_dve.sem, next_dve.at(g, "hT", K - 1))
                    pe.wait_ge(dve_s.sem, dve_s.before(g, "hs", 1))
                    for m in range(K):
                        products(pe, bank[m][:, :],
                                 [(w("W0", k, m * P, (m + 1) * P), (hT[0][:, k, :], hT[1][:, k, :]))
                                  for k in range(K)]).then_inc(pe_s.sem, pe_s.one("whT", m))
                    source_rows(pe, 0, hT, bank[2]).then_inc(pe_s.sem, pe_s.one("srow"))
                    pe.wait_ge(dve_s.sem, dve_s.before(g, "w", 1))
                    for r in range(R):
                        products(pe, bank[4 + r][:, 0:D + 1],
                                 [(cols(hT, k, r), w("W0", k)) for k in range(K)]
                                 ).then_inc(pe_s.sem, pe_s.one("wh", r))
                    pe.wait_ge(dve_s.sem, dve_s.at(g, "whT", K - 1))
                    pe.wait_ge(act_s.sem, act_s.at(g, "srow"))
                    for r in range(R):
                        products(pe, bank[r][:, 0:2 * S + 1],
                                 [(cols(whT, k, r), w("bcdt", k)) for k in range(K)], "bcdt"
                                 ).then_inc(pe_s.sem, pe_s.one("bcdt", r))
                    for r in range(R):
                        fe1(g, r)
                    pe.wait_ge(dve_s.sem, dve_s.at(g, "asmb", R - 1))
                    for r in range(R):
                        last = nc.tensor.transpose(bank[0][:, r * P:(r + 1) * P], ex[:, r, :], ident[:, :])
                    last.then_inc(pe_s.sem, pe_s.one("asmbT"))
                    pe.wait_ge(dve_s.sem, dve_s.at(g, "asmbT"))
                    for m in range(K):
                        products(pe, bank[1 + m][:, :],
                                 [(w("abp", 0, m * P, (m + 1) * P), (asmbT[0][:, :], asmbT[1][:, :]))]
                                 ).then_inc(pe_s.sem, pe_s.one("abT", m))
                    pe.wait_ge(dve_s.sem, dve_s.at(g, "hsT", K - 1))
                    for m in range(HK):
                        if m >= 2:
                            pe.wait_ge(act_s.sem, act_s.at(g, "hz", 2 * (m - 2) + 1))
                        for j, b in ((0, (0, 1)[m % 2]), (1, (3, 2)[m % 2])):
                            c0 = j * H + m * P
                            products(pe, bank[b][:, :],
                                     [(w("hz", k, c0, c0 + P), (hsT[0][:, k, :], hsT[1][:, k, :]))
                                      for k in range(K)]).then_inc(pe_s.sem, pe_s.one("hz", 2 * m + j))
                    pe.wait_ge(dve_s.sem, dve_s.at(g, "fey", R - 1))
                    for k in range(HK):
                        for r in range(R):
                            last = nc.tensor.transpose(bank[4 + k][:, r * P:(r + 1) * P],
                                                       fey[:, r, k * P:(k + 1) * P], ident[:, :])
                        last.then_inc(pe_s.sem, pe_s.one("feT", k))
                    pe.wait_ge(dve_s.sem, dve_s.at(g, "mT", HK - 1))
                    for r in range(R):
                        products(pe, bank[r // 2][:, (r % 2) * D:(r % 2 + 1) * D],
                                 [(cols(mT, m, r), w("out", m)) for m in range(HK)], "out"
                                 ).then_inc(pe_s.sem, pe_s.one("out", r))
                    next_hT(pe, g + 1)
                    pe.wait_ge(dve_s.sem, dve_s.at(g, "feT", HK - 1))
                    for r in range(R):
                        products(pe, bank[4 + r // 2][:, (r % 2) * D:(r % 2 + 1) * D],
                                 [(cols(feT, k, r), w("fe2", k)) for k in range(HK)], "fe2"
                                 ).then_inc(pe_s.sem, pe_s.one("fe2", r))
        for x_ in (pe_s, act_s, dve_s, pool_s):
            x_.close(G)
        for x_ in (next_pe, next_act, next_dve, next_pool):
            x_.close(G + 1)
        stored = [0]
        dense_mem.close()

        def v_row(V, part, t, n=D + 1):
            return V[:, ds(t * VW + part * (T * VW), n)]

        def moments(dve, g, srcs, st, mv, ve, names, ready_all=None):
            if ready_all is not None:
                dve.wait_ge(*ready_all)
                dve.sem_inc(s_pass[0], 1)
            for r, (src, ready) in enumerate(srcs):
                if ready is not None:
                    dve.wait_ge(*ready)
                nc.vector.bn_stats(st[:, r, :], src).then_inc(dve_s.sem, dve_s.one(names[0], r))
            dve.wait_ge(dve_s.sem, dve_s.at(g, names[0], R - 1))
            dve.sem_inc(s_pass[0], 1)
            for r in range(R):
                nc.vector.bn_aggr(mv[:, r, :], st[:, r, :]).then_inc(dve_s.sem, dve_s.one(names[1], r))
            dve.wait_ge(dve_s.sem, dve_s.at(g, names[1], R - 1))
            nc.vector.tensor_scalar(ve[:, :], mv[:, :, 1], EPS, None, ALU.add
                                    ).then_inc(dve_s.sem, dve_s.one(names[2]))

        def inverse_root(pool, g, rstd, ve, var, stage):
            pool.wait_ge(dve_s.sem, dve_s.at(g, var))
            nc.gpsimd.tensor_tensor(rstd[:, :], ve[:, :], nhalf[:, 0:R], ALU.pow
                                    ).then_inc(pool_s.sem, pool_s.one(stage))

        def shift(dve, g, nb, mv, rstd, stage, rstage):
            dve.wait_ge(pool_s.sem, pool_s.at(g, rstage))
            nc.vector.scalar_tensor_tensor(out=nb[:, :], in0=mv[:, :, 0], scalar=-1.0, in1=rstd[:, :],
                                           op0=ALU.mult, op1=ALU.mult).then_inc(dve_s.sem, dve_s.one(stage))

        def row(t, r, n=D):
            return t[:, r * n:(r + 1) * n]

        def cols(t, k, r):
            return t[0][:, k, r * P:(r + 1) * P], t[1][:, k, r * P:(r + 1) * P]

        def transposes(pe, dst, src, ready=None):
            for r in range(R):
                if ready is not None:
                    pe.wait_ge(*ready(r))
                last = nc.tensor.transpose(dst[:, r * P:(r + 1) * P], src(r), ident[:, :])
            return last

        def stats_tiles(mem, name):
            return (sb(mem, f"st_{name}", [P, R, 6], F32), sb(mem, f"mv_{name}", [P, R, 2], F32),
                    sb(mem, f"ve_{name}", [P, R], F32), sb(mem, f"rstd_{name}", [P, R], F32))


        loaded = [0]
        MS = 4
        Q = T // R

        def aggregate(V, side, slope=None, wh=None, sums_first=False):
            weighted = slope is not None
            with ExitStack() as mem, nc.Block() as block:
                mask = sb(mem, "mask", [P, MS, R * GW], U8)
                ph = sb(mem, "ph", [P, 2 * R, GW], F16)
                ag = sb(mem, "ag", [P, R * D], F32)
                rden = sb(mem, "rden", [P, R], F32)
                if weighted:
                    p32 = sb(mem, "p32", [P, R, GW], F32)
                    pl = sb(mem, "pl", [P, 2 * R, GW], F16)
                    v32 = sb(mem, "v32", [P, R, D + 1], F32)
                    dtil = sb(mem, "dtil", [P, T], F32)
                    red = sb(mem, "red", [P, 1], F32)
                work = side(mem, ag)
                pe_q.plan(("pv", R))
                act_q.plan(("hi", R))
                dve_q.plan(("p32", R), ("lo", R))
                pre_s.plan(("red", 1), ("dmax", 1), ("dtil", 1), ("omega", 1), ("vprime", 1), ("scale", 1))
                act_v.plan(("gam", 1), ("v32", R), ("hi", R))
                dve_v.plan(("relu", 1), ("scaled", 1), ("lo", R))
                masks = 16 * loaded[0]

                def slot(q, r):
                    return (q % 2) * R + r

                def gam(j):
                    return s_row[:, j * GW:(j + 1) * GW]

                def mask_here(g, q):
                    return s_mask[q % MS], g * (16 * Q // MS) + (masks + 16 * (q // MS + 1))

                def one_columns():
                    for part, value in ((0, 1.0), (1, 0.0)):
                        view = work["V"][:, part * (T * VW):(part + 1) * (T * VW)]
                        nc.vector.memset(view.rearrange("p (t w) -> p t w", w=VW)[:, :, D:D + 1], value)

                def groups(eng, quad, part, make=None, between=None):
                    for q in range(Q):
                        if make is not None:
                            make(q)
                        quad(0, q)
                    if between is not None:
                        between()
                    with eng.Fori(1, G) as g:
                        for q in range(Q):
                            quad(g, q)
                            part(eng, g - 1, q)
                    for q in range(Q):
                        part(eng, G - 1, q)

                @block.sync
                def _(sp):
                    def quad(g, q):
                        eng, stage = (dve_q, "p32") if weighted else (act_q, "hi")
                        sp.wait_ge(eng.sem, eng.before(g * Q + q, stage, R - 1, MS))
                        sp.sem_inc(s_pass[3], 1)
                        sp.dma_start(mask[:, q % MS, :], mask_d[ds(g * P, P), q * (R * GW):(q + 1) * (R * GW)]
                                     ).then_inc(s_mask[q % MS], 16)

                    groups(sp, quad, work["sync"])

                @block.gpsimd
                def _(pool):
                    if weighted:
                        pool.wait_ge(pre_s.sem, pre_s.at(0, "red"))
                        nc.gpsimd.partition_all_reduce(dmax[:, 0:1], red[:, :], P, RMAX).then_inc(pre_s.sem, 1)
                    with pool.Fori(0, G) as g:
                        work["pool"](pool, g)
                    work["end"](pool)

                @block.scalar
                def _(act):
                    def quad(g, q):
                        if not weighted:
                            act.wait_ge(*mask_here(g, q))
                        for r in range(R):
                            if weighted:
                                act.wait_ge(dve_q.sem, dve_q.at(g * Q + q, "p32", r))
                            act.wait_ge(pe_q.sem, pe_q.before(g * Q + q, "pv", r, 2))
                            nc.scalar.copy(ph[:, slot(q, r), :], p32[:, r, :] if weighted else
                                           mask[:, q % MS, r * GW:(r + 1) * GW]
                                           ).then_inc(act_q.sem, act_q.one("hi", r))

                    def make(q):
                        act.wait_ge(dve_v.sem, dve_v.at(q, "relu"))
                        nc.scalar.activation(gam(q), gam(q), ACT.Exp, scale=slope - 1.0
                                             ).then_inc(act_v.sem, act_v.one("gam"))
                        for r in range(R):
                            act.wait_ge(dve_v.sem, dve_v.before(q, "lo", r))
                            t = q * R + r
                            nc.scalar.mul(v32[:, r, 0:D], wh[:, t * D:(t + 1) * D], vprime[:, t:t + 1])
                            nc.scalar.copy(v32[:, r, D:D + 1], vprime[:, t:t + 1]
                                           ).then_inc(act_v.sem, act_v.one("v32", r))
                        for r in range(R):
                            act.wait_ge(act_v.sem, act_v.at(q, "v32", r))
                            nc.scalar.copy(v_row(V, 0, q * R + r), v32[:, r, :]
                                           ).then_inc(act_v.sem, act_v.one("hi", r))

                    def part(act, g, q):
                        if q == 0:
                            work["sums_free"](act, g)
                            for r in range(R):
                                act.wait_ge(dve_s.sem, dve_s.at(g, "rden", r))
                                nc.scalar.mul(row(ag, r), bank[r][:, 0:D], rden[:, r:r + 1]
                                              ).then_inc(act_s.sem, act_s.one("ag", r))
                        work["act"](act, g, q)

                    if weighted:
                        act.wait_ge(pre_s.sem, pre_s.at(0, "dtil"))
                        nc.scalar.activation(omega[:, :], dtil[:, :], ACT.Exp, scale=1.0 - slope
                                             ).then_inc(pre_s.sem, 1)
                        act.wait_ge(pre_s.sem, pre_s.at(0, "omega"))
                        nc.scalar.activation(vprime[:, :], dtil[:, :], ACT.Exp, scale=slope).then_inc(pre_s.sem, 1)
                        act.wait_ge(pre_s.sem, pre_s.at(0, "vprime"))
                    groups(act, quad, part, make if weighted else None)

                @block.vector
                def _(dve):
                    def quad(g, q):
                        if not weighted:
                            return
                        n = g * Q + q
                        dve.wait_ge(*mask_here(g, q))
                        for r in range(R):
                            dve.wait_ge(dve_q.sem, dve_q.before(n, "lo", r))
                            nc.vector.scalar_tensor_tensor(
                                out=p32[:, r, :], in0=s_row[:, ds(g * GW, GW)],
                                scalar=omega[:, q * R + r:q * R + r + 1],
                                in1=mask[:, q % MS, r * GW:(r + 1) * GW], op0=ALU.max, op1=ALU.mult
                                ).then_inc(dve_q.sem, dve_q.one("p32", r))
                        if q == 0 and not isinstance(g, int) and sums_first:
                            denominators(g - 1)
                        for r in range(R):
                            dve.wait_ge(act_q.sem, act_q.at(n, "hi", r))
                            nc.vector.tensor_tensor(pl[:, slot(q, r), :], p32[:, r, :], ph[:, slot(q, r), :],
                                                    ALU.subtract).then_inc(dve_q.sem, dve_q.one("lo", r))
                        if isinstance(g, int):
                            for r in range(R):
                                dve.wait_ge(act_v.sem, act_v.at(q, "hi", r))
                                nc.vector.tensor_tensor(v_row(V, 1, q * R + r), v32[:, r, :],
                                                        v_row(V, 0, q * R + r), ALU.subtract
                                                        ).then_inc(dve_v.sem, dve_v.one("lo", r))

                    def make(q):
                        nc.vector.tensor_scalar(gam(q), gam(q), dmax[:, 0:1], 0.0, ALU.add, ALU.max
                                                ).then_inc(dve_v.sem, dve_v.one("relu"))
                        dve.wait_ge(act_v.sem, act_v.at(q, "gam"))
                        nc.vector.tensor_scalar(gam(q), gam(q), PSCALE, None, ALU.mult
                                                ).then_inc(dve_v.sem, dve_v.one("scaled"))
                        dve.wait_ge(dve_v.sem, dve_v.at(q, "scaled"))

                    def denominators(g):
                        dve.wait_ge(pe_q.sem, pe_q.at(g * Q + (Q - 1), "pv", R - 1))
                        dve.wait_ge(act_s.sem, act_s.before(g, "ag", R - 1))
                        for r in range(R):
                            nc.vector.reciprocal(rden[:, r:r + 1], bank[r][:, D:D + 1]
                                                 ).then_inc(dve_s.sem, dve_s.one("rden", r))

                    def part(dve, g, q):
                        if q == 0 and (not sums_first or isinstance(g, int)):
                            denominators(g)
                        work["dve"](dve, g, q)

                    if weighted:
                        nc.vector.tensor_reduce(red[:, :], d_col[:, :], AX_X, ALU.max).then_inc(pre_s.sem, 1)
                        dve.wait_ge(pre_s.sem, pre_s.at(0, "dmax"))
                        nc.vector.tensor_scalar(dtil[:, :], d_col[:, :], dmax[:, 0:1], None, ALU.subtract
                                                ).then_inc(pre_s.sem, 1)
                        dve.wait_ge(pre_s.sem, pre_s.at(0, "vprime"))
                        nc.vector.tensor_scalar(omega[:, :], omega[:, :], PSCALE, None, ALU.mult
                                                ).then_inc(pre_s.sem, 1)
                        dve.wait_ge(pre_s.sem, pre_s.at(0, "scale"))
                    groups(dve, quad, part, make if weighted else None, one_columns if weighted else None)

                @block.tensor
                def _(pe):
                    def quad(g, q):
                        n = g * Q + q
                        for r in range(R):
                            if weighted:
                                pe.wait_ge(dve_q.sem, dve_q.at(n, "lo", r))
                                if isinstance(g, int):
                                    pe.wait_ge(dve_v.sem, dve_v.at(q, "lo", r))
                            else:
                                pe.wait_ge(act_q.sem, act_q.at(n, "hi", r))
                            first, final = q == 0 and r == 0, q == Q - 1 and r == R - 1
                            t = q * R + r
                            for i in range(R):
                                if first:
                                    pe.wait_ge(act_s.sem, act_s.before(g, "ag", i))
                                acc = bank[i][:, 0:D + 1]
                                c = slice(i * P, (i + 1) * P)
                                p_hi = ph[:, slot(q, r), c]
                                nc.tensor.matmul(acc, p_hi, v_row(V, 0, t), start=first, stop=False)
                                last = nc.tensor.matmul(acc, p_hi, v_row(V, 1, t), start=False,
                                                        stop=final and not weighted)
                                if weighted:
                                    last = nc.tensor.matmul(acc, pl[:, slot(q, r), c], v_row(V, 0, t),
                                                            start=False, stop=final)
                            last.then_inc(pe_q.sem, pe_q.one("pv", r))

                    groups(pe, quad, work["pe"])
            loaded[0] += G * Q // MS
            for x_ in (pe_s, act_s, dve_s, pool_s):
                x_.close(G)
            for x_ in (pe_q, act_q) + ((dve_q,) if weighted else ()):
                x_.close(G * Q)
            if weighted:
                pre_s.base += 6
                act_v.close(Q)
                dve_v.close(Q)

        def lo(dst, src, hi_part, stage, i):
            return nc.vector.tensor_tensor(dst, src, hi_part, ALU.subtract).then_inc(dve_s.sem, dve_s.one(stage, i))

        def hi(dst, src, stage, i):
            return nc.scalar.copy(dst, src).then_inc(act_s.sem, act_s.one(stage, i))

        def normal(act, g, h, x, nb, rs, stage="h"):
            act.wait_ge(dve_s.sem, dve_s.at(g, "nb"))
            for r in range(R):
                nc.scalar.activation(row(h, r), row(x, r), ACT.Relu, bias=nb[:, r:r + 1], scale=rs[:, r:r + 1]
                                     ).then_inc(act_s.sem, act_s.one(stage, r))

        def finish_layer0(mem, ag):
            hsg = sb(mem, "hsg", [P, R * D], F32)
            wg = sb(mem, "wg", [P, R * D], F32)
            xg = sb(mem, "xg2", [P, R * D], F32)
            xo = sb(mem, "xo", [P, R * D], F32)
            cT = [sb(mem, f"cT_{p}", [P, 2 * K, GW], F16) for p in ("hi", "lo")]
            gy = sb(mem, "gy", [P, HK, GW], F32)
            sT = [sb(mem, f"sT_{p}", [P, HK, GW], F16) for p in ("hi", "lo")]
            th = sb(mem, "th", [P, R * D], F32)
            dl = sb(mem, "dl", [P, R * D], F32)
            f = sb(mem, "f", [P, R * D], F32)
            h = th
            stg, mvg, veg, rsg = stats_tiles(mem, "g")
            stf, mvf, vef, rsf = stats_tiles(mem, "f")
            stx, mvx, vex, rsx = stats_tiles(mem, "x")
            nbg = sb(mem, "nbg", [P, R], F32)
            nb = sb(mem, "nb2", [P, R], F32)
            pe_s.plan(("cT", 2 * K), ("g1", R), ("gT", HK), ("g2", R))
            act_s.plan(("ag", R), ("cT", 2 * K), ("gy", R), ("silu", HK), ("sT", HK), ("tanh", 2), ("h", R),
                       ("V", R))
            dve_s.plan(("rden", R), ("cT", 2 * K), ("gs", R), ("gm", R), ("gv", 1), ("nbg", 1), ("sT", HK),
                       ("u", 1), ("f", 1), ("fs", R), ("fm", R), ("fv", 1), ("fg", R),
                       ("x", R), ("xs", R), ("xm", R), ("xv", 1), ("nb", 1), ("V", R))
            pool_s.plan(("dl", 1), ("xb", R), ("g", 1), ("f", 1), ("rx", 1))
            first_in, stores = 16 * (G + 2), stored[0]
            stored[0] += 16 * G
            V = value(VB)

            def sync(sp, g, q):
                if q == 3:
                    sp.wait_ge(dve_s.sem, dve_s.before(g, "x", R - 1))
                    sp.wait_ge(pe_s.sem, pe_s.before(g, "cT", 2 * K - 1))
                    sp.sem_inc(s_pass[3], 1)
                    for dst, src in ((hsg, hs_d), (wg, w_d), (xg, a["x"])):
                        sp.dma_start(dst[:, :], src[ds(g * P, P), :]).then_inc(s_xin, 16)

            def end(pool):
                pool.wait_ge(s_xout, stores + 16 * G)

            def sums_free(act, g):
                act.wait_ge(pool_s.sem, pool_s.before(g, "dl"))

            def pool_part(pool, g):
                pool.wait_ge(s_xin, g * 48 + (first_in + 48))
                pool.wait_ge(act_s.sem, act_s.at(g, "ag", R - 1))
                pool.wait_ge(dve_s.sem, dve_s.before(g, "u"))
                pool.sem_inc(s_pass[1], 1)
                nc.gpsimd.tensor_tensor(dl[:, :], ag[:, :], hsg[:, :], ALU.subtract
                                        ).then_inc(pool_s.sem, pool_s.one("dl"))
                for r in range(R):
                    nc.gpsimd.tensor_tensor(row(xg, r), row(xg, r), lnb[:, :], ALU.add
                                            ).then_inc(pool_s.sem, pool_s.one("xb", r))
                inverse_root(pool, g, rsg, veg, "gv", "g")
                inverse_root(pool, g, rsf, vef, "fv", "f")
                inverse_root(pool, g, rsx, vex, "xv", "rx")
                pool.wait_ge(dve_s.sem, dve_s.at(g, "x", R - 1))
                pool.sem_inc(s_pass[1], 1)
                nc.gpsimd.dma_start(x1_d[ds(g * P, P), :], xo[:, :]).then_inc(s_xout, 16)

            def act_part(act, g, q):
                if q == 1:
                    for k in range(2 * K):
                        act.wait_ge(pe_s.sem, pe_s.at(g, "cT", k))
                        hi(cT[0][:, k, :], bank[4 + k][:, :], "cT", k)
                if q == 3:
                    act.wait_ge(dve_s.sem, dve_s.at(g, "nbg"))
                    for r in range(R):
                        nc.scalar.activation(gy[:, r, :], bank[4 + r][:, :], ACT.Identity, bias=nbg[:, r:r + 1],
                                             scale=rsg[:, r:r + 1]).then_inc(act_s.sem, act_s.one("gy", r))
                if q == 4:
                    act.wait_ge(pe_s.sem, pe_s.at(g, "gT", HK - 1))
                    for k in range(HK):
                        nc.scalar.activation(gy[:, k, :], bank[4 + k][:, :], ACT.Silu,
                                             bias=col_b[:, GB + k:GB + k + 1], scale=col_b[:, GG + k:GG + k + 1]
                                             ).then_inc(act_s.sem, act_s.one("silu", k))
                    for k in range(HK):
                        act.wait_ge(act_s.sem, act_s.at(g, "silu", k))
                        hi(sT[0][:, k, :], gy[:, k, :], "sT", k)
                if q == 5:
                    act.wait_ge(dve_s.sem, dve_s.before(g, "V", R - 1))
                    for j in range(2):
                        act.wait_ge(pe_s.sem, pe_s.at(g, "g2", 2 * j + 1))
                        nc.scalar.activation(row(th, j, 2 * D), bank[4 + j][:, :], ACT.Tanh, scale=0.5
                                             ).then_inc(act_s.sem, act_s.one("tanh", j))
                if q == 6:
                    normal(act, g, h, xo, nb, rsx)
                    for r in range(R):
                        act.wait_ge(act_s.sem, act_s.at(g, "h", r))
                        hi(v_row(V, 0, g * R + r, D), row(h, r), "V", r)

            def dve_part(dve, g, q):
                if q == 1:
                    for k in range(2 * K):
                        dve.wait_ge(act_s.sem, act_s.at(g, "cT", k))
                        lo(cT[1][:, k, :], bank[4 + k][:, :], cT[0][:, k, :], "cT", k)
                if q == 3:
                    moments(dve, g, [(bank[4 + r][:, :], (pe_s.sem, pe_s.at(g, "g1", r))) for r in range(R)],
                            stg, mvg, veg, ("gs", "gm", "gv"))
                    shift(dve, g, nbg, mvg, rsg, "nbg", "g")
                if q == 4:
                    for k in range(HK):
                        dve.wait_ge(act_s.sem, act_s.at(g, "sT", k))
                        lo(sT[1][:, k, :], gy[:, k, :], sT[0][:, k, :], "sT", k)
                if q == 5:
                    dve.wait_ge(act_s.sem, act_s.at(g, "tanh", 1))
                    dve.wait_ge(pool_s.sem, pool_s.at(g, "dl"))
                    nc.vector.scalar_tensor_tensor(out=th[:, :], in0=th[:, :], scalar=1.0, in1=dl[:, :],
                                                   op0=ALU.add, op1=ALU.mult
                                                   ).then_inc(dve_s.sem, dve_s.one("u"))
                    dve.wait_ge(dve_s.sem, dve_s.at(g, "u"))
                    dve.wait_ge(s_xin, g * 48 + (first_in + 48))
                    nc.vector.scalar_tensor_tensor(out=f[:, :], in0=th[:, :], scalar=0.5, in1=wg[:, :],
                                                   op0=ALU.mult, op1=ALU.add
                                                   ).then_inc(dve_s.sem, dve_s.one("f"))
                    moments(dve, g, [(row(f, r), None) for r in range(R)], stf, mvf, vef, ("fs", "fm", "fv"),
                            (dve_s.sem, dve_s.at(g, "f")))
                if q == 6:
                    dve.wait_ge(s_xout, g * 16 + stores)
                    for r in range(R):
                        nc.vector.scalar_tensor_tensor(out=row(f, r), in0=row(f, r), scalar=mvf[:, r, 0:1],
                                                       in1=lng[:, :], op0=ALU.subtract, op1=ALU.mult
                                                       ).then_inc(dve_s.sem, dve_s.one("fg", r))
                    dve.wait_ge(pool_s.sem, pool_s.at(g, "f"))
                    for r in range(R):
                        dve.wait_ge(dve_s.sem, dve_s.at(g, "fg", r))
                        nc.vector.scalar_tensor_tensor(out=row(xo, r), in0=row(f, r), scalar=rsf[:, r:r + 1],
                                                       in1=row(xg, r), op0=ALU.mult, op1=ALU.add
                                                       ).then_inc(dve_s.sem, dve_s.one("x", r))
                    moments(dve, g, [(row(xo, r), None) for r in range(R)], stx, mvx, vex, ("xs", "xm", "xv"),
                            (dve_s.sem, dve_s.at(g, "x", R - 1)))
                    shift(dve, g, nb, mvx, rsx, "nb", "rx")
                if q == 7:
                    for r in range(R):
                        dve.wait_ge(act_s.sem, act_s.at(g, "V", r))
                        lo(v_row(V, 1, g * R + r, D), row(h, r), v_row(V, 0, g * R + r, D), "V", r)

            def pe_part(pe, g, q):
                if q == 0:
                    pe.wait_ge(s_xin, g * 48 + (first_in + 48))
                    for j, src in enumerate((hsg, ag)):
                        for k in range(K):
                            transposes(pe, bank[4 + j * K + k], lambda r: src[:, r * D + k * P:r * D + (k + 1) * P],
                                       (lambda r: (act_s.sem, act_s.at(g, "ag", r))) if j and not k else None
                                       ).then_inc(pe_s.sem, pe_s.one("cT", j * K + k))
                if q == 1:
                    pe.wait_ge(dve_s.sem, dve_s.at(g, "cT", 2 * K - 1))
                    for r in range(R):
                        products(pe, bank[4 + r][:, :],
                                 [(cols(cT, (k + K) % (2 * K), r), w("g1", k)) for k in range(2 * K)], "g1"
                                 ).then_inc(pe_s.sem, pe_s.one("g1", r))
                if q == 2:
                    pe.wait_ge(act_s.sem, act_s.at(g, "gy", R - 1))
                    for k in range(HK):
                        transposes(pe, bank[4 + k], lambda r: gy[:, r, k * P:(k + 1) * P]
                                   ).then_inc(pe_s.sem, pe_s.one("gT", k))
                if q == 3:
                    pe.wait_ge(dve_s.sem, dve_s.at(g, "sT", HK - 1))
                    for r in range(R):
                        products(pe, bank[4 + r // 2][:, (r % 2) * D:(r % 2 + 1) * D],
                                 [(cols(sT, k, r), w("g2", k)) for k in range(HK)], "g2"
                                 ).then_inc(pe_s.sem, pe_s.one("g2", r))

            return {"sync": sync, "pool": pool_part, "act": act_part, "dve": dve_part, "pe": pe_part, "end": end,
                    "sums_free": sums_free, "V": V}

        def finish_layer1(mem, ag):
            xg = sb(mem, "xg3", [P, R * D], F32)
            xo = sb(mem, "xo1", [P, R * D], F32)
            aT = [sb(mem, f"aT_{p}", [P, K, GW], F16) for p in ("hi", "lo")]
            h = sb(mem, "h1", [P, R * D], F32)
            hT = [sb(mem, f"h1T_{p}", [P, K, GW], F16) for p in ("hi", "lo")]
            stx, mvx, vex, rsx = stats_tiles(mem, "x1")
            nb = sb(mem, "nb3", [P, R], F32)
            pe_s.plan(("aT", K), ("lin", R), ("hT", K), ("srow", 1), ("wh", R))
            act_s.plan(("ag", R), ("aT", K), ("h", R), ("hT", K), ("srow", 1), ("wh", R))
            dve_s.plan(("rden", R), ("aT", K), ("x", 2), ("xs", R), ("xm", R), ("xv", 1), ("nb", 1), ("hT", K),
                       ("d", R))
            pool_s.plan(("rx", 1))
            first_in, stores = 16 * (G + 2) + 48 * G, stored[0]
            stored[0] += 16 * G
            wh = rows_of(VA)

            def sync(sp, g, q):
                if q == 3:
                    sp.wait_ge(dve_s.sem, dve_s.before(g, "x", 1))
                    sp.sem_inc(s_pass[3], 1)
                    sp.dma_start(xg[:, :], x1_d[ds(g * P, P), :]).then_inc(s_xin, 16)

            def end(pool):
                pool.wait_ge(s_xout, stores + 16 * G)

            def sums_free(act, g):
                act.wait_ge(pe_s.sem, pe_s.before(g, "aT", K - 1))

            def pool_part(pool, g):
                inverse_root(pool, g, rsx, vex, "xv", "rx")
                pool.wait_ge(dve_s.sem, dve_s.at(g, "x", 1))
                pool.sem_inc(s_pass[1], 1)
                nc.gpsimd.dma_start(x2_d[ds(g * P, P), :], xo[:, :]).then_inc(s_xout, 16)

            def act_part(act, g, q):
                if q == 1:
                    for k in range(K):
                        act.wait_ge(pe_s.sem, pe_s.at(g, "aT", k))
                        hi(aT[0][:, k, :], bank[4 + k][:, :], "aT", k)
                if q == 4:
                    normal(act, g, h, xo, nb, rsx)
                if q == 5:
                    for k in range(K):
                        act.wait_ge(pe_s.sem, pe_s.at(g, "hT", k))
                        hi(hT[0][:, k, :], bank[4 + k][:, :], "hT", k)
                if q == 7:
                    act.wait_ge(pe_s.sem, pe_s.at(g, "srow"))
                    nc.scalar.copy(s_row[:, ds(g * GW, GW)], bank[4][:, :]
                                   ).then_inc(act_s.sem, act_s.one("srow"))
                    for r in range(R):
                        act.wait_ge(pe_s.sem, pe_s.at(g, "wh", r))
                        nc.scalar.copy(wh[:, ds(g * (R * D) + r * D, D)], bank[(5, 6, 7, 4)[r]][:, 0:D]
                                       ).then_inc(act_s.sem, act_s.one("wh", r))

            def dve_part(dve, g, q):
                if q == 1:
                    for k in range(K):
                        dve.wait_ge(act_s.sem, act_s.at(g, "aT", k))
                        lo(aT[1][:, k, :], bank[4 + k][:, :], aT[0][:, k, :], "aT", k)
                if q == 3:
                    dve.wait_ge(s_xin, g * 16 + (first_in + 16))
                    dve.wait_ge(s_xout, g * 16 + stores)
                    dve.sem_inc(s_pass[0], 1)
                    for j in range(2):
                        dve.wait_ge(pe_s.sem, pe_s.at(g, "lin", 2 * j + 1))
                        nc.vector.tensor_tensor(row(xo, j, 2 * D), bank[6 + j][:, :], row(xg, j, 2 * D), ALU.add
                                                ).then_inc(dve_s.sem, dve_s.one("x", j))
                    moments(dve, g, [(row(xo, r), None) for r in range(R)], stx, mvx, vex, ("xs", "xm", "xv"),
                            (dve_s.sem, dve_s.at(g, "x", 1)))
                    shift(dve, g, nb, mvx, rsx, "nb", "rx")
                if q == 5:
                    for k in range(K):
                        dve.wait_ge(act_s.sem, act_s.at(g, "hT", k))
                        lo(hT[1][:, k, :], bank[4 + k][:, :], hT[0][:, k, :], "hT", k)
                if q == 7:
                    for r in range(R):
                        dve.wait_ge(act_s.sem, act_s.at(g, "wh", r))
                        nc.vector.tensor_copy(d_col[:, ds(g * R + r, 1)], bank[(5, 6, 7, 4)[r]][:, D:D + 1]
                                              ).then_inc(dve_s.sem, dve_s.one("d", r))

            def pe_part(pe, g, q):
                if q == 0:
                    pe.wait_ge(dve_s.sem, dve_s.before(g, "d", R - 1))
                    for k in range(K):
                        transposes(pe, bank[4 + k], lambda r: ag[:, r * D + k * P:r * D + (k + 1) * P],
                                   lambda r: (act_s.sem, act_s.at(g, "ag", r))
                                   ).then_inc(pe_s.sem, pe_s.one("aT", k))
                if q == 2:
                    pe.wait_ge(dve_s.sem, dve_s.at(g, "aT", K - 1))
                    for r in range(R):
                        products(pe, bank[6 + r // 2][:, (r % 2) * D:(r % 2 + 1) * D],
                                 [(cols(aT, k, r), w("W1", k)) for k in range(K)], "W1"
                                 ).then_inc(pe_s.sem, pe_s.one("lin", r))
                if q == 4:
                    for k in range(K):
                        transposes(pe, bank[4 + k], lambda r: h[:, r * D + k * P:r * D + (k + 1) * P],
                                   lambda r: (act_s.sem, act_s.at(g, "h", r))
                                   ).then_inc(pe_s.sem, pe_s.one("hT", k))
                if q == 6:
                    pe.wait_ge(dve_s.sem, dve_s.at(g, "hT", K - 1))
                    source_rows(pe, 1, hT, bank[4]).then_inc(pe_s.sem, pe_s.one("srow"))
                    for r in range(R):
                        if r == R - 1:
                            pe.wait_ge(act_s.sem, act_s.at(g, "srow"))
                        products(pe, bank[(5, 6, 7, 4)[r]][:, 0:D + 1],
                                 [(cols(hT, k, r), w("W2", k)) for k in range(K)]
                                 ).then_inc(pe_s.sem, pe_s.one("wh", r))

            return {"sync": sync, "pool": pool_part, "act": act_part, "dve": dve_part, "pe": pe_part, "end": end,
                    "sums_free": sums_free}

        def finish_layer2(mem, ag):
            xg = sb(mem, "xg4", [P, R * D], F32)
            xo = sb(mem, "xo2", [P, R * D], F32)
            e = w_gate[0][:, 0:2 * R * D].bitcast(F32)
            h = w_gate[1][:, 0:2 * R * D].bitcast(F32)
            hT = [sb(mem, f"h2T_{p}", [P, K, GW], F16) for p in ("hi", "lo")]
            qT = sb(mem, "qTg", [P, 2, K, GW], F16)
            stx, mvx, vex, rsx = stats_tiles(mem, "x2")
            nb = sb(mem, "nb4", [P, R], F32)
            pe_s.plan(("hT", K), ("qT", K), ("kT", K), ("v", R))
            act_s.plan(("ag", R), ("e", 1), ("h", R), ("hT", K), ("qT", K), ("kT", K), ("v", R))
            dve_s.plan(("rden", R), ("mn", 1), ("pos", 1), ("x", 1), ("xs", R), ("xm", R), ("xv", 1), ("nb", 1),
                       ("hT", K), ("qT", K), ("kT", K), ("v", R))
            pool_s.plan(("rx", 1))
            first_in, stores = 16 * (G + 2) + 64 * G, stored[0]
            stored[0] += 32 * G
            V = value(VA)

            def sync(sp, g, q):
                if q == 3:
                    sp.wait_ge(dve_s.sem, dve_s.before(g, "pos"))
                    sp.sem_inc(s_pass[3], 1)
                    sp.dma_start(xg[:, :], x2_d[ds(g * P, P), :]).then_inc(s_xin, 16)

            def end(pool):
                pool.wait_ge(s_xout, stores + 32 * G)

            def sums_free(act, g):
                act.wait_ge(dve_s.sem, dve_s.before(g, "pos"))

            def pool_part(pool, g):
                inverse_root(pool, g, rsx, vex, "xv", "rx")
                pool.wait_ge(dve_s.sem, dve_s.at(g, "x"))
                pool.sem_inc(s_pass[1], 1)
                nc.gpsimd.dma_start(x3_d[ds(g * P, P), :], xo[:, :]).then_inc(s_xout, 16)
                pool.wait_ge(dve_s.sem, dve_s.at(g, "qT", K - 1))
                pool.sem_inc(s_pass[1], 1)
                nc.gpsimd.dma_start(qT_d[ds(g * P, P), :], qT[:, :, :, :].rearrange("p a k n -> p (a k n)")
                                    ).then_inc(s_xout, 16)

            def act_part(act, g, q):
                if q == 1:
                    act.wait_ge(dve_s.sem, dve_s.at(g, "mn"))
                    nc.scalar.activation(e[:, :], e[:, :], ACT.Exp).then_inc(act_s.sem, act_s.one("e"))
                if q == 2:
                    normal(act, g, h, xo, nb, rsx)
                if q == 3:
                    for k in range(K):
                        act.wait_ge(pe_s.sem, pe_s.at(g, "hT", k))
                        hi(hT[0][:, k, :], bank[4 + k][:, :], "hT", k)
                if q == 5:
                    act.wait_ge(s_xout, g * 32 + stores)
                    for k in range(K):
                        act.wait_ge(pe_s.sem, pe_s.at(g, "qT", k))
                        hi(qT[:, 0, k, :], bank[4 + k][:, :], "qT", k)
                    for k in range(K):
                        act.wait_ge(pe_s.sem, pe_s.at(g, "kT", k))
                        hi(kT[0][:, k, ds(g * GW, GW)], bank[6 + k][:, :], "kT", k)
                if q == 7:
                    for r in range(R):
                        act.wait_ge(pe_s.sem, pe_s.at(g, "v", r))
                        hi(v_row(V, 0, g * R + r, D), bank[4 + r][:, 0:D], "v", r)

            def dve_part(dve, g, q):
                if q == 1:
                    dve.wait_ge(act_s.sem, act_s.at(g, "ag", R - 1))
                    nc.vector.tensor_scalar(e[:, :], ag[:, :], 0.0, None, ALU.min
                                            ).then_inc(dve_s.sem, dve_s.one("mn"))
                    dve.wait_ge(s_xin, g * 16 + (first_in + 16))
                    dve.wait_ge(s_xout, g * 32 + stores)
                    nc.vector.scalar_tensor_tensor(out=xo[:, :], in0=ag[:, :], scalar=0.0, in1=xg[:, :],
                                                   op0=ALU.max, op1=ALU.add
                                                   ).then_inc(dve_s.sem, dve_s.one("pos"))
                    dve.wait_ge(act_s.sem, act_s.at(g, "e"))
                    dve.wait_ge(dve_s.sem, dve_s.at(g, "pos"))
                    nc.vector.scalar_tensor_tensor(out=xo[:, :], in0=e[:, :], scalar=-1.0, in1=xo[:, :],
                                                   op0=ALU.add, op1=ALU.add).then_inc(dve_s.sem, dve_s.one("x"))
                    moments(dve, g, [(row(xo, r), None) for r in range(R)], stx, mvx, vex, ("xs", "xm", "xv"),
                            (dve_s.sem, dve_s.at(g, "x")))
                    shift(dve, g, nb, mvx, rsx, "nb", "rx")
                if q == 3:
                    for k in range(K):
                        dve.wait_ge(act_s.sem, act_s.at(g, "hT", k))
                        lo(hT[1][:, k, :], bank[4 + k][:, :], hT[0][:, k, :], "hT", k)
                if q == 5:
                    for k in range(K):
                        dve.wait_ge(act_s.sem, act_s.at(g, "qT", k))
                        lo(qT[:, 1, k, :], bank[4 + k][:, :], qT[:, 0, k, :], "qT", k)
                    for k in range(K):
                        dve.wait_ge(act_s.sem, act_s.at(g, "kT", k))
                        c = ds(g * GW, GW)
                        lo(kT[1][:, k, c], bank[6 + k][:, :], kT[0][:, k, c], "kT", k)
                if q == 7:
                    for r in range(R):
                        dve.wait_ge(act_s.sem, act_s.at(g, "v", r))
                        lo(v_row(V, 1, g * R + r, D), bank[4 + r][:, 0:D], v_row(V, 0, g * R + r, D), "v", r)

            def pe_part(pe, g, q):
                if q == 2:
                    pe.wait_ge(dve_s.sem, dve_s.before(g, "v", R - 1))
                    for k in range(K):
                        transposes(pe, bank[4 + k], lambda r: h[:, r * D + k * P:r * D + (k + 1) * P],
                                   lambda r: (act_s.sem, act_s.at(g, "h", r))
                                   ).then_inc(pe_s.sem, pe_s.one("hT", k))
                if q == 4:
                    pe.wait_ge(dve_s.sem, dve_s.at(g, "hT", K - 1))
                    for name, b in (("q", 4), ("k", 6)):
                        for m in range(K):
                            products(pe, bank[b + m][:, :],
                                     [(w("W" + name, k, m * P, (m + 1) * P), (hT[0][:, k, :], hT[1][:, k, :]))
                                      for k in range(K)]).then_inc(pe_s.sem, pe_s.one(name + "T", m))
                if q == 6:
                    pe.wait_ge(dve_s.sem, dve_s.at(g, "kT", K - 1))
                    for r in range(R):
                        products(pe, bank[4 + r][:, 0:D], [(cols(hT, k, r), w("Wv", k)) for k in range(K)]
                                 ).then_inc(pe_s.sem, pe_s.one("v", r))

            return {"sync": sync, "pool": pool_part, "act": act_part, "dve": dve_part, "pe": pe_part, "end": end,
                    "sums_free": sums_free, "V": V}

        whole = [0]

        def every_group(eng, body):
            for half in range(2):
                body(half, 0, half)
            with eng.Fori(1, G // 2 - 1) as b:
                for half in range(2):
                    body(b * 2 + half, b, half)
            for half in range(2):
                body(G - 2 + half, G // 2 - 1, half)

        def row_maxima():
            with ExitStack() as mem, nc.Block() as block:
                mask = sb(mem, "mask", [P, 2, T * GW], U8)
                q_hi = spare[:, 0:2 * K * GW].rearrange("p (h k n) -> p h k n", h=2, k=K)
                m16 = sb(mem, "m16", [P, R, GW], F16)
                top_of = sb(mem, "top_of", [P, 2 * R, GW], F32)
                own_of = sb(mem, "own_of", [P, R, P], F32)
                onto = sb(mem, "onto", [P, R, P], F32)
                pe_q.plan(("s", R))
                act_q.plan(("m16", R))
                dve_q.plan(("max", R))
                next_dve.plan(("clear", 1), ("own", R), ("loop", R), ("diag", R))
                pe_s.plan(("turn", 1), ("spread", 1))
                dve_s.plan(("join", 3), ("col", 1), ("m", 1), ("onto", R), ("row", 1))
                masks = 16 * whole[0]

                @block.sync
                def _(sp):
                    with sp.Fori(0, G // 2) as b:
                        for half in range(2):
                            sp.wait_ge(pe_q.sem, pe_q.before((b * 2 + half) * Q, "s", R - 1, Q + 1))
                            sp.sem_inc(s_pass[3], 1)
                            at = ds(b * (2 * P) + half * P, P)
                            sp.dma_start(mask[:, half, :], mask_d[at, :]).then_inc(s_whole[half], 16)
                            sp.dma_start(q_hi[:, half, :, :].rearrange("p k n -> p (k n)"), qT_d[at, 0:K * GW]
                                         ).then_inc(s_qin[half], 16)

                @block.scalar
                def _(act):
                    with act.Fori(0, G // 2) as b:
                        for half in range(2):
                            g = b * 2 + half
                            act.wait_ge(next_dve.sem, next_dve.at(g, "diag", R - 1))
                            with act.Fori(0, Q) as q:
                                n = g * Q + q
                                for r in range(R):
                                    act.wait_ge(pe_q.sem, pe_q.before(n, "s", r))
                                    nc.scalar.copy(m16[:, r, :], mask[:, half, ds(q * (R * GW) + r * GW, GW)]
                                                   ).then_inc(act_q.sem, act_q.one("m16", r))

                @block.vector
                def _(dve):
                    def diagonal(g, b, half):
                        dve.wait_ge(dve_s.sem, dve_s.before(g, "join", 2, 2))
                        dve.sem_inc(s_pass[0], 1)
                        nc.vector.memset(top_of[:, half * R:(half + 1) * R, :], -3.0e38
                                         ).then_inc(next_dve.sem, next_dve.one("clear"))

                        def own(r):
                            return mask[:, half, ds(g * (R * GW) + (r * GW + r * P), P)]

                        dve.wait_ge(s_whole[half], b * 16 + (masks + 16))
                        dve.wait_ge(next_dve.sem, next_dve.before(g, "loop", R - 1))
                        for r in range(R):
                            nc.vector.tensor_tensor(own_of[:, r, :], own(r), ident8[:, :], ALU.mult
                                                    ).then_inc(next_dve.sem, next_dve.one("own", r))
                        for r in range(R):
                            dve.wait_ge(next_dve.sem, next_dve.at(g, "own", r))
                            nc.vector.tensor_reduce(loop_col[:, ds(g * R + r, 1)], own_of[:, r, :], AX_X, ALU.max
                                                    ).then_inc(next_dve.sem, next_dve.one("loop", r))
                        for r in range(R):
                            nc.vector.tensor_tensor(own(r), own(r), ident8[:, :], ALU.max
                                                    ).then_inc(next_dve.sem, next_dve.one("diag", r))

                    def quads(g, half, q0, q1):
                        with dve.Fori(q0, q1) as q:
                            n = g * Q + q
                            for r in range(R):
                                dve.wait_ge(pe_q.sem, pe_q.at(n, "s", r))
                                dve.wait_ge(dve_q.sem, dve_q.before(n, "max", r))
                                top_r = top_of[:, half * R + r, :]
                                nc.vector.tensor_tensor(top_r, bank[r][:, :], top_r, ALU.max
                                                        ).then_inc(dve_q.sem, dve_q.one("max", r))

                    def join(g, half):
                        top_r = [top_of[:, half * R + r, :] for r in range(R)]
                        dve.wait_ge(dve_q.sem, dve_q.at(g * Q + (Q - 1), "max", R - 1))
                        nc.vector.tensor_tensor(top_r[0], top_r[0], top_r[1], ALU.max
                                                ).then_inc(dve_s.sem, dve_s.one("join", 0))
                        nc.vector.tensor_tensor(top_r[2], top_r[2], top_r[3], ALU.max
                                                ).then_inc(dve_s.sem, dve_s.one("join", 1))
                        dve.wait_ge(dve_s.sem, dve_s.at(g, "join", 1))
                        nc.vector.tensor_tensor(top_r[0], top_r[0], top_r[2], ALU.max
                                                ).then_inc(dve_s.sem, dve_s.one("join", 2))

                    def columns(g):
                        dve.wait_ge(pe_s.sem, pe_s.at(g, "turn"))
                        nc.vector.tensor_reduce(m_col[:, ds(g * R, R)],
                                                bank[4][:, :].rearrange("p (r n) -> p r n", r=R), AX_X, ALU.max
                                                ).then_inc(dve_s.sem, dve_s.one("col"))
                        dve.wait_ge(dve_s.sem, dve_s.at(g, "col"))
                        nc.vector.tensor_scalar(m_col[:, ds(g * R, R)], m_col[:, ds(g * R, R)], BIG, None,
                                                ALU.subtract).then_inc(dve_s.sem, dve_s.one("m"))
                        dve.wait_ge(dve_s.sem, dve_s.at(g, "m"))
                        for r in range(R):
                            nc.vector.tensor_scalar(onto[:, r, :], ident[:, :], m_col[:, ds(g * R + r, 1)], None,
                                                    ALU.mult).then_inc(dve_s.sem, dve_s.one("onto", r))

                    def spread(g):
                        dve.wait_ge(pe_s.sem, pe_s.at(g, "spread"))
                        nc.vector.tensor_copy(m_row[:, ds(g * GW, GW)], bank[5][:, :]
                                              ).then_inc(dve_s.sem, dve_s.one("row"))

                    def body(g, b, half):
                        first, final = isinstance(g, int) and g == 0, isinstance(g, int) and g == G - 1
                        quads(g, half, 0, 2)
                        if not first:
                            columns(g - 1)
                        quads(g, half, 2, 4)
                        if not first:
                            spread(g - 1)
                        if not final:
                            diagonal(g + 1, b + half, 1 - half)
                        quads(g, half, 4, Q)
                        join(g, half)

                    diagonal(0, 0, 0)
                    every_group(dve, body)
                    columns(G - 1)
                    spread(G - 1)

                @block.tensor
                def _(pe):
                    def quads(g, half, q0, q1):
                        with pe.Fori(q0, q1) as q:
                            n = g * Q + q
                            for r in range(R):
                                pe.wait_ge(dve_q.sem, dve_q.before(n, "max", r))
                                c = ds(q * (R * P) + r * P, P)
                                for k in range(K):
                                    nc.tensor.matmul(bank[r][:, :], kT[0][:, k, c], q_hi[:, half, k, :],
                                                     start=(k == 0), stop=False)
                                pe.wait_ge(act_q.sem, act_q.at(n, "m16", r))
                                nc.tensor.matmul(bank[r][:, :], big16[:, :], m16[:, r, :], start=False,
                                                 stop=True).then_inc(pe_q.sem, pe_q.one("s", r))

                    def turn(g, half):
                        pe.wait_ge(dve_s.sem, dve_s.at(g, "join", 2))
                        transposes(pe, bank[4], lambda r: top_of[:, half * R, r * P:(r + 1) * P]
                                   ).then_inc(pe_s.sem, pe_s.one("turn"))

                    def spread(g):
                        for r in range(R):
                            pe.wait_ge(dve_s.sem, dve_s.at(g, "onto", r))
                            last = nc.tensor.matmul(bank[5][:, r * P:(r + 1) * P], ones[:, :], onto[:, r, :],
                                                    start=True, stop=True)
                        last.then_inc(pe_s.sem, pe_s.one("spread"))

                    def body(g, b, half):
                        first = isinstance(g, int) and g == 0
                        pe.wait_ge(s_qin[half], b * 16 + 16)
                        pe.sem_inc(s_pass[2], 1)
                        quads(g, half, 0, 1)
                        if not first:
                            turn(g - 1, 1 - half)
                        quads(g, half, 1, 3)
                        if not first:
                            spread(g - 1)
                        quads(g, half, 3, Q)

                    every_group(pe, body)
                    turn(G - 1, 1)
                    spread(G - 1)
            whole[0] += G // 2
            for x_ in (dve_s, pe_s, next_dve):
                x_.close(G)
            for x_ in (pe_q, act_q, dve_q):
                x_.close(G * Q)

        def attend():
            with ExitStack() as mem, nc.Block() as block:
                mask = sb(mem, "mask", [P, 2, T * GW], U8)
                qh = spare[:, 0:4 * K * GW].rearrange("p (h a k n) -> p h a k n", h=2, a=2, k=K)
                p32 = sb(mem, "p32", [P, R, GW], F32)
                ph = sb(mem, "ph", [P, R, GW], F16)
                pl = sb(mem, "pl", [P, R, GW], F16)
                rden = sb(mem, "rden", [P, R], F32)
                res = w_gate[0][:, 0:2 * R * D].bitcast(F32)
                gap = w_gate[1][:, 0:2 * R * D].bitcast(F32)
                xg = [s_row[:, i * R * D:(i + 1) * R * D] for i in range(2)]
                xo = s_row[:, 2 * R * D:3 * R * D]
                pe_l.plan(("s", R))
                pe_q.plan(("pv", R))
                act_q.plan(("exp", R), ("hi", R))
                dve_q.plan(("z", R), ("p", R), ("lo", R))
                act_s.plan(("res", R))
                next_dve.plan(("diag", R))
                dve_s.plan(("rden", R), ("gap", R), ("gap2", R), ("sel", R), ("out", 1))
                masks = 16 * whole[0]
                qs = 16 * (G // 2)

                def last_of(g):
                    return pe_q.sem, pe_q.at(g * Q + (Q - 1), "pv", R - 1)

                @block.sync
                def _(sp):
                    with sp.Fori(0, G // 2) as b:
                        for half in range(2):
                            g = b * 2 + half
                            sp.wait_ge(pe_q.sem, pe_q.before(g * Q, "pv", R - 1, Q + 1))
                            sp.wait_ge(dve_s.sem, dve_s.before(g, "out", 0, 2))
                            sp.sem_inc(s_pass[3], 1)
                            at = ds(b * (2 * P) + half * P, P)
                            sp.dma_start(mask[:, half, :], mask_d[at, :]).then_inc(s_whole[half], 16)
                            sp.dma_start(qh[:, half, :, :, :].rearrange("p a k n -> p (a k n)"), qT_d[at, :]
                                         ).then_inc(s_qin[half], 16)
                            sp.dma_start(xg[half], x3_d[at, :]).then_inc(s_qin[half], 16)
                    sp.wait_ge(s_out, 16 * G)

                @block.gpsimd
                def _(pool):
                    with pool.Fori(0, G) as g:
                        pool.wait_ge(dve_s.sem, dve_s.at(g, "out"))
                        pool.sem_inc(s_pass[1], 1)
                        nc.gpsimd.dma_start(out[ds(g * P, P), :], xo).then_inc(s_out, 16)

                @block.scalar
                def _(act):
                    def quad(g, q):
                        n = g * Q + q
                        for r in range(R):
                            act.wait_ge(dve_q.sem, dve_q.at(n, "z", r))
                            nc.scalar.activation(p32[:, r, :], p32[:, r, :], ACT.Exp
                                                 ).then_inc(act_q.sem, act_q.one("exp", r))
                        for r in range(R):
                            act.wait_ge(dve_q.sem, dve_q.at(n, "p", r))
                            act.wait_ge(pe_q.sem, pe_q.before(n, "pv", r))
                            nc.scalar.copy(ph[:, r, :], p32[:, r, :]).then_inc(act_q.sem, act_q.one("hi", r))

                    def sums(g):
                        act.wait_ge(dve_s.sem, dve_s.before(g, "out"))
                        for r in range(R):
                            act.wait_ge(dve_s.sem, dve_s.at(g, "rden", r))
                            nc.scalar.mul(row(res, r), bank[4 + r][:, 0:D], rden[:, r:r + 1]
                                          ).then_inc(act_s.sem, act_s.one("res", r))

                    def body(g, b, half):
                        quad(g, 0)
                        if not (isinstance(g, int) and g == 0):
                            sums(g - 1)
                        with act.Fori(1, Q) as q:
                            quad(g, q)

                    every_group(act, body)
                    sums(G - 1)

                @block.vector
                def _(dve):
                    def diagonal(g, b, half):
                        dve.wait_ge(s_whole[half], b * 16 + (masks + 16))
                        for r in range(R):
                            own = mask[:, half, ds(g * (R * GW) + (r * GW + r * P), P)]
                            nc.vector.tensor_tensor(own, own, ident8[:, :], ALU.max
                                                    ).then_inc(next_dve.sem, next_dve.one("diag", r))

                    def quad(g, q, half):
                        n = g * Q + q
                        for r in range(R):
                            dve.wait_ge(pe_l.sem, pe_l.at(n, "s", r))
                            dve.wait_ge(dve_q.sem, dve_q.before(n, "lo", r))
                            nc.vector.tensor_tensor(p32[:, r, :], bank[r][:, :], m_row[:, ds(g * GW, GW)],
                                                    ALU.subtract).then_inc(dve_q.sem, dve_q.one("z", r))
                        for r in range(R):
                            dve.wait_ge(act_q.sem, act_q.at(n, "exp", r))
                            nc.vector.scalar_tensor_tensor(
                                out=p32[:, r, :], in0=p32[:, r, :], scalar=TOP,
                                in1=mask[:, half, ds(q * (R * GW) + r * GW, GW)], op0=ALU.min, op1=ALU.mult
                                ).then_inc(dve_q.sem, dve_q.one("p", r))
                        for r in range(R):
                            dve.wait_ge(act_q.sem, act_q.at(n, "hi", r))
                            nc.vector.tensor_tensor(pl[:, r, :], p32[:, r, :], ph[:, r, :], ALU.subtract
                                                    ).then_inc(dve_q.sem, dve_q.one("lo", r))

                    def sums(g):
                        dve.wait_ge(*last_of(g))
                        for r in range(R):
                            nc.vector.reciprocal(rden[:, r:r + 1], bank[4 + r][:, D:D + 1]
                                                 ).then_inc(dve_s.sem, dve_s.one("rden", r))

                    def result(g, b, half):
                        for r in range(R):
                            dve.wait_ge(act_s.sem, act_s.at(g, "res", r))
                            nc.vector.tensor_tensor(row(gap, r), v_row(V, 0, g * R + r, D), row(res, r), ALU.subtract
                                                    ).then_inc(dve_s.sem, dve_s.one("gap", r))
                        for r in range(R):
                            dve.wait_ge(dve_s.sem, dve_s.at(g, "gap", r))
                            nc.vector.tensor_tensor(row(gap, r), row(gap, r), v_row(V, 1, g * R + r, D), ALU.add
                                                    ).then_inc(dve_s.sem, dve_s.one("gap2", r))
                        for r in range(R):
                            dve.wait_ge(dve_s.sem, dve_s.at(g, "gap2", r))
                            nc.vector.scalar_tensor_tensor(out=row(res, r), in0=row(gap, r),
                                                           scalar=loop_col[:, ds(g * R + r, 1)],
                                                           in1=row(res, r), op0=ALU.mult, op1=ALU.add
                                                           ).then_inc(dve_s.sem, dve_s.one("sel", r))
                        dve.wait_ge(dve_s.sem, dve_s.at(g, "sel", R - 1))
                        dve.wait_ge(s_out, g * 16)
                        dve.wait_ge(s_qin[half], b * 32 + (qs + 32))
                        nc.vector.tensor_tensor(xo, res, xg[half], ALU.add
                                                ).then_inc(dve_s.sem, dve_s.one("out"))

                    def body(g, b, half):
                        first, final = isinstance(g, int) and g == 0, isinstance(g, int) and g == G - 1
                        quad(g, 0, half)
                        if not first:
                            sums(g - 1)
                        quad(g, 1, half)
                        if not first:
                            result(g - 1, b - (1 - half), 1 - half)
                        with dve.Fori(2, Q - 2) as q:
                            quad(g, q, half)
                        if not final:
                            diagonal(g + 1, b + half, 1 - half)
                        with dve.Fori(Q - 2, Q) as q:
                            quad(g, q, half)

                    diagonal(0, 0, 0)
                    dve.wait_ge(next_dve.sem, next_dve.at(0, "diag", R - 1))
                    dve.sem_inc(s_pass[0], 1)
                    every_group(dve, body)
                    sums(G - 1)
                    result(G - 1, G // 2 - 1, 1)

                @block.tensor
                def _(pe):
                    def logits(g, q, half):
                        n = g * Q + q
                        for r in range(R):
                            pe.wait_ge(dve_q.sem, dve_q.before(n, "z", r))
                            c = ds(q * (R * P) + r * P, P)
                            products(pe, bank[r][:, :],
                                     [((kT[0][:, k, c], kT[1][:, k, c]), (qh[:, half, 0, k, :], qh[:, half, 1, k, :]))
                                      for k in range(K)]).then_inc(pe_l.sem, pe_l.one("s", r))

                    def values(g, q, edge=0):
                        n = g * Q + q
                        for r in range(R):
                            pe.wait_ge(dve_q.sem, dve_q.at(n, "lo", r))
                            first, final = edge == -1 and r == 0, edge == 1 and r == R - 1
                            t = q * R + r
                            for i in range(R):
                                if first:
                                    pe.wait_ge(act_s.sem, act_s.before(g, "res", i))
                                acc = bank[4 + i][:, 0:D + 1]
                                c = slice(i * P, (i + 1) * P)
                                nc.tensor.matmul(acc, ph[:, r, c], v_row(V, 0, t), start=first, stop=False)
                                nc.tensor.matmul(acc, ph[:, r, c], v_row(V, 1, t), start=False, stop=False)
                                last = nc.tensor.matmul(acc, pl[:, r, c], v_row(V, 0, t), start=False, stop=final)
                            last.then_inc(pe_q.sem, pe_q.one("pv", r))

                    def load(b, half):
                        pe.wait_ge(s_qin[half], b * 32 + (qs + 32))
                        pe.sem_inc(s_pass[2], 1)

                    def body(g, b, half):
                        logits(g, 1, half)
                        values(g, 0, -1)
                        with pe.Fori(1, Q - 1) as q:
                            logits(g, q + 1, half)
                            values(g, q)
                        if not (isinstance(g, int) and g == G - 1):
                            load(b + half, 1 - half)
                            logits(g + 1, 0, 1 - half)
                        values(g, Q - 1, 1)

                    load(0, 0)
                    logits(0, 0, 0)
                    every_group(pe, body)
            whole[0] += G // 2
            for x_ in (dve_s, act_s, next_dve):
                x_.close(G)
            for x_ in (pe_q, act_q, dve_q, pe_l):
                x_.close(G * Q)

        aggregate(value(VA), finish_layer0, 0.2, rows_of(VB), sums_first=True)
        aggregate(value(VB), finish_layer1)
        kT = [sb(top, f"kT_{p}", [P, K, N], F16) for p in ("hi", "lo")]
        aggregate(value(VB), finish_layer2, 0.01, rows_of(VA))
        m_row = VB[:, 0:2 * N].bitcast(F32)
        spare = VB[:, 2 * N:4 * N]
        V = value(VA)
        row_maxima()
        attend()


_NAMES = ["L0_gnn_W", "L0_gnn_a_src", "L0_gnn_a_dst", "L0_gnn_W_bcdt", "L0_gnn_b_bcdt", "L0_gnn_abp_w",
          "L0_gnn_abp_b", "L0_gnn_cp_w", "L0_gnn_cp_b", "L0_gnn_W_hz", "L0_gnn_b_hz", "L0_gnn_out_w",
          "L0_gnn_out_b", "L0_gnn_fe1_w", "L0_gnn_fe1_b", "L0_gnn_fe_ln_g", "L0_gnn_fe_ln_b", "L0_gnn_fe2_w",
          "L0_gnn_fe2_b", "L0_gnn_A", "L0_gnn_D", "L0_gnn_g1_w", "L0_gnn_g1_b", "L0_gnn_g_ln_g",
          "L0_gnn_g_ln_b", "L0_gnn_g2_w", "L0_gnn_g2_b", "L0_gnn_ln_g", "L0_gnn_ln_b", "L1_gnn_b",
          "L2_gnn_W", "L2_gnn_a", "L3_gnn_Wq", "L3_gnn_Wk", "L3_gnn_Wv"]
_FLAT = ("L0_gnn_a_src", "L0_gnn_a_dst", "L0_gnn_cp_w", "L2_gnn_a")


def kernel(**inputs):
    import numpy as np
    import concourse.bacc as bacc
    from concourse.bass_utils import run_bass_kernel_spmd

    x, adj = np.asarray(inputs["x"]), np.asarray(inputs["adj"])
    arrays = {name: np.ascontiguousarray(inputs[name]) for name in _NAMES}
    for name in _FLAT:
        arrays[name] = arrays[name].reshape(-1)
    arrays["L1_gnn_WT"] = np.ascontiguousarray(np.asarray(inputs["L1_gnn_W"]).T)
    arrays["x"] = np.ascontiguousarray(x.reshape(G, R, P, D).transpose(0, 2, 1, 3)).reshape(G * P, R * D)
    arrays["adj"] = np.ascontiguousarray(adj.reshape(G, GW, T, P).transpose(0, 3, 2, 1)).reshape(G * P, T * GW)

    nc = bacc.Bacc("TRN2", target_bir_lowering=False, num_devices=1)
    aps = {name: nc.dram_tensor(f"in_{name}", v.shape, mybir.dt.from_np(v.dtype), kind="ExternalInput").ap()
           for name, v in arrays.items()}
    out = nc.dram_tensor("out_x", (G * P, R * D), F32, kind="ExternalOutput").ap()
    build(nc, aps, out)
    result = run_bass_kernel_spmd(nc, [{f"in_{name}": v for name, v in arrays.items()}], core_ids=[0])
    got = result.results[0]["out_x"]
    return np.ascontiguousarray(got.reshape(G, P, R, D).transpose(0, 2, 1, 3)).reshape(N, D)
```
